# Optimizing a Trainium2 kernel written in Bass

```python
import numpy as np
import jax
import jax.numpy as jnp

def _softmax(x, axis=-1):
    return jax.nn.softmax(x, axis=axis)

def _gelu(x):
    return jax.nn.gelu(x, approximate=True)

def _silu(x):
    return jax.nn.silu(x)

def _sigmoid(x):
    return jax.nn.sigmoid(x)

def _layernorm(x, axis=-1, eps=1e-05):
    m = jnp.mean(x, axis=axis, keepdims=True)
    v = jnp.var(x, axis=axis, keepdims=True)
    return (x - m) / jnp.sqrt(v + eps)

def _scatter_add(tgt, idx, src, axis=0):
    return tgt.at[idx].add(src)

def _segment_sum(src, seg, n):
    return jax.ops.segment_sum(src, seg, n)
kernel_name = 'mk_macaron_d1_jaxref_r4_ecffb5'

def setup_inputs(seed: int=0):
    np.random.seed(seed)
    _w = jnp.asarray

    def _L0_attn_setup():
        import math
        import jax, jax.numpy as jnp
        import numpy as np
        from jax.scipy.special import logsumexp
        B, L, D_MODEL = (2, 256, 256)
        H = 16
        DH = D_MODEL // H
        M = 24
        WINDOW = 128
        MASK_VAL = -10000.0
        EPS = 0.0001
        SCALE = 1.0 / math.sqrt(DH)

        def _sb_features(x, proj, is_query):
            xh = x * math.sqrt(SCALE)
            x_dash = jnp.einsum('bhld,md->bhlm', xh, proj)
            diag = 0.5 * jnp.sum(xh * xh, axis=-1, keepdims=True)
            log_feat = x_dash - diag
            if is_query:
                stab = jax.lax.stop_gradient(jnp.max(log_feat, axis=-1, keepdims=True))
            else:
                stab = jax.lax.stop_gradient(jnp.max(log_feat, axis=(-2, -1), keepdims=True))
            prime = jnp.exp(log_feat - stab) + EPS
            return (prime, stab)

        def _local_mask(L):
            i = jnp.arange(L)[:, None]
            j = jnp.arange(L)[None, :]
            keep = (j <= i) & (j >= i - WINDOW)
            return jnp.where(keep, 0.0, MASK_VAL).astype(jnp.float32)
        if __name__ == '__main__':
            o = reference(**setup_inputs())
            print(o.shape, o.dtype)
        key = jax.random.key(seed)
        ks = jax.random.split(key, 4)
        x = jax.random.normal(ks[0], (B, L, D_MODEL), dtype=jnp.float32)
        Wqkv_w = jax.random.normal(ks[1], (3 * D_MODEL, D_MODEL), dtype=jnp.float32) * D_MODEL ** (-0.5)
        Wqkv_b = jnp.zeros((3 * D_MODEL,), dtype=jnp.float32)
        proj = jax.random.normal(ks[2], (M, DH), dtype=jnp.float32)
        out_w = jax.random.normal(ks[3], (D_MODEL, D_MODEL), dtype=jnp.float32) * D_MODEL ** (-0.5)
        out_b = jnp.zeros((D_MODEL,), dtype=jnp.float32)
        return {'x': x, 'Wqkv_w': Wqkv_w, 'Wqkv_b': Wqkv_b, 'proj': proj, 'out_w': out_w, 'out_b': out_b}
    _L0_attn_in = _L0_attn_setup()

    def _L0_ffn_setup():
        import jax, jax.numpy as jnp
        import numpy as np
        B, S, DIM = (4, 1024, 256)
        BASE_COUPLING = 0.1
        NUM_CYCLES = 3

        def _gelu(x):
            return jax.nn.gelu(x, approximate=False)

        def _coupling_net(h, w1, b1, w2, b2, w3, b3, w4, b4):
            h = _gelu(h @ w1 + b1)
            h = _gelu(h @ w2 + b2)
            h = _gelu(h @ w3 + b3)
            return jax.nn.sigmoid(h @ w4 + b4)

        def _global_net(h, w1, b1, w2, b2, w3, b3):
            h = _gelu(h @ w1 + b1)
            h = _gelu(h @ w2 + b2)
            return jax.nn.sigmoid(h @ w3 + b3)

        def _twist(x):
            o_r, o_i, p_r, p_i = jnp.split(x, 4, axis=-1)
            return jnp.concatenate([p_r, -p_i, -o_r, o_i], axis=-1)
        key = jax.random.key(seed)
        ks = jax.random.split(key, 9)
        d = DIM

        def w(k, fan_in, fan_out):
            return jax.random.normal(k, (fan_in, fan_out), dtype=jnp.float32) / np.sqrt(fan_in).astype(np.float32)
        inp = {'x': jax.random.normal(ks[0], (B, S, d), dtype=jnp.float32)}
        cn_dims = [(d, d), (d, d // 2), (d // 2, d // 4), (d // 4, 1)]
        for i, (a, b) in enumerate(cn_dims):
            inp[f'cn_w{i + 1}'] = w(ks[1 + i], a, b)
            inp[f'cn_b{i + 1}'] = jnp.zeros((b,), dtype=jnp.float32)
        gc_dims = [(d, d // 2), (d // 2, d // 4), (d // 4, 1)]
        for i, (a, b) in enumerate(gc_dims):
            inp[f'gc_w{i + 1}'] = w(ks[5 + i], a, b)
            inp[f'gc_b{i + 1}'] = jnp.zeros((b,), dtype=jnp.float32)
        inp['adaptive_range'] = jnp.full((1,), 0.2, dtype=jnp.float32)
        return inp
    _L0_ffn_in = _L0_ffn_setup()
    _d = {'L0_attn_x': _L0_attn_in['x'], 'L0_attn_Wqkv_w': _L0_attn_in['Wqkv_w'], 'L0_attn_Wqkv_b': _L0_attn_in['Wqkv_b'], 'L0_attn_proj': _L0_attn_in['proj'], 'L0_attn_out_w': _L0_attn_in['out_w'], 'L0_attn_out_b': _L0_attn_in['out_b'], 'L0_ffn_cn_w1': _L0_ffn_in['cn_w1'], 'L0_ffn_cn_b1': _L0_ffn_in['cn_b1'], 'L0_ffn_cn_w2': _L0_ffn_in['cn_w2'], 'L0_ffn_cn_b2': _L0_ffn_in['cn_b2'], 'L0_ffn_cn_w3': _L0_ffn_in['cn_w3'], 'L0_ffn_cn_b3': _L0_ffn_in['cn_b3'], 'L0_ffn_cn_w4': _L0_ffn_in['cn_w4'], 'L0_ffn_cn_b4': _L0_ffn_in['cn_b4'], 'L0_ffn_gc_w1': _L0_ffn_in['gc_w1'], 'L0_ffn_gc_b1': _L0_ffn_in['gc_b1'], 'L0_ffn_gc_w2': _L0_ffn_in['gc_w2'], 'L0_ffn_gc_b2': _L0_ffn_in['gc_b2'], 'L0_ffn_gc_w3': _L0_ffn_in['gc_w3'], 'L0_ffn_gc_b3': _L0_ffn_in['gc_b3'], 'L0_ffn_adaptive_range': _L0_ffn_in['adaptive_range']}
    _x0 = _d['L0_attn_x']
    _d['L0_attn_x'] = jax.random.normal(jax.random.fold_in(jax.random.key(seed), 1), (2, 2048, 256), dtype=_x0.dtype)
    del _x0
    return _d

def reference(L0_attn_x, L0_attn_Wqkv_w, L0_attn_Wqkv_b, L0_attn_proj, L0_attn_out_w, L0_attn_out_b, L0_ffn_cn_w1, L0_ffn_cn_b1, L0_ffn_cn_w2, L0_ffn_cn_b2, L0_ffn_cn_w3, L0_ffn_cn_b3, L0_ffn_cn_w4, L0_ffn_cn_b4, L0_ffn_gc_w1, L0_ffn_gc_b1, L0_ffn_gc_w2, L0_ffn_gc_b2, L0_ffn_gc_w3, L0_ffn_gc_b3, L0_ffn_adaptive_range):

    def _L0_attn_ref(x, Wqkv_w, Wqkv_b, proj, out_w, out_b):
        import math
        import jax, jax.numpy as jnp
        import numpy as np
        from jax.scipy.special import logsumexp
        B, L, D_MODEL = (2, 256, 256)
        H = 16
        DH = D_MODEL // H
        M = 24
        WINDOW = 128
        MASK_VAL = -10000.0
        EPS = 0.0001
        SCALE = 1.0 / math.sqrt(DH)

        def _sb_features(x, proj, is_query):
            xh = x * math.sqrt(SCALE)
            x_dash = jnp.einsum('bhld,md->bhlm', xh, proj)
            diag = 0.5 * jnp.sum(xh * xh, axis=-1, keepdims=True)
            log_feat = x_dash - diag
            if is_query:
                stab = jax.lax.stop_gradient(jnp.max(log_feat, axis=-1, keepdims=True))
            else:
                stab = jax.lax.stop_gradient(jnp.max(log_feat, axis=(-2, -1), keepdims=True))
            prime = jnp.exp(log_feat - stab) + EPS
            return (prime, stab)

        def _local_mask(L):
            i = jnp.arange(L)[:, None]
            j = jnp.arange(L)[None, :]
            keep = (j <= i) & (j >= i - WINDOW)
            return jnp.where(keep, 0.0, MASK_VAL).astype(jnp.float32)
        if __name__ == '__main__':
            o = reference(**setup_inputs())
            print(o.shape, o.dtype)
        b, l, dm = x.shape
        qkv = (x @ Wqkv_w.T + Wqkv_b).reshape(b, l, 3, H, DH)
        q = jnp.transpose(qkv[:, :, 0], (0, 2, 1, 3))
        k = jnp.transpose(qkv[:, :, 1], (0, 2, 1, 3))
        v = jnp.transpose(qkv[:, :, 2], (0, 2, 1, 3))
        q_prime, q_ls = _sb_features(q, proj, is_query=True)
        k_prime, k_ls = _sb_features(k, proj, is_query=False)
        global_scale = q_ls + k_ls
        global_out_cumsum = jnp.einsum('bhnm,bhnm->bhn', q_prime, jnp.cumsum(k_prime, axis=-2))
        kv = jnp.cumsum(k_prime[..., :, :, None] * v[..., :, None, :], axis=-3)
        global_out = jnp.einsum('bhlm,bhlmd->bhld', q_prime, kv)
        mask = _local_mask(l)
        g_scores = jnp.einsum('bhmd,bhnd->bhmn', q_prime, k_prime) * SCALE + mask
        global_qk = jnp.where(g_scores <= 0, 0.0, g_scores)
        l_scores = jnp.einsum('bhmd,bhnd->bhmn', q, k) * SCALE + mask
        QK_lse = logsumexp(l_scores, axis=-1, keepdims=True)
        gqk_sum = jnp.sum(global_qk, axis=-1, keepdims=True)
        g_log_norm = jnp.log(jnp.clip(global_out_cumsum[..., None] - gqk_sum, 1e-24)) + global_scale
        log_norm = jnp.logaddexp(QK_lse, g_log_norm)
        g_prime_scale = jnp.exp(global_scale - log_norm)
        local_score = jax.nn.softmax(l_scores - log_norm, axis=-1) - global_qk * g_prime_scale
        out = jnp.einsum('bhmn,bhnd->bhmd', local_score, v) + global_out * g_prime_scale
        ctx = jnp.transpose(out, (0, 2, 1, 3)).reshape(b, l, dm)
        return ctx @ out_w.T + out_b

    def _L0_ffn_ref(x, cn_w1, cn_b1, cn_w2, cn_b2, cn_w3, cn_b3, cn_w4, cn_b4, gc_w1, gc_b1, gc_w2, gc_b2, gc_w3, gc_b3, adaptive_range):
        import jax, jax.numpy as jnp
        import numpy as np
        B, S, DIM = (4, 1024, 256)
        BASE_COUPLING = 0.1
        NUM_CYCLES = 3

        def _gelu(x):
            return jax.nn.gelu(x, approximate=False)

        def _coupling_net(h, w1, b1, w2, b2, w3, b3, w4, b4):
            h = _gelu(h @ w1 + b1)
            h = _gelu(h @ w2 + b2)
            h = _gelu(h @ w3 + b3)
            return jax.nn.sigmoid(h @ w4 + b4)

        def _global_net(h, w1, b1, w2, b2, w3, b3):
            h = _gelu(h @ w1 + b1)
            h = _gelu(h @ w2 + b2)
            return jax.nn.sigmoid(h @ w3 + b3)

        def _twist(x):
            o_r, o_i, p_r, p_i = jnp.split(x, 4, axis=-1)
            return jnp.concatenate([p_r, -p_i, -o_r, o_i], axis=-1)
        global_context = x.mean(axis=1, keepdims=True)
        gf = _global_net(global_context, gc_w1, gc_b1, gc_w2, gc_b2, gc_w3, gc_b3)
        out = x
        for _ in range(NUM_CYCLES):
            tf = _coupling_net(out, cn_w1, cn_b1, cn_w2, cn_b2, cn_w3, cn_b3, cn_w4, cn_b4)
            combined = 0.7 * gf + 0.3 * tf
            coupling = BASE_COUPLING + adaptive_range * (combined - 0.5) * 2.0
            out = out + coupling * _twist(out)
        return out
    x = L0_attn_x
    x = x + 0.5 * _L0_ffn_ref(_layernorm(x, axis=-1), L0_ffn_cn_w1, L0_ffn_cn_b1, L0_ffn_cn_w2, L0_ffn_cn_b2, L0_ffn_cn_w3, L0_ffn_cn_b3, L0_ffn_cn_w4, L0_ffn_cn_b4, L0_ffn_gc_w1, L0_ffn_gc_b1, L0_ffn_gc_w2, L0_ffn_gc_b2, L0_ffn_gc_w3, L0_ffn_gc_b3, L0_ffn_adaptive_range)
    x = x + _L0_attn_ref(_layernorm(x, axis=-1), L0_attn_Wqkv_w, L0_attn_Wqkv_b, L0_attn_proj, L0_attn_out_w, L0_attn_out_b)
    x = x + 0.5 * _L0_ffn_ref(_layernorm(x, axis=-1), L0_ffn_cn_w1, L0_ffn_cn_b1, L0_ffn_cn_w2, L0_ffn_cn_b2, L0_ffn_cn_w3, L0_ffn_cn_b3, L0_ffn_cn_w4, L0_ffn_cn_b4, L0_ffn_gc_w1, L0_ffn_gc_b1, L0_ffn_gc_w2, L0_ffn_gc_b2, L0_ffn_gc_w3, L0_ffn_gc_b3, L0_ffn_adaptive_range)
    return x

_drawn_inputs = setup_inputs


def setup_inputs(seed=0):
    import zlib

    import numpy as np

    out = dict(_drawn_inputs(seed))
    spreads = {'L0_attn_Wqkv_b': (0.0, 0.1),
     'L0_attn_out_b': (0.0, 0.1),
     'L0_ffn_cn_b1': (0.0, 2.0),
     'L0_ffn_cn_b2': (0.0, 2.0),
     'L0_ffn_cn_b3': (0.0, 2.0),
     'L0_ffn_gc_b1': (0.0, 0.8),
     'L0_ffn_gc_b2': (0.0, 0.8)}
    factors = {'L0_ffn_cn_w1': 6.474,
     'L0_ffn_cn_w2': 6.91,
     'L0_ffn_cn_w3': 5.496,
     'L0_ffn_cn_w4': 6.126,
     'L0_ffn_gc_w1': 8.0,
     'L0_ffn_gc_w2': 8.0,
     'L0_ffn_gc_w3': 4.47}
    for name, (base, spread) in spreads.items():
        noise = np.random.default_rng([zlib.crc32(name.encode()), seed]).standard_normal(out[name].shape)
        drawn = base * np.exp(spread * noise) if base else spread * noise
        out[name] = jnp.asarray(drawn.astype(out[name].dtype))
    for name, factor in factors.items():
        out[name] = (out[name] * factor).astype(out[name].dtype)
    return out
```

```python
from contextlib import ExitStack
from math import sqrt

import concourse.bass as bass
from concourse import mybir

ds = bass.ds
ALU = mybir.AluOpType
ACT = mybir.ActivationFunctionType
F32 = mybir.dt.float32
F16 = mybir.dt.float16
BF16 = mybir.dt.bfloat16
AX_X = mybir.AxisListType.X

P = 128
LN_EPS = 1e-5
FEATURE_EPS = 1e-4
MASKED = -30000.0


def macaron_kernel(nc, x_in, wqkv, bqkv, proj, wout, bout, cn_w1, cn_b1, cn_w2, cn_b2, cn_w3, cn_b3,
                   cn_w4, cn_b4, gc_w1, gc_b1, gc_w2, gc_b2, gc_w3, gc_b3, adaptive_range, out):
    BATCH, SEQ, DM = x_in.shape
    NBLK = BATCH * SEQ // P
    BLK_B = SEQ // P
    HALVES = DM // P
    TILE = 512
    TILES_B = SEQ // TILE
    BLK_T = TILE // P
    CYCLES = 3
    D1, D2, D3 = cn_w1.shape[1], cn_w2.shape[1], cn_w3.shape[1]
    MCH = D1 // P
    assert HALVES == 2 and DM == 256 and D2 == P and D3 == 64 and SEQ % TILE == 0

    x_blocks = x_in.rearrange("b (n p) c -> p (b n) c", p=P)
    out_blocks = out.rearrange("b (n p) c -> p (b n) c", p=P)

    with ExitStack() as keep:
        def sb(name, shape, dt, scope=keep):
            return scope.enter_context(nc.sbuf_tensor(name, shape, dt))

        def psum(name, shape, scope, dt=F32):
            return scope.enter_context(nc.psum_tensor(name, shape, dt))

        def sem(name, scope):
            return scope.enter_context(nc.semaphore(name))

        x_tok = sb("x_tok", [P, NBLK, DM], F32)
        xn_ch = sb("xn_ch", [P, HALVES, (NBLK + 1) * P], F32)
        ident = sb("ident", [P, P], F32)
        twist_sign = sb("twist_sign", [P, 1], F32)
        ones_col = sb("ones_col", [P, 1], F32)
        eps_col = sb("eps_col", [P, 1], F32)
        block_sums = sb("block_sums", [P, HALVES, NBLK], F32)

        w1 = sb("w1", [P, HALVES, D1], F32)
        w2 = sb("w2", [P, MCH, D2], F32)
        w3 = sb("w3", [P, D3], F32)
        w4 = sb("w4", [D3, 1], F32)
        w4_rep = sb("w4_rep", [D3, P], F32)
        b1 = sb("b1", [P, MCH], F32)
        b2 = sb("b2", [P, 1], F32)
        b3 = sb("b3", [D3, 1], F32)
        b4_half = sb("b4_half", [P, 1], F32)
        g1 = sb("g1", [P, HALVES, P], F32)
        g2 = sb("g2", [P, D3], F32)
        g3 = sb("g3", [D3, 1], F32)
        g3_rep = sb("g3_rep", [D3, P], F32)
        gb1 = sb("gb1", [P, 1], F32)
        gb2 = sb("gb2", [D3, 1], F32)
        gb3_half = sb("gb3_half", [P, 1], F32)
        rng = sb("rng", [P, 1], F32)
        gain = sb("gain", [P, 1], F32)

        with ExitStack() as scope:
            loaded = sem("loaded", scope)
            blank = sem("blank", scope)
            drawn = sem("drawn", scope)
            col = lambda v: v.rearrange("(p a) -> p a", a=1)
            spread = lambda v, n: v.rearrange("(a p) -> a p", a=1).broadcast_to([n, 1])
            with nc.Block() as block:
                loads = [
                    (w1[:, :, :], cn_w1.rearrange("(k p) n -> p k n", p=P)),
                    (w2[:, :, :], cn_w2.rearrange("(k p) n -> p k n", p=P)),
                    (w3[:, :], cn_w3),
                    (w4[:, :], cn_w4),
                    (b1[:, :], cn_b1.rearrange("(k p) -> p k", p=P)),
                    (b2[:, :], col(cn_b2)),
                    (b3[:, :], col(cn_b3)),
                    (b4_half[:, :], spread(cn_b4, P)),
                    (g1[:, :, :], gc_w1.rearrange("(k p) n -> p k n", p=P)),
                    (g2[:, :], gc_w2),
                    (g3[:, :], gc_w3),
                    (gb1[:, :], col(gc_b1)),
                    (gb2[:, :], col(gc_b2)),
                    (gb3_half[:, :], spread(gc_b3, P)),
                    (rng[:, :], spread(adaptive_range, P)),
                ]

                @block.scalar
                def _(act):
                    for dst, src in loads:
                        act.dma_start(dst, src, allow_slow_non_contiguous=True).then_inc(loaded, 16)

                @block.gpsimd
                def _(pool):
                    nc.gpsimd.memset(ident[:, :], 0.0).then_inc(blank, 1)
                    nc.gpsimd.memset(twist_sign[:, :], 1.0).then_inc(blank, 1)
                    nc.gpsimd.memset(ones_col[:, :], 1.0)
                    nc.gpsimd.memset(eps_col[:, :], LN_EPS)
                    nc.gpsimd.memset(xn_ch[:, :, NBLK * P:], 0.0)
                    pool.wait_ge(blank, 2)
                    nc.gpsimd.affine_select(out=ident[:, :], in_=ident[:, :], compare_op=ALU.not_equal,
                                            fill=1.0, base=0, pattern=[[-1, P]], channel_multiplier=1)
                    nc.gpsimd.affine_select(out=twist_sign[:, :], in_=twist_sign[:, :], compare_op=ALU.is_gt,
                                            fill=-1.0, base=P // 2, pattern=[[0, 1]],
                                            channel_multiplier=-1).then_inc(drawn, 1)

                @block.vector
                def _(dve):
                    dve.wait_ge(loaded, 16 * len(loads))
                    dve.wait_ge(drawn, 1)
                    nc.vector.tensor_scalar(w1[:, 1, :], w1[:, 1, :], twist_sign[:, 0:1], None, ALU.mult)
                    nc.vector.tensor_scalar(g1[:, 1, :], g1[:, 1, :], twist_sign[:, 0:1], None, ALU.mult)
                    nc.vector.tensor_copy(w4_rep[:, :], w4[:, 0:1].broadcast_to([D3, P]))
                    nc.vector.tensor_copy(g3_rep[:, :], g3[:, 0:1].broadcast_to([D3, P]))
                    nc.vector.tensor_scalar(b4_half[:, :], b4_half[:, :], 0.5, None, ALU.mult)
                    nc.vector.tensor_scalar(gb3_half[:, :], gb3_half[:, :], 0.5, None, ALU.mult)
                    nc.vector.tensor_scalar(gain[:, :], rng[:, :], 0.3, None, ALU.mult)

        def layernorm(name, first, scale_half1):
            G = 4
            STEPS = NBLK // G
            with ExitStack() as scope:
                xn_tok = sb(name + "_xn_tok", [P, 2, G, DM], F32, scope)
                stats = sb(name + "_stats", [P, 2, G, 6], F32, scope)
                moments = sb(name + "_moments", [P, 2, G, 2], F32, scope)
                std = sb(name + "_std", [P, G], F32, scope)
                rstd = sb(name + "_rstd", [P, G], F32, scope)
                turned = [psum(f"{name}_turned{i}", [P, HALVES, 2, P], scope) for i in range(4)]
                x_loaded = [sem(f"{name}_x_loaded{i}", scope) for i in range(STEPS)] if first else []
                stats_done = sem(name + "_stats_done", scope)
                moments_done = sem(name + "_moments_done", scope)
                std_done = sem(name + "_std_done", scope)
                rstd_done = sem(name + "_rstd_done", scope)
                xn_ready = sem(name + "_xn_ready", scope)
                turned_ready = sem(name + "_turned_ready", scope)
                turned_used = sem(name + "_turned_used", scope)
                with nc.Block() as block:
                    if first:
                        @block.sync
                        def _(sp):
                            for i in range(STEPS):
                                sp.dma_start(x_tok[:, i * G:(i + 1) * G, :],
                                             x_blocks[:, i * G:(i + 1) * G, :]).then_inc(x_loaded[i], 16)
                            for i in range(STEPS):
                                sp.wait_ge(x_loaded[i], 16)

                    @block.vector
                    def _(dve):
                        def rows(blk):
                            return x_tok[:, ds(blk, 1), :].rearrange("p a c -> p (a c)")

                        def statistics(par, blk):
                            for j in range(G):
                                s = nc.vector.bn_stats(stats[:, par, j, :], rows(blk + j))
                            s.then_inc(stats_done, 1)

                        def moments_of(par):
                            for j in range(G):
                                s = nc.vector.bn_aggr(moments[:, par, j, :], stats[:, par, j, :])
                            s.then_inc(moments_done, 1)

                        def normalise(i, par, blk, peeled):
                            dve.wait_ge(std_done, i + 1)
                            nc.vector.reciprocal(rstd[:, :], std[:, :]).then_inc(rstd_done, 1)
                            dve.wait_ge(rstd_done, i + 1)
                            if not peeled:
                                dve.wait_ge(turned_ready, (i - 1) * 2)
                            for j in range(G):
                                s = nc.vector.tensor_scalar(xn_tok[:, par, j, :], rows(blk + j), moments[:, par, j, 0:1],
                                                            rstd[:, j:j + 1], ALU.subtract, ALU.mult)
                            s.then_inc(xn_ready, 1)

                        def step(i, par, peeled):
                            if first:
                                dve.wait_ge(x_loaded[i], 16)
                            if not isinstance(i, int) or i >= 2:
                                dve.wait_ge(moments_done, i - 1)
                                dve.wait_ge(xn_ready, i - 1)
                            statistics(par, i * G)
                            dve.wait_ge(stats_done, i + 1)
                            normalise(i - 1, 1 - par, (i - 1) * G, peeled)
                            moments_of(par)

                        if first:
                            dve.wait_ge(x_loaded[0], 16)
                        statistics(0, 0)
                        dve.wait_ge(stats_done, 1)
                        moments_of(0)
                        if first:
                            for i in range(1, STEPS):
                                step(i, i % 2, i < 3)
                        else:
                            step(1, 1, True)
                            step(2, 0, True)
                            step(3, 1, False)
                            with dve.Fori(2, STEPS // 2) as k:
                                for par in range(2):
                                    step(k * 2 + par, par, False)
                        normalise(STEPS - 1, (STEPS - 1) % 2, (STEPS - 1) * G, False)

                    @block.tensor
                    def _(pe):
                        def step(i, par, peeled):
                            pe.wait_ge(xn_ready, i + 1)
                            for pair in range(2):
                                bank = turned[2 * par + pair]
                                if not peeled:
                                    pe.wait_ge(turned_used, 4 * (i - 2) + 2 * pair + 2)
                                for j in range(2):
                                    for h in range(HALVES):
                                        t = nc.tensor.transpose(bank[:, h, j, :],
                                                                xn_tok[:, par, 2 * pair + j, h * P:(h + 1) * P],
                                                                ident[:, :])
                                t.then_inc(turned_ready, 1)

                        step(0, 0, True)
                        step(1, 1, True)
                        with pe.Fori(1, STEPS // 2) as k:
                            for par in range(2):
                                step(k * 2 + par, par, False)

                    @block.scalar
                    def _(act):
                        scales = [ones_col, scale_half1]

                        def deviation(i, par):
                            act.wait_ge(moments_done, i + 1)
                            nc.scalar.activation(std[:, :], moments[:, par, :, 1], ACT.Sqrt,
                                                 bias=eps_col[:, 0:1]).then_inc(std_done, 1)

                        def keep_turned(i, par):
                            for pair in range(2):
                                act.wait_ge(turned_ready, i * 2 + pair + 1)
                                blk = i * G + 2 * pair
                                for h in range(HALVES):
                                    nc.scalar.activation(
                                        xn_ch[:, h, ds(blk * P, 2 * P)],
                                        turned[2 * par + pair][:, h, :, :].rearrange("p j c -> p (j c)"),
                                        ACT.Identity, scale=scales[h][:, 0:1],
                                        accum_out=block_sums[:, h, ds(blk, 1)]).then_inc(turned_used, 1)

                        deviation(0, 0)
                        deviation(1, 1)
                        keep_turned(0, 0)
                        with act.Fori(1, STEPS // 2) as k:
                            for par in range(2):
                                deviation(k * 2 + par, par)
                                keep_turned(k * 2 + par - 1, 1 - par)
                        keep_turned(STEPS - 1, 1)

        def ffn(name, last):
            JOBS = CYCLES * TILES_B
            with ExitStack() as scope:
                act1 = sb(name + "_act1", [P, MCH, TILE], F32, scope)
                act2 = sb(name + "_act2", [P, TILE], F32, scope)
                act3 = sb(name + "_act3", [D3, TILE], F32, scope)
                gate = sb(name + "_gate", [P, 2, TILE], F32, scope)
                coupling = sb(name + "_coupling", [P, TILE], F32, scope)
                moved = sb(name + "_moved", [P, HALVES, TILE], F32, scope)
                final = sb(name + "_final", [P, HALVES, TILE], F32, scope)
                mean = sb(name + "_mean", [P, HALVES, BATCH], F32, scope)
                gact1 = sb(name + "_gact1", [P, BATCH], F32, scope)
                gact2 = sb(name + "_gact2", [D3, BATCH], F32, scope)
                gtanh = sb(name + "_gtanh", [P, BATCH], F32, scope)
                base = sb(name + "_base", [P, BATCH], F32, scope)
                ps1 = psum(name + "_ps1", [P, MCH, TILE], scope)
                ps2 = psum(name + "_ps2", [P, TILE], scope)
                ps3 = psum(name + "_ps3", [P, TILE], scope)
                ps4 = psum(name + "_ps4", [P, TILE], scope)
                ps_out = psum(name + "_ps_out", [P, 2, 2, DM], scope)

                mean_done = sem(name + "_mean_done", scope)
                g_prod = sem(name + "_g_prod", scope)
                g_act = sem(name + "_g_act", scope)
                base_done = sem(name + "_base_done", scope)
                l1_done = sem(name + "_l1_done", scope)
                l2_done = sem(name + "_l2_done", scope)
                l3_done = sem(name + "_l3_done", scope)
                l4_done = sem(name + "_l4_done", scope)
                gelu1_done = sem(name + "_gelu1_done", scope)
                gelu2_done = sem(name + "_gelu2_done", scope)
                gelu3_done = sem(name + "_gelu3_done", scope)
                gate_done = sem(name + "_gate_done", scope)
                coupling_done = sem(name + "_coupling_done", scope)
                moved_done = sem(name + "_moved_done", scope)
                state_done = sem(name + "_state_done", scope)
                final_turned = sem(name + "_final_turned", scope)
                residual_done = sem(name + "_residual_done", scope)
                stored = sem(name + "_stored", scope) if last else None

                def state(h, b, s):
                    return xn_ch[:, h, ds((b * TILES_B + s) * TILE, TILE)]

                with nc.Block() as block:
                    @block.tensor
                    def _(pe):
                        pe.wait_ge(mean_done, BATCH + 1)
                        for h in range(HALVES):
                            m = nc.tensor.matmul(ps1[:, 0, 0:BATCH], g1[:, h, :], mean[:, h, :],
                                                 start=(h == 0), stop=(h == HALVES - 1))
                        m.then_inc(g_prod, 1)
                        pe.wait_ge(g_act, 1)
                        nc.tensor.matmul(ps2[0:D3, 0:BATCH], g2[:, :], gact1[:, :], start=True,
                                         stop=True).then_inc(g_prod, 1)
                        pe.wait_ge(g_act, 2)
                        nc.tensor.matmul(ps3[:, 0:BATCH], g3_rep[:, :], gact2[:, :], start=True,
                                         stop=True).then_inc(g_prod, 1)
                        pe.wait_ge(g_act, 3)

                        with pe.Fori(0, BATCH) as b:
                            for n in range(JOBS + 3):
                                if n >= 3:
                                    j = n - 3
                                    pe.wait_ge(gelu3_done, b * JOBS + j + 1)
                                    if j > 0:
                                        pe.wait_ge(gate_done, b * JOBS + j)
                                    nc.tensor.matmul(ps4[:, :], w4_rep[:, :], act3[:, :], start=True,
                                                     stop=True).then_inc(l4_done, 1)
                                if 2 <= n < JOBS + 2:
                                    j = n - 2
                                    pe.wait_ge(gelu2_done, b * JOBS + j + 1)
                                    nc.tensor.matmul(ps3[0:D3, :], w3[:, :], act2[:, :], start=True,
                                                     stop=True).then_inc(l3_done, 1)
                                if 1 <= n < JOBS + 1:
                                    j = n - 1
                                    pe.wait_ge(gelu1_done, MCH * (b * JOBS + j + 1))
                                    for k in range(MCH):
                                        m = nc.tensor.matmul(ps2[:, :], w2[:, k, :], act1[:, k, :],
                                                             start=(k == 0), stop=(k == MCH - 1))
                                    m.then_inc(l2_done, 1)
                                if n >= 3 and (n - 3) >= 2 * TILES_B:
                                    s = (n - 3) % TILES_B
                                    pe.wait_ge(state_done, 2 * (b * JOBS + n - 3 + 1))
                                    for pair in range(2):
                                        if s > 0:
                                            pe.wait_ge(residual_done, (b * TILES_B + s - 1) * 2 + pair + 1)
                                        for j in range(2):
                                            for h in range(HALVES):
                                                tok = (2 * pair + j) * P
                                                m = nc.tensor.transpose(ps_out[:, pair, j, h * P:(h + 1) * P],
                                                                        final[:, h, tok:tok + P], ident[:, :])
                                        m.then_inc(final_turned, 1)
                                if n < JOBS:
                                    s = n % TILES_B
                                    if n >= TILES_B:
                                        pe.wait_ge(state_done, 2 * (b * JOBS + n - TILES_B + 1))
                                    for m_ch in range(MCH):
                                        for h in range(HALVES):
                                            m = nc.tensor.matmul(ps1[:, m_ch, :], w1[:, h, m_ch * P:(m_ch + 1) * P],
                                                                 state(h, b, s), start=(h == 0),
                                                                 stop=(h == HALVES - 1))
                                        m.then_inc(l1_done, 1)

                    @block.scalar
                    def _(act):
                        act.wait_ge(g_prod, 1)
                        nc.scalar.activation(gact1[:, :], ps1[:, 0, 0:BATCH], ACT.Gelu,
                                             bias=gb1[:, 0:1]).then_inc(g_act, 1)
                        act.wait_ge(g_prod, 2)
                        nc.scalar.activation(gact2[:, :], ps2[0:D3, 0:BATCH], ACT.Gelu,
                                             bias=gb2[:, 0:1]).then_inc(g_act, 1)
                        act.wait_ge(g_prod, 3)
                        nc.scalar.activation(gtanh[:, :], ps3[:, 0:BATCH], ACT.Tanh, bias=gb3_half[:, 0:1],
                                             scale=0.5).then_inc(g_act, 1)
                        with act.Fori(0, BATCH) as b:
                            for n in range(JOBS + 3):
                                if n >= 3:
                                    j = n - 3
                                    act.wait_ge(l4_done, b * JOBS + j + 1)
                                    if j >= 2:
                                        act.wait_ge(coupling_done, b * JOBS + j - 1)
                                    nc.scalar.activation(gate[:, j % 2, :], ps4[:, :], ACT.Tanh,
                                                         bias=b4_half[:, 0:1], scale=0.5).then_inc(gate_done, 1)
                                if 2 <= n < JOBS + 2:
                                    act.wait_ge(l3_done, b * JOBS + n - 2 + 1)
                                    if n > 2:
                                        act.wait_ge(l4_done, b * JOBS + n - 2)
                                    nc.scalar.activation(act3[:, :], ps3[0:D3, :], ACT.Gelu,
                                                         bias=b3[:, 0:1]).then_inc(gelu3_done, 1)
                                if 1 <= n < JOBS + 1:
                                    act.wait_ge(l2_done, b * JOBS + n - 1 + 1)
                                    if n > 1:
                                        act.wait_ge(l3_done, b * JOBS + n - 1)
                                    nc.scalar.activation(act2[:, :], ps2[:, :], ACT.Gelu,
                                                         bias=b2[:, 0:1]).then_inc(gelu2_done, 1)
                                if n < JOBS:
                                    for m_ch in range(MCH):
                                        act.wait_ge(l1_done, MCH * (b * JOBS + n) + m_ch + 1)
                                        if n > 0:
                                            act.wait_ge(l2_done, b * JOBS + n)
                                        nc.scalar.activation(act1[:, m_ch, :], ps1[:, m_ch, :], ACT.Gelu,
                                                             bias=b1[:, m_ch:m_ch + 1]).then_inc(gelu1_done, 1)

                    @block.vector
                    def _(dve):
                        per_blk = BLK_B // 2
                        for b in range(BATCH):
                            sums = block_sums[:, :, b * BLK_B:(b + 1) * BLK_B].rearrange(
                                "p h (n two) -> p h n two", two=2)[:, :, :, 0]
                            nc.vector.tensor_reduce(mean[:, :, b:b + 1], sums, AX_X, ALU.add)\
                                .then_inc(mean_done, 1)
                        dve.wait_ge(mean_done, BATCH)
                        nc.vector.tensor_scalar(mean[:, :, :], mean[:, :, :], 1.0 / SEQ, None,
                                                ALU.mult).then_inc(mean_done, 1)
                        dve.wait_ge(g_act, 3)
                        nc.vector.tensor_scalar(base[:, :], gtanh[:, :], rng[:, 0:1], 0.7, ALU.mult,
                                                ALU.mult).then_inc(base_done, 1)
                        dve.wait_ge(base_done, 1)
                        nc.vector.tensor_scalar(base[:, :], base[:, :], 0.1, None, ALU.add)\
                            .then_inc(base_done, 1)
                        dve.wait_ge(base_done, 2)
                        with dve.Fori(0, BATCH) as b:
                            def residual(s):
                                for pair in range(2):
                                    dve.wait_ge(final_turned, (b * TILES_B + s) * 2 + pair + 1)
                                    blk = (b * TILES_B + s) * BLK_T + 2 * pair
                                    kept, turned = DM - P // 2, P // 2
                                    nc.vector.scalar_tensor_tensor(
                                        x_tok[:, ds(blk, 2), 0:kept], ps_out[:, pair, :, 0:kept], 0.5,
                                        x_tok[:, ds(blk, 2), 0:kept], ALU.mult, ALU.add)
                                    nc.vector.scalar_tensor_tensor(
                                        x_tok[:, ds(blk, 2), kept:DM], ps_out[:, pair, :, kept:DM], -0.5,
                                        x_tok[:, ds(blk, 2), kept:DM], ALU.mult, ALU.add)\
                                        .then_inc(residual_done, 1)

                            for j in range(JOBS):
                                s = j % TILES_B
                                dst = final if j >= 2 * TILES_B else None
                                dve.wait_ge(gate_done, b * JOBS + j + 1)
                                nc.vector.tensor_scalar(coupling[:, :], gate[:, j % 2, :], gain[:, 0:1],
                                                        base[:, ds(b, 1)], ALU.mult, ALU.add)\
                                    .then_inc(coupling_done, 1)
                                dve.wait_ge(coupling_done, b * JOBS + j + 1)
                                both = xn_ch[:, :, ds((b * TILES_B + s) * TILE, TILE)]
                                nc.vector.tensor_tensor(
                                    moved[:, :, :], both,
                                    coupling[:, :].unsqueeze(1).broadcast_to([P, HALVES, TILE]), ALU.mult)\
                                    .then_inc(moved_done, 1)
                                dve.wait_ge(moved_done, b * JOBS + j + 1)
                                if dst is not None and s > 0:
                                    dve.wait_ge(final_turned, (b * TILES_B + s) * 2)
                                d0 = dst[:, 0, :] if dst is not None else state(0, b, s)
                                d1 = dst[:, 1, :] if dst is not None else state(1, b, s)
                                nc.vector.tensor_tensor(d0, state(0, b, s), moved[:, 1, :], ALU.add)\
                                    .then_inc(state_done, 1)
                                nc.vector.tensor_tensor(d1, state(1, b, s), moved[:, 0, :], ALU.subtract)\
                                    .then_inc(state_done, 1)
                                if j >= 2 * TILES_B:
                                    residual(s)

                    if last:
                        @block.sync
                        def _(sp):
                            for k in range(BATCH * TILES_B):
                                sp.wait_ge(residual_done, k * 2 + 2)
                                sp.dma_start(out_blocks[:, k * BLK_T:(k + 1) * BLK_T, :],
                                             x_tok[:, k * BLK_T:(k + 1) * BLK_T, :]).then_inc(stored, 16)
                            sp.wait_ge(stored, 16 * BATCH * TILES_B)

        HEADS, DH = 16, DM // 16
        FEAT = proj.shape[0]
        STRIP = 32
        PER_G = P // STRIP
        GROUPS = HEADS // PER_G
        HALF_HEADS = HEADS // 2
        SCALE = DH ** -0.5
        X_SCALE = sqrt(SCALE)
        FSCALE = 4096.0
        UNSCALE = 1.0 / (FSCALE * FSCALE)
        WSCALE = 64.0
        LOCAL_SHARE = 1.0 - SCALE
        assert DH == 16 and FEAT == 24 and GROUPS == 4 and PER_G == 4

        def attention():
            with ExitStack() as scope:
                wq_s = [sb(f"wq_s_{part}", [P, HALVES, HEADS * STRIP], F16, scope) for part in ("high", "low")]
                wk_s = [sb(f"wk_s_{part}", [P, HALVES, HEADS * STRIP], F16, scope) for part in ("high", "low")]
                w_vq = [sb(f"w_vq_{part}", [P, HALVES, 2 * DM], F16, scope) for part in ("high", "low")]
                w_qf = [sb(f"w_qf_{part}", [P, HALVES, HEADS * FEAT], F16, scope) for part in ("high", "low")]
                w_o = sb("w_o", [P, HALVES, DM], F32, scope)
                bq_s = sb("bq_s", [P, GROUPS], F32, scope)
                bk_s = sb("bk_s", [P, GROUPS], F32, scope)
                b_vq = sb("b_vq", [P, 2 * DM], F32, scope)
                b_qf = sb("b_qf", [P, HEADS * FEAT], F32, scope)
                b_o = sb("b_o", [P, DM], F32, scope)
                log_k = nc.dram_tensor("log_k", (NBLK + 2, P, GROUPS, P), F32, kind="Internal").ap()
                neg_kmax = sb("neg_kmax", [P, NBLK + 1, GROUPS], F32, scope)
                kmax_tok = sb("kmax_tok", [P, NBLK + 1, HEADS], F32, scope)
                penalty = sb("penalty", [P, NBLK + 1], F32, scope)
                has_prev = sb("has_prev", [P, NBLK + 1], F32, scope)
                keep_state = sb("keep_state", [P, NBLK + 1], F32, scope)
                low_rows = sb("low_rows", [P, 1], F32, scope)
                ident16 = sb("ident16", [P, P], BF16, scope)
                mask_q = sb("mask_q", [P, 2, 2, P], BF16, scope)
                stair_own_l = sb("stair_own_l", [P, P], BF16, scope)
                stair_prev_l = sb("stair_prev_l", [P, P], BF16, scope)
                stair_own_r = sb("stair_own_r", [P, HEADS, P], BF16, scope)
                stair_prev_r = sb("stair_prev_r", [P, HEADS, P], BF16, scope)
                gmask = sb("gmask", [P, 2, P], F32, scope)
                diag_strips = sb("diag_strips", [P, PER_G, STRIP], F32, scope)

                def attention_weights(outer):
                    with ExitStack() as scope:
                        rows = sb("qkv_rows", [P, 3 * HALVES, DM], F32, scope)
                        o_rows = sb("o_rows", [P, HALVES, DM], F32, scope)
                        bq_col = sb("bq_col", [P, HALVES], F32, scope)
                        bq_rep = sb("bq_rep", [P, HALVES, P], F32, scope)
                        ps = [psum(f"prep_ps{i}", [P, 512], scope) for i in range(8)]
                        loaded = sem("prep_loaded", scope)
                        blank = sem("prep_blank", scope)
                        drawn = sem("prep_drawn", scope)
                        tables = sem("prep_tables", scope)
                        product = sem("prep_product", scope)
                        evacuated = sem("prep_evacuated", scope)
                        reps = sem("prep_reps", scope)
                        high_kept = sem("prep_high_kept", scope)

                        row = lambda v, n: v.rearrange("(a n) -> a n", a=1).broadcast_to([P, n])
                        loads = [
                            (rows[:, :, :], wqkv.rearrange("(k p) n -> p k n", p=P)),
                            (o_rows[:, :, :], wout.rearrange("(k p) n -> p k n", p=P)),
                            (bq_col[:, :], bqkv[0:DM].rearrange("(k p) -> p k", p=P)),
                            (bk_col[:, :], bqkv[DM:2 * DM].rearrange("(k p) -> p k", p=P)),
                            (b_vq[:, 0:DM], row(bqkv[2 * DM:3 * DM], DM)),
                            (b_vq[:, DM:2 * DM], row(bqkv[0:DM], DM)),
                            (b_o[:, :], row(bout, DM)),
                        ]
                        for j in range(HALF_HEADS):
                            loads.append((proj_bd[j * DH:(j + 1) * DH, j, :], proj.rearrange("m d -> d m")))
                        for which, dst in ((0, bq_s), (1, bk_s)):
                            src = bqkv[which * DM:(which + 1) * DM].rearrange("(g r d) -> r d g", g=GROUPS, r=PER_G)
                            for r in range(PER_G):
                                for dup in range(2):
                                    at = r * STRIP + dup * DH
                                    loads.append((dst[at:at + DH, :], src[r]))

                        jobs = []
                        for k in range(HALVES):
                            for i in range(HALVES):
                                def strips(w, dup, k=k, i=i):
                                    return [part[:, k, i * HALF_HEADS * STRIP:(i + 1) * HALF_HEADS * STRIP].rearrange(
                                        "p (h s) -> p h s", s=STRIP)[:, :, dup * DH:(dup + 1) * DH] for part in w]

                                def halves(w, at, k=k):
                                    return [part[:, k, at] for part in w]
                                heads = "p (h d) -> p h d"
                                jobs.append((("turn", rows, i, k), [(strips(wq_s, 0), SCALE, heads), (strips(wq_s, 1), SCALE, heads),
                                                                    (halves(w_vq, slice(DM + i * P, DM + (i + 1) * P)), 1.0, None)]))
                                jobs.append((("turn", rows, 2 + i, k), [(strips(wk_s, 0), 1.0, heads), (strips(wk_s, 1), 1.0, heads),
                                                                        (w_k[:, k, i * P:(i + 1) * P], 1.0, None)]))
                                jobs.append((("turn", rows, 4 + i, k), [(halves(w_vq, slice(i * P, (i + 1) * P)), 1.0, None)]))
                                jobs.append((("turn", o_rows, i, k), [(w_o[:, k, i * P:(i + 1) * P], 1.0, None)]))
                                jobs.append((("feat", rows, i, k), [(halves(w_qf, slice(i * HALF_HEADS * FEAT, (i + 1) * HALF_HEADS * FEAT)),
                                                                     X_SCALE, None)]))
                        for i in range(HALVES):
                            jobs.append((("bias", bq_rep, i, 0), [(b_qf[:, i * HALF_HEADS * FEAT:(i + 1) * HALF_HEADS * FEAT],
                                                                   X_SCALE, None)]))

                        def evacuations(n):
                            (kind, *_), views = jobs[n]
                            src = ps[n % 8][:, 0:P if kind == "turn" else HALF_HEADS * FEAT]
                            return [(view, scale, src.rearrange(split, d=DH) if split else src)
                                    for view, scale, split in views]

                        highs_until = [sum(isinstance(view, list) for _, views in jobs[:n + 1] for view, *_ in views)
                                       for n in range(len(jobs))]

                        with nc.Block() as block:
                            @block.sync
                            def _(sp):
                                sp.wait_ge(blank, 1)
                                for dst, src in loads:
                                    sp.dma_start(dst, src, allow_slow_non_contiguous=True).then_inc(loaded, 16)

                            @block.gpsimd
                            def _(pool):
                                nc.gpsimd.memset(proj_bd[:, :, :], 0.0).then_inc(blank, 1)
                                zero = [(ident16, 0.0), (mask_q, 0.0), (stair_own_l, 1.0), (stair_prev_l, 1.0),
                                        (stair_own_r, 0.0), (stair_prev_r, 0.0), (gmask[:, 0, :], LOCAL_SHARE),
                                        (gmask[:, 1, :], 1.0), (diag_strips, 1.0), (low_rows, 1.0),
                                        (penalty, 0.0), (has_prev, 1.0), (keep_state, 1.0),
                                        ]
                                for buf, value in zero:
                                    last = nc.gpsimd.memset(buf if isinstance(buf, bass.AP) else buf[tuple([slice(None)] * len(buf.shape))], value)
                                last.then_inc(blank, 1)
                                pool.wait_ge(blank, 2)

                                selected = [0]

                                def select(view, op, fill, base, pattern, mult):
                                    selected[0] += 1
                                    nc.gpsimd.affine_select(out=view, in_=view, compare_op=op, fill=fill, base=base,
                                                            pattern=pattern, channel_multiplier=mult)\
                                        .then_inc(drawn, 1)
                                    pool.wait_ge(drawn, selected[0])

                                select(ident16[:, :], ALU.not_equal, 1.0, 0, [[-1, P]], 1)
                                for order in range(2):
                                    own, prev = 1 - order, order
                                    select(mask_q[:, order, own, :], ALU.is_ge, MASKED, 0, [[-1, P]], 1)
                                    select(mask_q[:, order, prev, :], ALU.is_ge, MASKED, 0, [[1, P]], -1)
                                select(stair_own_l[:, :], ALU.is_ge, 0.0, 0, [[1, P]], -1)
                                select(stair_prev_l[:, :], ALU.is_ge, 0.0, 0, [[-1, P]], 1)
                                select(stair_own_r[:, :, :], ALU.not_equal, MASKED, -1, [[0, HEADS], [-1, P]], 1)
                                select(stair_prev_r[:, :, :], ALU.not_equal, MASKED, 1, [[0, HEADS], [-1, P]], 1)
                                select(gmask[:, 0, :], ALU.is_ge, 0.0, 0, [[1, P]], -1)
                                select(gmask[:, 1, :], ALU.is_gt, LOCAL_SHARE, 0, [[1, P]], -1)
                                select(diag_strips[:, :, :], ALU.is_ge, 0.0, 0, [[-STRIP, PER_G], [0, STRIP]], 1)
                                select(diag_strips[:, :, :], ALU.is_ge, 0.0, STRIP - 1, [[STRIP, PER_G], [0, STRIP]], -1)
                                first_of_batch = [b * BLK_B for b in range(BATCH + 1)]
                                for blk in first_of_batch:
                                    nc.gpsimd.memset(penalty[:, blk:blk + 1], MASKED)
                                    nc.gpsimd.memset(has_prev[:, blk:blk + 1], 0.0)
                                    nc.gpsimd.memset(keep_state[:, blk:blk + 1], 0.0)
                                    if blk:
                                        nc.gpsimd.memset(keep_state[:, blk - 1:blk], 0.0)
                                nc.gpsimd.memset(ident16[0:1, 0:1], 1.0).then_inc(tables, 1)

                            @block.vector
                            def _(dve):
                                dve.wait_ge(loaded, 16 * len(loads))
                                nc.vector.tensor_copy(bq_rep[:, :, :], bq_col[:, :].unsqueeze(2).broadcast_to([P, HALVES, P]))\
                                    .then_inc(reps, 1)
                                dve.wait_ge(tables, 1)
                                nc.vector.tensor_reduce(
                                    low_rows[:, :],
                                    ident16[:, :].rearrange("p (r two d) -> p r two d", two=2, d=DH)[:, :, 1, :],
                                    mybir.AxisListType.XY, ALU.add)
                                nc.vector.tensor_scalar(bq_s[:, :], bq_s[:, :], SCALE, None, ALU.mult)
                                for n in range(len(jobs)):
                                    dve.wait_ge(product, n + 1)
                                    if highs_until[n] > (highs_until[n - 1] if n else 0):
                                        dve.wait_ge(high_kept, highs_until[n])
                                    for view, scale, src in evacuations(n):
                                        if isinstance(view, list):
                                            last = nc.vector.scalar_tensor_tensor(view[1], src, scale * WSCALE, view[0],
                                                                                  ALU.mult, ALU.subtract)
                                        else:
                                            last = nc.vector.tensor_scalar(view, src, scale, None, ALU.mult)
                                    last.then_inc(evacuated, 1)

                            @block.scalar
                            def _(act):
                                for n in range(len(jobs)):
                                    parted = [e for e in evacuations(n) if isinstance(e[0], list)]
                                    if parted:
                                        act.wait_ge(product, n + 1)
                                    for view, scale, src in parted:
                                        nc.scalar.activation(view[0], src, ACT.Copy, scale=scale * WSCALE)\
                                            .then_inc(high_kept, 1)

                            @block.tensor
                            def _(pe):
                                pe.wait_ge(loaded, 16 * len(loads))
                                for n, ((kind, src, i, k), _) in enumerate(jobs):
                                    if n >= 8:
                                        pe.wait_ge(evacuated, n - 7)
                                    bank = ps[n % 8]
                                    if kind == "turn":
                                        last = nc.tensor.transpose(bank[:, 0:P], src[:, i, k * P:(k + 1) * P], ident[:, :])
                                    else:
                                        if kind == "bias":
                                            pe.wait_ge(reps, 1)
                                        left = src[:, i, k * P:(k + 1) * P] if kind == "feat" else src[:, i, :]
                                        last = nc.tensor.matmul(bank[:, 0:HALF_HEADS * FEAT], left,
                                                                proj_bd[:, :, :].rearrange("p h m -> p (h m)"),
                                                                start=True, stop=True)
                                    last.then_inc(product, 1)

                def key_features(outer):
                    TILES = NBLK // BLK_T
                    with ExitStack() as scope:
                        lift = sb("lift", [P, 2, PER_G, STRIP], F32, scope)
                        halve = sb("halve", [P, HALF_HEADS, STRIP], F32, scope)
                        ones_sq = sb("ones_sq", [P, P], F32, scope)
                        strip_head = sb("strip_head", [P, PER_G], F32, scope)
                        k_and_sq = sb("k_and_sq", [P, 2, GROUPS, TILE], F32, scope)
                        logs_sb = sb("logs_sb", [P, 2, GROUPS, TILE], F32, scope)
                        no_logs = sb("no_logs", [P, GROUPS, P], F32, scope)
                        tile_max = sb("tile_max", [P, BATCH, GROUPS, TILES_B], F32, scope)
                        row_max = sb("row_max", [P, STRIP], F32, scope)
                        row_max_t = sb("row_max_t", [P, STRIP], F32, scope)
                        head_max = sb("head_max", [P, 1], F32, scope)
                        head_max_b = sb("head_max_b", [P, STRIP], F32, scope)
                        kmax = sb("kmax", [P, STRIP], F32, scope)
                        one_row = sb("one_row", [P, BATCH, GROUPS, PER_G], F32, scope)
                        ps_k = psum("ps_k", [P, HALVES, TILE], scope)
                        ps_log = psum("ps_log", [P, GROUPS, TILE], scope)
                        ps_spread = psum("ps_spread", [P, 512], scope)
                        blank = sem("kf_blank", scope)
                        drawn = sem("kf_drawn", scope)
                        lift_ready = sem("lift_ready", scope)
                        k_product = sem("k_product", scope)
                        k_ready = sem("k_ready", scope)
                        k_sq_ready = sem("k_sq_ready", scope)
                        log_product = sem("log_product", scope)
                        log_kept = sem("log_kept", scope)
                        log_max = sem("log_max", scope)
                        log_stored = [sem(f"log_stored{i}", scope) for i in range(2)]
                        pad_stored = sem("pad_stored", scope)
                        chain = sem("kmax_chain", scope)
                        spread = sem("kmax_spread", scope)
                        with nc.Block() as block:
                            @block.gpsimd
                            def _(pool):
                                nc.gpsimd.memset(halve[:, :, :], -SCALE / 2)
                                nc.gpsimd.memset(strip_head[:, :], 0.0)
                                nc.gpsimd.memset(row_max[:, :], 0.0)
                                nc.gpsimd.memset(no_logs[:, :, :], 0.0)
                                nc.gpsimd.memset(ones_sq[:, :], 1.0).then_inc(blank, 1)
                                pool.wait_ge(blank, 1)
                                nc.gpsimd.affine_select(out=halve[:, :, :], in_=halve[:, :, :], compare_op=ALU.is_ge, fill=0.0,
                                                        base=0, pattern=[[-DH, HALF_HEADS], [0, STRIP]], channel_multiplier=1)\
                                    .then_inc(blank, 1)
                                pool.wait_ge(blank, 2)
                                nc.gpsimd.affine_select(out=halve[:, :, :], in_=halve[:, :, :], compare_op=ALU.is_ge, fill=0.0,
                                                        base=DH - 1, pattern=[[DH, HALF_HEADS], [0, STRIP]], channel_multiplier=-1)
                                nc.gpsimd.affine_select(out=strip_head[:, :], in_=strip_head[:, :], compare_op=ALU.not_equal,
                                                        fill=1.0, base=0, pattern=[[-STRIP, PER_G]], channel_multiplier=1)\
                                    .then_inc(drawn, 1)

                            @block.tensor
                            def _(pe):
                                def keys(n):
                                    for i in range(HALVES):
                                        for k in range(HALVES):
                                            m = nc.tensor.matmul(ps_k[:, i, :], w_k[:, k, i * P:(i + 1) * P],
                                                                 xn_ch[:, k, ds(n * TILE, TILE)], start=(k == 0),
                                                                 stop=(k == HALVES - 1))
                                    m.then_inc(k_product, 1)

                                def logs(n, par, peeled):
                                    pe.wait_ge(k_sq_ready, n + 1)
                                    for g in range(GROUPS):
                                        if not peeled:
                                            pe.wait_ge(log_kept, (n - 1) * GROUPS + g + 1)
                                            pe.wait_ge(log_max, (n - 1) * GROUPS + g + 1)
                                        nc.tensor.matmul(ps_log[:, g, :], lift[:, g % 2, :, :].rearrange("p h m -> p (h m)"),
                                                         k_and_sq[:, par, g, :], start=True, stop=True)\
                                            .then_inc(log_product, 1)

                                pe.wait_ge(drawn, 1)
                                pe.wait_ge(lift_ready, 1)
                                keys(0)
                                for n in range(2):
                                    pe.wait_ge(k_ready, n + 1)
                                    keys(n + 1)
                                    logs(n, n, n == 0)
                                with pe.Fori(1, TILES // 2 - 1) as j:
                                    for par in range(2):
                                        n = j * 2 + par
                                        pe.wait_ge(k_ready, n + 1)
                                        keys(n + 1)
                                        logs(n, par, False)
                                for n in range(TILES - 2, TILES):
                                    pe.wait_ge(k_ready, n + 1)
                                    if n + 1 < TILES:
                                        keys(n + 1)
                                    logs(n, n % 2, False)
                                pe.wait_ge(chain, 7)
                                nc.tensor.matmul(ps_spread[:, 0:BATCH * HEADS], ones_sq[:, :],
                                                 one_row[:, :, :, :].rearrange("p b g r -> p (b g r)"), start=True,
                                                 stop=True).then_inc(spread, 1)

                            @block.scalar
                            def _(act):
                                def tile(n, par, peeled):
                                    act.wait_ge(k_ready, n + 1)
                                    if not peeled:
                                        act.wait_ge(log_product, (n - 1) * GROUPS)
                                    for q in range(2):
                                        own, other = slice(q * P // 2, (q + 1) * P // 2), slice((1 - q) * P // 2, (2 - q) * P // 2)
                                        a = nc.scalar.activation(k_and_sq[other, par, q::2, :], k_and_sq[own, par, q::2, :],
                                                                 ACT.Square)
                                    a.then_inc(k_sq_ready, 1)

                                def keep_logs(n, par, before):
                                    if before is not None:
                                        act.wait_ge(log_stored[par], 16 * before)
                                    for g in range(GROUPS):
                                        act.wait_ge(log_product, n * GROUPS + g + 1)
                                        act.wait_ge(log_max, n * GROUPS + g + 1)
                                        nc.scalar.activation(logs_sb[:, par, g, :], ps_log[:, g, :],
                                                             ACT.Identity).then_inc(log_kept, 1)

                                tile(0, 0, True)
                                tile(1, 1, True)
                                keep_logs(0, 0, None)
                                tile(2, 0, False)
                                keep_logs(1, 1, None)
                                tile(3, 1, False)
                                keep_logs(2, 0, 1)
                                with act.Fori(2, TILES // 2) as j:
                                    tile(j * 2, 0, False)
                                    keep_logs(j * 2 - 1, 1, j - 1)
                                    tile(j * 2 + 1, 1, False)
                                    keep_logs(j * 2, 0, j)
                                keep_logs(TILES - 1, 1, TILES // 2 - 1)

                            @block.sync
                            def _(sp):
                                for n in range(TILES):
                                    sp.wait_ge(log_kept, (n + 1) * GROUPS)
                                    sp.dma_start(log_k[n * BLK_T:(n + 1) * BLK_T, :, :, :].rearrange("a p g q -> p g a q"),
                                                 logs_sb[:, n % 2, :, :].rearrange("p g (a q) -> p g a q", q=P))\
                                        .then_inc(log_stored[n % 2], 16)
                                sp.wait_ge(drawn, 1)
                                for pad in range(2):
                                    sp.dma_start(log_k[NBLK + pad, :, :, :], no_logs[:, :, :]).then_inc(pad_stored, 16)
                                for stored in log_stored:
                                    sp.wait_ge(stored, 16 * (TILES // 2))
                                sp.wait_ge(pad_stored, 32)

                            @block.vector
                            def _(dve):
                                dve.wait_ge(drawn, 1)
                                for q in range(2):
                                    own, other = slice(q * P // 2, (q + 1) * P // 2), slice((1 - q) * P // 2, (2 - q) * P // 2)
                                    mine, theirs = slice(q * PER_G, (q + 1) * PER_G), slice((1 - q) * PER_G, (2 - q) * PER_G)
                                    nc.vector.tensor_scalar(lift[own, q, :, 0:FEAT], proj_bd[own, mine, :], X_SCALE, None,
                                                            ALU.mult)
                                    nc.vector.tensor_scalar(lift[own, q, :, FEAT:STRIP],
                                                            proj_bd[own, mine, 0:1].broadcast_to([P // 2, PER_G, STRIP - FEAT]),
                                                            X_SCALE, None, ALU.mult)
                                    last = nc.vector.tensor_copy(lift[other, q, :, :], halve[other, theirs, :])
                                last.then_inc(lift_ready, 1)

                                def keys(n):
                                    dve.wait_ge(k_product, n + 1)
                                    if n >= 2:
                                        dve.wait_ge(log_product, (n - 1) * GROUPS)
                                    for q in range(2):
                                        own = slice(q * P // 2, (q + 1) * P // 2)
                                        k = nc.vector.tensor_tensor(
                                            k_and_sq[own, n % 2, q::2, :], ps_k[own, :, :],
                                            bk_col[own, :].unsqueeze(2).broadcast_to([P // 2, HALVES, TILE]), ALU.add)
                                    k.then_inc(k_ready, 1)

                                keys(0)
                                for b in range(BATCH):
                                    for s in range(TILES_B):
                                        if b * TILES_B + s + 1 < TILES:
                                            keys(b * TILES_B + s + 1)
                                        for g in range(GROUPS):
                                            n = (b * TILES_B + s) * GROUPS + g
                                            dve.wait_ge(log_product, n + 1)
                                            nc.vector.tensor_reduce(tile_max[:, b, g, s:s + 1], ps_log[:, g, :], AX_X,
                                                                    ALU.max).then_inc(log_max, 1)
                                dve.wait_ge(log_max, NBLK // BLK_T * GROUPS)
                                dve.wait_ge(drawn, 1)

                                steps = [0]

                                def link(ins):
                                    steps[0] += 1
                                    ins.then_inc(chain, 1)
                                    dve.wait_ge(chain, steps[0])

                                link(nc.vector.tensor_reduce(row_max[:, 0:BATCH * GROUPS],
                                                             tile_max[:, :, :, :].rearrange("p b g s -> p (b g) s"), AX_X, ALU.max))
                                link(nc.vector.transpose(row_max_t[:, :], row_max[:, :]))
                                link(nc.vector.tensor_reduce(head_max[:, :], row_max_t[:, :], AX_X, ALU.max))
                                link(nc.vector.tensor_copy(head_max_b[:, :], head_max[:, :].broadcast_to([P, STRIP])))
                                link(nc.vector.transpose(kmax[:, :], head_max_b[:, :]))
                                km = kmax[:, 0:BATCH * GROUPS].rearrange("p (b g) -> p b g", b=BATCH)
                                link(nc.vector.memset(neg_kmax[:, NBLK:, :], 0.0))
                                link(nc.vector.tensor_tensor(
                                    one_row[:, :, :, :].rearrange("p b g r -> p (b g) r"),
                                    kmax[:, 0:BATCH * GROUPS].unsqueeze(2).broadcast_to([P, BATCH * GROUPS, PER_G]),
                                    strip_head[:, :].unsqueeze(1).broadcast_to([P, BATCH * GROUPS, PER_G]), ALU.mult))
                                for b in range(BATCH):
                                    nc.vector.tensor_scalar(neg_kmax[:, b * BLK_B:(b + 1) * BLK_B, :],
                                                            km[:, b:b + 1, :].broadcast_to([P, BLK_B, GROUPS]), -1.0, None,
                                                            ALU.mult)
                                dve.wait_ge(spread, 1)
                                nc.vector.memset(kmax_tok[:, NBLK:, :], 0.0)
                                for b in range(BATCH):
                                    nc.vector.tensor_copy(
                                        kmax_tok[:, b * BLK_B:(b + 1) * BLK_B, :],
                                        ps_spread[:, b * HEADS:(b + 1) * HEADS].unsqueeze(1).broadcast_to([P, BLK_B, HEADS]))

                def attention_blocks(outer):
                    RING = 4
                    FEATURE_ITEMS = (5, 7, 9, 12)
                    with ExitStack() as scope:
                        x_high = sb("x_high", [P, 2, HALVES, P], F16, scope)
                        x_low = sb("x_low", [P, 2, HALVES, P], F16, scope)
                        q32 = sb("q32", [P, GROUPS, P], F32, scope)
                        k32 = sb("k32", [P, GROUPS, P], F32, scope)
                        q_high = sb("q_high", [P, GROUPS, P], F16, scope)
                        q_low = sb("q_low", [P, GROUPS, P], F16, scope)
                        k_lowhigh = sb("k_lowhigh", [P, GROUPS, P], F16, scope)
                        q_bd = sb("q_bd", [P, 2, 2, GROUPS, PER_G, P], F16, scope)
                        k_mix = sb("k_mix", [P, GROUPS, RING, P], F16, scope)
                        v_ext = sb("v_ext", [P, RING, HEADS, STRIP], F32, scope)
                        q_tok = sb("q_tok", [P, DM], F32, scope)
                        qf_tok = sb("qf_tok", [P, HEADS, FEAT], F32, scope)
                        qf_pad = sb("qf_pad", [P, HEADS, STRIP], F32, scope)
                        q_norm = sb("q_norm", [P, HEADS], F32, scope)
                        qf_max = sb("qf_max", [P, HEADS], F32, scope)
                        q_scale = sb("q_scale", [P, HEADS], F32, scope)
                        g_scale = sb("g_scale", [P, 2, HEADS], F32, scope)
                        log_blk = sb("log_blk", [P, GROUPS, P], F32, scope)
                        scaled_eps = sb("scaled_eps", [P, 1], F32, scope)
                        kf32 = sb("kf32", [P, GROUPS, P], F32, scope)
                        kf_high = sb("kf_high", [P, RING, GROUPS, P], F16, scope)
                        kf_low = sb("kf_low", [P, RING, GROUPS, P], F16, scope)
                        kf_tok = sb("kf_tok", [P, 2, HEADS * STRIP], F32, scope)
                        qf32 = sb("qf32", [P, 2, GROUPS, P], F32, scope)
                        qf_high = sb("qf_high", [P, GROUPS, P], F16, scope)
                        qf_low = sb("qf_low", [P, GROUPS, P], F16, scope)
                        qf_bd = sb("qf_bd", [P, 2, 1, GROUPS, PER_G, P], F16, scope)
                        block_max = sb("block_max", [P, GROUPS, PER_G, 2], F32, scope)
                        row_top = sb("row_top", [P, HEADS], F32, scope)
                        neg_max = sb("neg_max", [P, 2, HEADS], BF16, scope)
                        max_rows = sb("max_rows", [2 * HEADS, P], BF16, scope)
                        lift_arg = sb("lift_arg", [P, HEADS], F32, scope)
                        lift_exp = sb("lift_exp", [P, 2, HEADS], F32, scope)
                        probs = sb("probs", [P, 2, 2, PER_G, P], F32, scope)
                        feats = sb("feats", [P, 2, 2, PER_G, P], F32, scope)
                        state = sb("kv_state", [P, GROUPS, P], F32, scope)
                        state_inc = sb("kv_state_inc", [P, GROUPS, P], F32, scope)
                        sums = sb("sums", [P, 2, GROUPS * P], F32, scope)
                        r_local = sb("r_local", [P, HEADS], F32, scope)
                        norm_a = sb("norm_a", [P, HEADS], F32, scope)
                        norm_b = sb("norm_b", [P, HEADS], F32, scope)
                        norm_c = sb("norm_c", [P, HEADS], F32, scope)
                        norm_r = sb("norm_r", [P, HEADS], F32, scope)
                        r_global = sb("r_global", [P, HEADS], F32, scope)
                        ctx_a = sb("ctx_a", [P, HEADS, DH], F32, scope)
                        ctx = sb("ctx", [P, DM], F32, scope)
                        ctx_ch = sb("ctx_ch", [P, HALVES, P], F32, scope)

                        pairs = [psum(f"pair{i}", [P, 2, 512], scope) for i in range(3)]
                        ps_local = psum("ps_local", [P, GROUPS * P], scope)
                        ps_global = psum("ps_global", [P, GROUPS * P], scope)

                        def pair(item):
                            return pairs[item % 3]

                        PASSES = ((0, x_high), (1, x_high), (0, x_low))

                        def S(name):
                            return sem("a_" + name, scope)

                        cleared, cleared_dve = S("cleared"), S("cleared_dve")
                        x_high_ready, x_ready = S("x_high_ready"), S("x_ready")
                        qk_product, q32_ready, k32_ready = S("qk_product"), S("q32_ready"), S("k32_ready")
                        q_high_ready, k_lowhigh_ready = S("q_high_ready"), S("k_lowhigh_ready")
                        q_low_ready, k_mix_ready, q_bd_ready = S("q_low_ready"), S("k_mix_ready"), S("q_bd_ready")
                        vq_product, v_ready, q_tok_ready, qf_ready = S("vq_product"), S("v_ready"), S("q_tok_ready"), S("qf_ready")
                        q_sq_ready, q_norm_ready, qf_max_ready, qf_shifted = S("q_sq_ready"), S("q_norm_ready"), S("qf_max_ready"), S("qf_shifted")
                        q_scale_ready, g_scale_ready = S("q_scale_ready"), S("g_scale_ready")
                        qf_exp_ready, qf_pad_ready = S("qf_exp_ready"), S("qf_pad_ready")
                        log_loaded = S("log_loaded")
                        kf_exp_ready, kf32_ready, kf_high_ready, kf_low_ready = S("kf_exp_ready"), S("kf32_ready"), S("kf_high_ready"), S("kf_low_ready")
                        turned, qf32_ready, kf_tok_ready = S("turned"), S("qf32_ready"), S("kf_tok_ready")
                        qf_high_ready, qf_low_ready, qf_bd_ready = S("qf_high_ready"), S("qf_low_ready"), S("qf_bd_ready")
                        qs_product, qs_max = S("qs_product"), S("qs_max")
                        row_top_ready, neg_max_ready, penal_ready = S("row_top_ready"), S("neg_max_ready"), S("penal_ready")
                        lift_arg_ready, lift_exp_ready = S("lift_arg_ready"), S("lift_exp_ready")
                        max_turned, max_rows_ready, max_placed = S("max_turned"), S("max_rows_ready"), S("max_placed")
                        f_product, f_ready = S("f_product"), S("f_ready")
                        ks_product, p_ready = S("ks_product"), S("p_ready")
                        global_done, local_done = S("global_done"), S("local_done")
                        state_read, inc_product, inc_ready, state_ready = S("state_read"), S("inc_product"), S("inc_ready"), S("state_ready")
                        sums_ready, sums_turned = S("sums_ready"), S("sums_turned")
                        norm_parts, norm_ready = S("norm_parts"), S("norm_ready")
                        r_ready, ctx_parts, ctx_ready = S("r_ready"), S("ctx_parts"), S("ctx_ready")
                        ctx_turned, ctx_ch_ready = S("ctx_turned"), S("ctx_ch_ready")
                        y_product, y_ready, x_biased = S("y_product"), S("y_ready"), S("x_biased")

                        def wait(eng, signal, count):
                            if not isinstance(count, int) or count > 0:
                                eng.wait_ge(signal, count)

                        def flat(v):
                            return v.rearrange("p a b -> p (a b)")

                        def scheduled(eng, one_block):
                            for par in range(RING):
                                one_block(par, par)
                            with eng.Fori(1, NBLK // RING) as i:
                                for par in range(RING):
                                    one_block(i * RING + par, par)

                        with nc.Block() as block:
                            @block.gpsimd
                            def _(pool):
                                nc.gpsimd.memset(scaled_eps[:, :], FEATURE_EPS * FSCALE).then_inc(cleared, 1)
                                for buf in (v_ext, kf_tok, qf_pad, state):
                                    last = nc.gpsimd.memset(buf[tuple([slice(None)] * len(buf.shape))], 0.0)
                                last.then_inc(cleared, 1)
                                pool.wait_ge(cleared, 2)
                                nc.gpsimd.memset(v_ext[:, :, :, DH:DH + 1], 1.0).then_inc(cleared, 1)

                                def low_x(f, par):
                                    pool.wait_ge(x_high_ready, f + 1)
                                    nc.gpsimd.tensor_tensor(x_low[:, par % 2, :, :], xn_ch[:, :, ds(f * P, P)],
                                                            x_high[:, par % 2, :, :], ALU.subtract).then_inc(x_ready, 1)

                                def front(f, par):
                                    pool.wait_ge(kf32_ready, f + 1)
                                    pool.wait_ge(kf_high_ready, f + 1)
                                    nc.gpsimd.tensor_tensor(kf_low[:, par, :, :], kf32[:, :, :], kf_high[:, par, :, :],
                                                            ALU.subtract).then_inc(kf_low_ready, 1)
                                    pool.wait_ge(q_high_ready, f + 1)
                                    wait(pool, q_bd_ready, 2 * f)
                                    nc.gpsimd.tensor_tensor(q_low[:, :, :], q32[:, :, :], q_high[:, :, :], ALU.subtract)\
                                        .then_inc(q_low_ready, 1)
                                    pool.wait_ge(k_lowhigh_ready, f + 1)
                                    nc.gpsimd.tensor_tensor(k_mix[:, :, par, :], k32[:, :, :], k_lowhigh[:, :, :],
                                                            ALU.subtract).then_inc(k_mix_ready, 1)
                                    pool.wait_ge(qf_max_ready, f + 1)
                                    nc.gpsimd.tensor_tensor(qf_tok[:, :, :], qf_tok[:, :, :],
                                                            qf_max[:, :].unsqueeze(2).broadcast_to([P, HEADS, FEAT]),
                                                            ALU.subtract).then_inc(qf_shifted, 1)
                                    pool.wait_ge(qf_high_ready, f + 1)
                                    wait(pool, qf_bd_ready, 2 * f)
                                    nc.gpsimd.tensor_tensor(qf_low[:, :, :], qf32[:, par % 2, :, :], qf_high[:, :, :],
                                                            ALU.subtract).then_inc(qf_low_ready, 1)

                                low_x(0, 0)
                                pool.wait_ge(cleared_dve, 1)
                                front(0, 0)

                                def output_bias(n):
                                    x_row = x_tok[:, ds(n, 1), :].rearrange("p a c -> p (a c)")
                                    nc.gpsimd.tensor_tensor(x_row, x_row, b_o[:, :], ALU.add).then_inc(x_biased, 1)

                                def one_block(n, par):
                                    low_x(n + 1, (par + 1) % RING)
                                    output_bias(n)
                                    front(n + 1, (par + 1) % RING)

                                scheduled(pool, one_block)

                            @block.sync
                            def _(sp):
                                def one_block(n, par):
                                    sp.wait_ge(max_rows_ready, n + 1)
                                    sp.dma_start(stair_own_r[0:1, :, :], max_rows[0:HEADS, :]).then_inc(max_placed, 16)
                                    sp.dma_start(stair_prev_r[P - 1:P, :, :], max_rows[HEADS:, :]).then_inc(max_placed, 16)

                                scheduled(sp, one_block)

                            @block.tensor
                            def _(pe):
                                def queries_keys(f, par):
                                    pe.wait_ge(x_ready, f + 1)
                                    wait(pe, qs_max, GROUPS * (f - 1) + 1)
                                    dst = pair(3)
                                    for which, w in ((0, wq_s), (1, wk_s)):
                                        for g in range(GROUPS):
                                            for k in range(HALVES):
                                                for i, (part, x_part) in enumerate(PASSES):
                                                    m = nc.tensor.matmul(dst[:, which, g * P:(g + 1) * P],
                                                                         w[part][:, k, g * P:(g + 1) * P],
                                                                         x_part[:, par % 2, k, :],
                                                                         start=(k == 0 and i == 0),
                                                                         stop=(k == HALVES - 1 and i == 2))
                                    m.then_inc(qk_product, 1)

                                def values(f, par):
                                    wait(pe, f_ready, 2 * GROUPS * (f - 1) + 2)
                                    dst = pair(8)
                                    for k in range(HALVES):
                                        for i, (part, x_part) in enumerate(PASSES):
                                            ends = dict(start=(k == 0 and i == 0), stop=(k == HALVES - 1 and i == 2))
                                            nc.tensor.matmul(dst[:, 0, :], x_part[:, par % 2, k, :], w_vq[part][:, k, :],
                                                             **ends)
                                            m = nc.tensor.matmul(dst[:, 1, 0:HEADS * FEAT], x_part[:, par % 2, k, :],
                                                                 w_qf[part][:, k, :], **ends)
                                    m.then_inc(vq_product, 1)

                                def turn_features(f):
                                    pe.wait_ge(qf_pad_ready, f + 1)
                                    pe.wait_ge(kf32_ready, f + 1)
                                    wait(pe, max_rows_ready, f)
                                    wait(pe, inc_ready, f)
                                    dst = pair(13)
                                    for g in range(GROUPS):
                                        nc.tensor.transpose(dst[:, 0, g * P:(g + 1) * P],
                                                            flat(qf_pad[:, g * PER_G:(g + 1) * PER_G, :]), ident[:, :])
                                    for g in range(GROUPS):
                                        m = nc.tensor.transpose(dst[:, 1, g * P:(g + 1) * P], kf32[:, g, :], ident[:, :])
                                    m.then_inc(turned, 1)

                                def query_scores(n, par, g):
                                    item = g if g < 3 else 4
                                    if g == 0:
                                        pe.wait_ge(q_bd_ready, 2 * n + 2)
                                        pe.wait_ge(k_mix_ready, n + 1)
                                        if isinstance(n, int) and n == 0:
                                            pe.wait_ge(qf_ready, 1)
                                        wait(pe, p_ready, GROUPS * (n - 1) + 2)
                                    if g == 1:
                                        if isinstance(n, int) and n == 0:
                                            pe.wait_ge(kf_tok_ready, 1)
                                        wait(pe, p_ready, GROUPS * (n - 1) + 3)
                                    if g == 2:
                                        wait(pe, p_ready, GROUPS * n)
                                    if g == 3:
                                        pe.wait_ge(qs_max, GROUPS * n + 2)
                                    dst = pair(item)
                                    order, keys = key_pair(par)
                                    for bank in range(2):
                                        nc.tensor.matmul(dst[:, bank, :], ident16[:, :],
                                                         mask_q[:, order, :, :].rearrange("p s k -> p (s k)").unsqueeze(1)
                                                         .broadcast_to([P, 2, 2 * P]),
                                                         start=True, stop=False)
                                        for h in range(2):
                                            m = nc.tensor.matmul(dst[:, bank, h * 2 * P:(h + 1) * 2 * P],
                                                                 q_bd[:, 0, par % 2, g, 2 * bank + h, :],
                                                                 k_mix[:, g, keys, :], start=False, stop=(h == 1))
                                    m.then_inc(qs_product, 1)

                                def maxima_state(n, par):
                                    pe.wait_ge(f_ready, 2 * GROUPS * n + 4)
                                    pe.wait_ge(penal_ready, n + 1)
                                    dst = pair(10)
                                    nc.tensor.transpose(dst[:, 1, :].bitcast(BF16)[0:2 * HEADS, 0:P],
                                                        neg_max[:, :, :].rearrange("p a h -> p (a h)"), ident16[:, :])\
                                        .then_inc(max_turned, 1)
                                    if isinstance(n, int) and n == 0:
                                        pe.wait_ge(cleared, 3)
                                    before = (par - 1) % RING
                                    for g in range(GROUPS):
                                        m = nc.tensor.matmul(dst[:, 0, g * P:(g + 1) * P],
                                                             kf_tok[:, before % 2, g * P:(g + 1) * P],
                                                             flat(v_ext[:, before, g * PER_G:(g + 1) * PER_G, :]),
                                                             start=True, stop=True)
                                    m.then_inc(inc_product, 1)

                                def feature_scores(n, par, g):
                                    item = FEATURE_ITEMS[g]
                                    if g == 0:
                                        pe.wait_ge(qf_bd_ready, 2 * n + 2)
                                        pe.wait_ge(kf_low_ready, n + 1)
                                        pe.wait_ge(qs_max, GROUPS * n + 3)
                                    if g == 1:
                                        pe.wait_ge(qs_max, GROUPS * (n + 1))
                                    if g == 2:
                                        wait(pe, ctx_ready, n)
                                        if isinstance(n, int) and n == 0:
                                            pe.wait_ge(k32_ready, 2)
                                    if g == 3:
                                        pe.wait_ge(f_ready, 2 * GROUPS * n + 6)
                                    dst = pair(item)
                                    for side in range(2):
                                        at = (par - side) % RING
                                        parts = ((kf_high, 0), (kf_high, 1), (kf_low, 0))
                                        for i, (kf, part) in enumerate(parts):
                                            m = nc.tensor.matmul(dst[:, side, :], kf[:, at, g, :],
                                                                 flat(qf_bd[:, part, 0, g, :, :]),
                                                                 start=(i == 0), stop=(i == 2))
                                        m.then_inc(f_product, 1)

                                def state_part(n, par):
                                    wait(pe, sums_ready, 2 * n)
                                    wait(pe, state_ready, n)
                                    if isinstance(n, int) and n == 0:
                                        pe.wait_ge(cleared, 3)
                                    for g in range(GROUPS):
                                        m = nc.tensor.matmul(ps_global[:, g * P:(g + 1) * P], state[:, g, :],
                                                             qf32[:, par % 2, g, :], start=(g == 0), stop=False,
                                                             skip_group_check=True)
                                    m.then_inc(state_read, 1)

                                def weighted(n, par, g, bank, weights, ready, done, unit, first):
                                    pe.wait_ge(ready, unit * (GROUPS * n + g + 1))
                                    if g == 0:
                                        pe.wait_ge(v_ready, n + 1)
                                    for side in range(2):
                                        at = (par - side) % RING
                                        for h in range(PER_G):
                                            m = nc.tensor.matmul(bank[h * STRIP:(h + 1) * STRIP, g * P:(g + 1) * P],
                                                                 v_ext[:, at, g * PER_G + h, :], weights[:, g % 2, side, h, :],
                                                                 start=(first and side == 0), stop=(side == 1),
                                                                 skip_group_check=True)
                                    m.then_inc(done, 1)

                                def weighted_features(n, par, g):
                                    weighted(n, par, g, ps_global, feats, f_ready, global_done, 2, False)

                                def weighted_probs(n, par, g):
                                    weighted(n, par, g, ps_local, probs, p_ready, local_done, 1, True)

                                def key_scores(n, par, g):
                                    item = 14 + g
                                    if g == 0:
                                        pe.wait_ge(max_placed, 32 * (n + 1))
                                        wait(pe, y_ready, n)
                                        if isinstance(n, int) and n == 0:
                                            pe.wait_ge(qf_ready, 2)
                                    if g == 1:
                                        pe.wait_ge(f_ready, 2 * GROUPS * (n + 1))
                                    if g == 2:
                                        pe.wait_ge(kf_tok_ready, n + 2)
                                    if g == 3:
                                        pe.wait_ge(p_ready, GROUPS * n + 1)
                                    dst = pair(item)
                                    for side, (left, right) in enumerate(((stair_own_l, stair_own_r),
                                                                          (stair_prev_l, stair_prev_r))):
                                        at = (par - side) % RING
                                        nc.tensor.matmul(dst[:, side, :], left[:, :], flat(right[:, g * PER_G:(g + 1) * PER_G, :]),
                                                         start=True, stop=False)
                                        for part in range(2):
                                            m = nc.tensor.matmul(dst[:, side, :], k_mix[:, g, at, :],
                                                                 flat(q_bd[:, part, par % 2, g, :, :]), start=False,
                                                                 stop=(part == 1))
                                    m.then_inc(ks_product, 1)

                                def turn_sums(n):
                                    pe.wait_ge(sums_ready, 2 * n + 2)
                                    pe.wait_ge(k32_ready, n + 3)
                                    dst = pair(6)
                                    for which in range(2):
                                        for g in range(GROUPS):
                                            m = nc.tensor.transpose(dst[:, which, g * P:(g + 1) * P],
                                                                    sums[:, which, g * P:(g + 1) * P], ident[:, :])
                                    m.then_inc(sums_turned, 1)

                                def turn_context(n, last=False):
                                    pe.wait_ge(ctx_ready, n + 1)
                                    if not last:
                                        pe.wait_ge(qf_ready, n + 3)
                                    dst = pair(11)
                                    for k in range(HALVES):
                                        m = nc.tensor.transpose(dst[:, 0, k * P:(k + 1) * P], ctx[:, k * P:(k + 1) * P],
                                                                ident[:, :])
                                    m.then_inc(ctx_turned, 1)

                                def output_product(n):
                                    pe.wait_ge(ctx_ch_ready, n + 1)
                                    dst = pair(11)
                                    for k in range(HALVES):
                                        m = nc.tensor.matmul(dst[:, 1, 0:DM], ctx_ch[:, k, :], w_o[:, k, :],
                                                             start=(k == 0), stop=(k == HALVES - 1))
                                    m.then_inc(y_product, 1)

                                queries_keys(0, 0)
                                values(0, 0)
                                turn_features(0)

                                def one_block(n, par):
                                    tail = not (isinstance(n, int) and n == 0)
                                    nxt = (par + 1) % RING
                                    query_scores(n, par, 0)
                                    query_scores(n, par, 1)
                                    query_scores(n, par, 2)
                                    queries_keys(n + 1, nxt)
                                    state_part(n, par)
                                    query_scores(n, par, 3)
                                    feature_scores(n, par, 0)
                                    if tail:
                                        turn_sums(n - 1)
                                    feature_scores(n, par, 1)
                                    values(n + 1, nxt)
                                    weighted_features(n, par, 0)
                                    feature_scores(n, par, 2)
                                    maxima_state(n, par)
                                    weighted_features(n, par, 1)
                                    if tail:
                                        turn_context(n - 1)
                                    feature_scores(n, par, 3)
                                    if tail:
                                        output_product(n - 1)
                                    weighted_features(n, par, 2)
                                    turn_features(n + 1)
                                    key_scores(n, par, 0)
                                    key_scores(n, par, 1)
                                    weighted_probs(n, par, 0)
                                    key_scores(n, par, 2)
                                    weighted_probs(n, par, 1)
                                    key_scores(n, par, 3)
                                    weighted_features(n, par, 3)
                                    weighted_probs(n, par, 2)
                                    weighted_probs(n, par, 3)

                                scheduled(pe, one_block)
                                pe.wait_ge(p_ready, GROUPS * NBLK)
                                pe.wait_ge(sums_ready, 2 * NBLK)
                                dst = pair(6)
                                for which in range(2):
                                    for g in range(GROUPS):
                                        m = nc.tensor.transpose(dst[:, which, g * P:(g + 1) * P],
                                                                sums[:, which, g * P:(g + 1) * P], ident[:, :])
                                m.then_inc(sums_turned, 1)
                                turn_context(NBLK - 1, last=True)
                                output_product(NBLK - 1)

                            @block.scalar
                            def _(act):
                                def high_x(f, par):
                                    wait(act, vq_product, f - 1)
                                    nc.scalar.activation(x_high[:, par % 2, :, :], xn_ch[:, :, ds(f * P, P)], ACT.Copy)\
                                        .then_inc(x_high_ready, 1)

                                def load_logs(f):
                                    wait(act, kf32_ready, f)
                                    act.dma_start(log_blk[:, :, :],
                                                  log_k[ds(f, 1), :, :, :].rearrange("a p g q -> (a p) g q"))\
                                        .then_inc(log_loaded, 16)

                                def key_exponentials(f):
                                    act.wait_ge(log_loaded, 16 * (f + 1))
                                    for g in range(GROUPS):
                                        a = nc.scalar.activation(log_blk[:, g, :], log_blk[:, g, :], ACT.Exp,
                                                                 bias=neg_kmax[:, ds(f, 1), g:g + 1].rearrange("p a b -> p (a b)"))
                                    a.then_inc(kf_exp_ready, 1)
                                    act.wait_ge(kf_exp_ready, f + 1)
                                    if isinstance(f, int) and f == 0:
                                        act.wait_ge(cleared, 1)
                                    wait(act, kf_low_ready, f)
                                    wait(act, turned, f)
                                    nc.scalar.activation(kf32[:, :, :], log_blk[:, :, :], ACT.Identity,
                                                         bias=scaled_eps[:, 0:1], scale=FSCALE).then_inc(kf32_ready, 1)

                                def splits(f, par):
                                    act.wait_ge(q32_ready, f + 1)
                                    wait(act, q_bd_ready, 2 * f)
                                    wait(act, q_low_ready, f)
                                    nc.scalar.activation(q_high[:, :, :], q32[:, :, :], ACT.Copy).then_inc(q_high_ready, 1)
                                    act.wait_ge(k32_ready, f + 1)
                                    wait(act, k_mix_ready, f)
                                    nc.scalar.activation(k_lowhigh[:, :, :], k32[:, :, :], ACT.Copy, scale=low_rows[:, 0:1])\
                                        .then_inc(k_lowhigh_ready, 1)
                                    act.wait_ge(kf32_ready, f + 1)
                                    wait(act, f_product, 2 * GROUPS * (f - 2))
                                    nc.scalar.activation(kf_high[:, par, :, :], kf32[:, :, :], ACT.Copy)\
                                        .then_inc(kf_high_ready, 1)

                                def query_squares(f):
                                    act.wait_ge(q_tok_ready, f + 1)
                                    nc.scalar.activation(q_tok[:, :], q_tok[:, :], ACT.Square).then_inc(q_sq_ready, 1)

                                def feature_exponentials(f):
                                    act.wait_ge(qf_shifted, f + 1)
                                    nc.scalar.activation(qf_tok[:, :, :], qf_tok[:, :, :], ACT.Exp).then_inc(qf_exp_ready, 1)

                                def turned_features(f, par):
                                    act.wait_ge(turned, f + 1)
                                    wait(act, state_read, f - 1)
                                    dst = pair(13)
                                    nc.scalar.activation(flat(qf32[:, par % 2, :, :]), dst[:, 0, :], ACT.Copy)\
                                        .then_inc(qf32_ready, 1)
                                    nc.scalar.activation(kf_tok[:, par % 2, :], dst[:, 1, :], ACT.Copy).then_inc(kf_tok_ready, 1)
                                    act.wait_ge(qf32_ready, f + 1)
                                    wait(act, qf_bd_ready, 2 * f)
                                    wait(act, qf_low_ready, f)
                                    nc.scalar.activation(qf_high[:, :, :], qf32[:, par % 2, :, :], ACT.Copy)\
                                        .then_inc(qf_high_ready, 1)

                                def context_turned(n):
                                    act.wait_ge(ctx_turned, n + 1)
                                    wait(act, y_product, n)
                                    nc.scalar.activation(flat(ctx_ch[:, :, :]), pair(11)[:, 0, 0:DM], ACT.Copy)\
                                        .then_inc(ctx_ch_ready, 1)

                                high_x(0, 0)
                                load_logs(0)
                                key_exponentials(0)
                                act.wait_ge(cleared, 3)
                                act.wait_ge(cleared_dve, 1)
                                splits(0, 0)
                                query_squares(0)
                                feature_exponentials(0)
                                load_logs(1)
                                turned_features(0, 0)

                                def one_block(n, par):
                                    tail = not (isinstance(n, int) and n == 0)
                                    nxt = (par + 1) % RING
                                    high_x(n + 1, nxt)
                                    key_exponentials(n + 1)
                                    splits(n + 1, nxt)
                                    load_logs(n + 2)
                                    act.wait_ge(lift_arg_ready, n + 1)
                                    nc.scalar.activation(lift_exp[:, par % 2, :], lift_arg[:, :], ACT.Exp)\
                                        .then_inc(lift_exp_ready, 1)
                                    query_squares(n + 1)
                                    act.wait_ge(max_turned, n + 1)
                                    wait(act, max_placed, 32 * n)
                                    nc.scalar.activation(max_rows[:, :], pair(10)[:, 1, :].bitcast(BF16)[0:2 * HEADS, 0:P],
                                                         ACT.Copy).then_inc(max_rows_ready, 1)
                                    if tail:
                                        context_turned(n - 1)
                                    feature_exponentials(n + 1)
                                    turned_features(n + 1, nxt)
                                    for g in range(GROUPS):
                                        act.wait_ge(ks_product, GROUPS * n + g + 1)
                                        wait(act, local_done, GROUPS * n + g - 1)
                                        nc.scalar.activation(probs[:, g % 2, :, :, :].rearrange("p s h q -> p (s h q)"),
                                                             pair(14 + g)[:, :, :].rearrange("p s c -> p (s c)"), ACT.Exp)\
                                            .then_inc(p_ready, 1)
                                    wait(act, sums_turned, n)
                                    act.wait_ge(global_done, GROUPS * (n + 1))
                                    nc.scalar.activation(sums[:, 1, :], ps_global[:, :], ACT.Copy).then_inc(sums_ready, 1)
                                    act.wait_ge(local_done, GROUPS * (n + 1))
                                    nc.scalar.activation(sums[:, 0, :], ps_local[:, :], ACT.Copy).then_inc(sums_ready, 1)

                                scheduled(act, one_block)
                                context_turned(NBLK - 1)
                                act.wait_ge(log_loaded, 16 * (NBLK + 2))

                            @block.vector
                            def _(dve):
                                def queries_keys(f):
                                    src = pair(3)
                                    dve.wait_ge(qk_product, f + 1)
                                    wait(dve, q_low_ready, f)
                                    wait(dve, k_mix_ready, f)
                                    for which, bias, dst, ready in ((0, bq_s, q32, q32_ready), (1, bk_s, k32, k32_ready)):
                                        nc.vector.scalar_tensor_tensor(
                                            dst[:, :, :], src[:, which, :].rearrange("p (g q) -> p g q", q=P), 1.0 / WSCALE,
                                            bias[:, :].unsqueeze(2).broadcast_to([P, GROUPS, P]), ALU.mult, ALU.add)\
                                            .then_inc(ready, 1)

                                def values(f, par):
                                    src = pair(8)
                                    dve.wait_ge(vq_product, f + 1)
                                    wait(dve, local_done, GROUPS * (f - 2))
                                    nc.vector.scalar_tensor_tensor(v_ext[:, par, :, 0:DH],
                                                                   src[:, 0, 0:DM].rearrange("p (h d) -> p h d", d=DH), 1.0 / WSCALE,
                                                                   b_vq[:, 0:DM].rearrange("p (h d) -> p h d", d=DH),
                                                                   ALU.mult, ALU.add)\
                                        .then_inc(v_ready, 1)
                                    wait(dve, q_norm_ready, f)
                                    nc.vector.scalar_tensor_tensor(q_tok[:, :], src[:, 0, DM:], 1.0 / WSCALE, b_vq[:, DM:],
                                                                   ALU.mult, ALU.add)\
                                        .then_inc(q_tok_ready, 1)
                                    wait(dve, qf_pad_ready, f)
                                    nc.vector.scalar_tensor_tensor(
                                        qf_tok[:, :, :], src[:, 1, 0:HEADS * FEAT].rearrange("p (h m) -> p h m", m=FEAT),
                                        1.0 / WSCALE, b_qf[:, :].rearrange("p (h m) -> p h m", m=FEAT), ALU.mult, ALU.add)\
                                        .then_inc(qf_ready, 1)

                                def feature_maxima(f, par):
                                    dve.wait_ge(qf_ready, f + 1)
                                    nc.vector.tensor_reduce(qf_max[:, :], qf_tok[:, :, :], AX_X, ALU.max).then_inc(qf_max_ready, 1)
                                    dve.wait_ge(q_sq_ready, f + 1)
                                    nc.vector.tensor_reduce(q_norm[:, :], q_tok[:, :].rearrange("p (h d) -> p h d", d=DH), AX_X,
                                                            ALU.add).then_inc(q_norm_ready, 1)
                                    dve.wait_ge(q_norm_ready, f + 1)
                                    dve.wait_ge(qf_max_ready, f + 1)
                                    nc.vector.scalar_tensor_tensor(q_scale[:, :], q_norm[:, :], -SCALE / 2, qf_max[:, :],
                                                                   ALU.mult, ALU.add).then_inc(q_scale_ready, 1)
                                    dve.wait_ge(q_scale_ready, f + 1)
                                    nc.vector.tensor_tensor(g_scale[:, par % 2, :], q_scale[:, :],
                                                            kmax_tok[:, ds(f, 1), :].rearrange("p a h -> p (a h)"), ALU.add)\
                                        .then_inc(g_scale_ready, 1)

                                def place(f, slot, bd, high, low, high_ready, low_ready, placed):
                                    for part, src, ready in ((0, high, high_ready), (1, low, low_ready)):
                                        dve.wait_ge(ready, f + 1)
                                        for r in range(PER_G):
                                            rows = slice(r * STRIP, (r + 1) * STRIP)
                                            c = nc.vector.tensor_copy(bd[rows, part, slot, :, r, :], src[rows, :, :])
                                        c.then_inc(placed, 1)

                                def place_queries(f, par):
                                    wait(dve, ks_product, GROUPS * (f - 1))
                                    place(f, par % 2, q_bd, q_high, q_low, q_high_ready, q_low_ready, q_bd_ready)

                                def place_features(f, par):
                                    wait(dve, f_product, 2 * GROUPS * f)
                                    place(f, 0, qf_bd, qf_high, qf_low, qf_high_ready, qf_low_ready, qf_bd_ready)

                                def pad_features(f):
                                    dve.wait_ge(qf_exp_ready, f + 1)
                                    wait(dve, turned, f)
                                    nc.vector.tensor_scalar(qf_pad[:, :, 0:FEAT], qf_tok[:, :, :], FEATURE_EPS, FSCALE,
                                                            ALU.add, ALU.mult).then_inc(qf_pad_ready, 1)

                                def maximum(n, par, g):
                                    dve.wait_ge(qs_product, GROUPS * n + g + 1)
                                    if g == 0:
                                        wait(dve, row_top_ready, n)
                                    nc.vector.tensor_reduce(
                                        block_max[:, g, :, :],
                                        pair(g if g < 3 else 4)[:, :, :].rearrange("p b (h s k) -> p (b h s) k", h=2, s=2),
                                        AX_X, ALU.max).then_inc(qs_max, 1)

                                def maxima(n, par):
                                    order, _ = key_pair(par)
                                    own, prev = 1 - order, order
                                    bm = block_max[:, :, :, :].rearrange("p g h s -> p (g h) s")
                                    dve.wait_ge(qs_max, GROUPS * (n + 1))
                                    nc.vector.scalar_tensor_tensor(row_top[:, :], bm[:, :, prev], penalty[:, ds(n, 1)],
                                                                   bm[:, :, own], ALU.add, ALU.max).then_inc(row_top_ready, 1)
                                    dve.wait_ge(row_top_ready, n + 1)
                                    wait(dve, max_turned, n)
                                    wait(dve, lift_arg_ready, n)
                                    nc.vector.tensor_scalar(neg_max[:, 0, :], row_top[:, :], -1.0, None, ALU.mult)\
                                        .then_inc(neg_max_ready, 1)
                                    dve.wait_ge(neg_max_ready, n + 1)
                                    nc.vector.tensor_scalar(neg_max[:, 1, :], neg_max[:, 0, :], penalty[:, ds(n, 1)], None,
                                                            ALU.add).then_inc(penal_ready, 1)
                                    dve.wait_ge(g_scale_ready, n + 1)
                                    wait(dve, lift_exp_ready, n)
                                    nc.vector.scalar_tensor_tensor(lift_arg[:, :], neg_max[:, 0, :], -1.0,
                                                                   g_scale[:, par % 2, :], ALU.mult, ALU.subtract)\
                                        .then_inc(lift_arg_ready, 1)

                                def masked_features(n, par, g):
                                    src = pair(FEATURE_ITEMS[g])
                                    for side in range(2):
                                        dve.wait_ge(f_product, 2 * (GROUPS * n + g) + side + 1)
                                        wait(dve, global_done, GROUPS * n + g - 1)
                                        s = src[:, side, :].rearrange("p (h q) -> p h q", q=P)
                                        mask = gmask[:, side:side + 1, :].broadcast_to([P, PER_G, P])
                                        if side == 0:
                                            m = nc.vector.tensor_tensor(feats[:, g % 2, side, :, :], s, mask, ALU.mult)
                                        else:
                                            m = nc.vector.scalar_tensor_tensor(feats[:, g % 2, side, :, :], s,
                                                                               has_prev[:, ds(n, 1)], mask, ALU.mult, ALU.mult)
                                        m.then_inc(f_ready, 1)

                                def new_state(n):
                                    src = pair(10)[:, 0, :]
                                    dve.wait_ge(inc_product, n + 1)
                                    nc.vector.scalar_tensor_tensor(
                                        state_inc[:, :, :], src.rearrange("p (g c) -> p g c", c=P), keep_state[:, ds(n, 1)],
                                        flat(diag_strips[:, :, :]).unsqueeze(1).broadcast_to([P, GROUPS, P]),
                                        ALU.mult, ALU.mult).then_inc(inc_ready, 1)
                                    dve.wait_ge(inc_ready, n + 1)
                                    dve.wait_ge(state_read, n + 1)
                                    nc.vector.scalar_tensor_tensor(state[:, :, :], state[:, :, :], keep_state[:, ds(n, 1)],
                                                                   state_inc[:, :, :], ALU.mult, ALU.add)\
                                        .then_inc(state_ready, 1)

                                def normalise(n, par):
                                    src = pair(6)
                                    local = src[:, 0, :].rearrange("p (h d) -> p h d", d=STRIP)
                                    whole = src[:, 1, :].rearrange("p (h d) -> p h d", d=STRIP)
                                    dve.wait_ge(sums_turned, n + 1)
                                    dve.wait_ge(lift_exp_ready, n + 1)
                                    nc.vector.tensor_tensor(norm_a[:, :], lift_exp[:, par % 2, :], local[:, :, DH], ALU.mult)\
                                        .then_inc(norm_parts, 1)
                                    nc.vector.tensor_scalar(norm_b[:, :], whole[:, :, DH], UNSCALE, 1e-24, ALU.mult, ALU.max)\
                                        .then_inc(norm_parts, 1)
                                    nc.vector.reciprocal(r_local[:, :], local[:, :, DH]).then_inc(r_ready, 1)
                                    dve.wait_ge(norm_parts, 2 * n + 2)
                                    nc.vector.tensor_tensor(norm_c[:, :], norm_a[:, :], norm_b[:, :], ALU.add).then_inc(norm_ready, 1)
                                    dve.wait_ge(r_ready, 2 * n + 1)
                                    nc.vector.tensor_tensor(ctx_a[:, :, :], local[:, :, 0:DH],
                                                            r_local[:, :].unsqueeze(2).broadcast_to([P, HEADS, DH]), ALU.mult)\
                                        .then_inc(ctx_parts, 1)
                                    dve.wait_ge(norm_ready, 2 * n + 1)
                                    nc.vector.reciprocal(norm_r[:, :], norm_c[:, :]).then_inc(norm_ready, 1)
                                    dve.wait_ge(norm_ready, 2 * n + 2)
                                    nc.vector.tensor_scalar(r_global[:, :], norm_r[:, :], UNSCALE, None, ALU.mult)\
                                        .then_inc(r_ready, 1)
                                    dve.wait_ge(r_ready, 2 * n + 2)
                                    wait(dve, ctx_turned, n)
                                    nc.vector.tensor_tensor(ctx[:, :].rearrange("p (h d) -> p h d", d=DH), whole[:, :, 0:DH],
                                                            r_global[:, :].unsqueeze(2).broadcast_to([P, HEADS, DH]), ALU.mult)\
                                        .then_inc(ctx_parts, 1)
                                    dve.wait_ge(ctx_parts, 2 * n + 2)
                                    wait(dve, ctx_turned, n)
                                    nc.vector.tensor_tensor(ctx[:, :], flat(ctx_a[:, :, :]), ctx[:, :], ALU.add)\
                                        .then_inc(ctx_ready, 1)

                                def add_output(n):
                                    dve.wait_ge(y_product, n + 1)
                                    dve.wait_ge(x_biased, n + 1)
                                    x_row = x_tok[:, ds(n, 1), :].rearrange("p a c -> p (a c)")
                                    nc.vector.tensor_tensor(x_row, pair(11)[:, 1, 0:DM], x_row, ALU.add)\
                                        .then_inc(y_ready, 1)

                                for buf in (q_bd, qf_bd, k_mix, kf_high, kf_low):
                                    last = nc.vector.memset(buf[tuple([slice(None)] * len(buf.shape))], 0.0)
                                last.then_inc(cleared_dve, 1)
                                dve.wait_ge(cleared_dve, 1)
                                dve.wait_ge(cleared, 3)
                                queries_keys(0)
                                values(0, 0)
                                feature_maxima(0, 0)
                                place_queries(0, 0)
                                pad_features(0)
                                place_features(0, 0)

                                def one_block(n, par):
                                    tail = not (isinstance(n, int) and n == 0)
                                    nxt = (par + 1) % RING
                                    for g in range(3):
                                        maximum(n, par, g)
                                    queries_keys(n + 1)
                                    maximum(n, par, 3)
                                    maxima(n, par)
                                    masked_features(n, par, 0)
                                    if tail:
                                        normalise(n - 1, (par - 1) % RING)
                                    masked_features(n, par, 1)
                                    values(n + 1, nxt)
                                    masked_features(n, par, 2)
                                    feature_maxima(n + 1, nxt)
                                    new_state(n)
                                    pad_features(n + 1)
                                    masked_features(n, par, 3)
                                    if tail:
                                        add_output(n - 1)
                                    place_queries(n + 1, nxt)
                                    place_features(n + 1, nxt)

                                scheduled(dve, one_block)
                                normalise(NBLK - 1, (NBLK - 1) % RING)
                                add_output(NBLK - 1)

                def key_pair(par):
                    return (0, slice(par - 1, par + 1)) if par else (1, slice(0, 4, 3))

                with ExitStack() as prep:
                    proj_bd = sb("proj_bd", [P, HALF_HEADS, FEAT], F32, prep)
                    w_k = sb("w_k", [P, HALVES, DM], F32, prep)
                    bk_col = sb("bk_col", [P, HALVES], F32, prep)
                    attention_weights(prep)
                    key_features(prep)
                attention_blocks(scope)

        layernorm("ln1", True, twist_sign)
        ffn("ffn1", False)
        layernorm("ln2", False, ones_col)
        attention()
        layernorm("ln3", False, twist_sign)
        ffn("ffn2", True)


_INS = ["L0_attn_x", "L0_attn_Wqkv_w", "L0_attn_Wqkv_b", "L0_attn_proj", "L0_attn_out_w", "L0_attn_out_b",
        "L0_ffn_cn_w1", "L0_ffn_cn_b1", "L0_ffn_cn_w2", "L0_ffn_cn_b2", "L0_ffn_cn_w3", "L0_ffn_cn_b3",
        "L0_ffn_cn_w4", "L0_ffn_cn_b4", "L0_ffn_gc_w1", "L0_ffn_gc_b1", "L0_ffn_gc_w2", "L0_ffn_gc_b2",
        "L0_ffn_gc_w3", "L0_ffn_gc_b3", "L0_ffn_adaptive_range"]


def kernel(**inputs):
    import numpy as _np
    import concourse.bacc as _bacc
    from concourse.bass_utils import run_bass_kernel_spmd as _run

    nc = _bacc.Bacc("TRN2", target_bir_lowering=False, num_devices=1)
    arrays, args = {}, []
    for name in _INS:
        a = _np.ascontiguousarray(inputs[name])
        arrays[name + "_dram"] = a
        args.append(nc.dram_tensor(name + "_dram", a.shape, mybir.dt.from_np(a.dtype),
                                   kind="ExternalInput").ap())
    x = inputs["L0_attn_x"]
    out = nc.dram_tensor("out_dram", tuple(x.shape), F32, kind="ExternalOutput").ap()
    macaron_kernel(nc, *args, out)
    r = _run(nc, [arrays], core_ids=[0])
    return r.results[0]["out_dram"]
```

```python
from contextlib import ExitStack
from math import sqrt

import concourse.bass as bass
from concourse import mybir

ds = bass.ds
ALU = mybir.AluOpType
ACT = mybir.ActivationFunctionType
F32 = mybir.dt.float32
F16 = mybir.dt.float16
BF16 = mybir.dt.bfloat16
AX_X = mybir.AxisListType.X

P = 128
LN_EPS = 1e-5
FEATURE_EPS = 1e-4
MASKED = -30000.0


def macaron_kernel(nc, x_in, wqkv, bqkv, proj, wout, bout, cn_w1, cn_b1, cn_w2, cn_b2, cn_w3, cn_b3,
                   cn_w4, cn_b4, gc_w1, gc_b1, gc_w2, gc_b2, gc_w3, gc_b3, adaptive_range, out):
    BATCH, SEQ, DM = x_in.shape
    NBLK = BATCH * SEQ // P
    BLK_B = SEQ // P
    HALVES = DM // P
    TILE = 512
    TILES_B = SEQ // TILE
    BLK_T = TILE // P
    CYCLES = 3
    D1, D2, D3 = cn_w1.shape[1], cn_w2.shape[1], cn_w3.shape[1]
    MCH = D1 // P
    assert HALVES == 2 and DM == 256 and D2 == P and D3 == 64 and SEQ % TILE == 0

    x_blocks = x_in.rearrange("b (n p) c -> p (b n) c", p=P)
    out_blocks = out.rearrange("b (n p) c -> p (b n) c", p=P)

    with ExitStack() as keep:
        def sb(name, shape, dt, scope=keep):
            return scope.enter_context(nc.sbuf_tensor(name, shape, dt))

        def psum(name, shape, scope, dt=F32):
            return scope.enter_context(nc.psum_tensor(name, shape, dt))

        def sem(name, scope):
            return scope.enter_context(nc.semaphore(name))

        x_tok = sb("x_tok", [P, NBLK, DM], F32)
        xn_ch = sb("xn_ch", [P, HALVES, (NBLK + 1) * P], F32)
        ident = sb("ident", [P, P], F32)
        twist_sign = sb("twist_sign", [P, 1], F32)
        ones_col = sb("ones_col", [P, 1], F32)
        eps_col = sb("eps_col", [P, 1], F32)
        block_sums = sb("block_sums", [P, HALVES, NBLK], F32)

        w1 = sb("w1", [P, HALVES, D1], F32)
        w2 = sb("w2", [P, MCH, D2], F32)
        w3 = sb("w3", [P, D3], F32)
        w4 = sb("w4", [D3, 1], F32)
        w4_rep = sb("w4_rep", [D3, P], F32)
        b1 = sb("b1", [P, MCH], F32)
        b2 = sb("b2", [P, 1], F32)
        b3 = sb("b3", [D3, 1], F32)
        b4_half = sb("b4_half", [P, 1], F32)
        g1 = sb("g1", [P, HALVES, P], F32)
        g2 = sb("g2", [P, D3], F32)
        g3 = sb("g3", [D3, 1], F32)
        g3_rep = sb("g3_rep", [D3, P], F32)
        gb1 = sb("gb1", [P, 1], F32)
        gb2 = sb("gb2", [D3, 1], F32)
        gb3_half = sb("gb3_half", [P, 1], F32)
        rng = sb("rng", [P, 1], F32)
        gain = sb("gain", [P, 1], F32)

        G = 4
        STEPS = NBLK // G
        x_loaded = [sem(f"x_loaded{i}", keep) for i in range(STEPS)]
        loaded = sem("loaded", keep)
        with ExitStack() as scope:
            constants = sem("constants", scope)
            col = lambda v: v.rearrange("(p a) -> p a", a=1)
            spread = lambda v, n: v.rearrange("(a p) -> a p", a=1).broadcast_to([n, 1])
            with nc.Block() as block:
                loads = [
                    (w1[:, :, :], cn_w1.rearrange("(k p) n -> p k n", p=P)),
                    (w2[:, :, :], cn_w2.rearrange("(k p) n -> p k n", p=P)),
                    (w3[:, :], cn_w3),
                    (w4[:, :], cn_w4),
                    (b1[:, :], cn_b1.rearrange("(k p) -> p k", p=P)),
                    (b2[:, :], col(cn_b2)),
                    (b3[:, :], col(cn_b3)),
                    (b4_half[:, :], spread(cn_b4, P)),
                    (g1[:, :, :], gc_w1.rearrange("(k p) n -> p k n", p=P)),
                    (g2[:, :], gc_w2),
                    (g3[:, :], gc_w3),
                    (gb1[:, :], col(gc_b1)),
                    (gb2[:, :], col(gc_b2)),
                    (gb3_half[:, :], spread(gc_b3, P)),
                    (rng[:, :], spread(adaptive_range, P)),
                ]

                @block.sync
                def _(sp):
                    for i in range(STEPS):
                        sp.dma_start(x_tok[:, i * G:(i + 1) * G, :],
                                     x_blocks[:, i * G:(i + 1) * G, :]).then_inc(x_loaded[i], 16)

                @block.gpsimd
                def _(pool):
                    nc.gpsimd.memset(ident[:, :], 0.0).then_inc(constants, 1)
                    nc.gpsimd.memset(twist_sign[:, :], 1.0).then_inc(constants, 1)
                    nc.gpsimd.memset(ones_col[:, :], 1.0)
                    nc.gpsimd.memset(eps_col[:, :], LN_EPS)
                    nc.gpsimd.memset(xn_ch[:, :, NBLK * P:], 0.0)
                    pool.wait_ge(constants, 2)
                    nc.gpsimd.affine_select(out=ident[:, :], in_=ident[:, :], compare_op=ALU.not_equal,
                                            fill=1.0, base=0, pattern=[[-1, P]], channel_multiplier=1)
                    nc.gpsimd.affine_select(out=twist_sign[:, :], in_=twist_sign[:, :], compare_op=ALU.is_gt,
                                            fill=-1.0, base=P // 2, pattern=[[0, 1]],
                                            channel_multiplier=-1).then_inc(constants, 1)

        def ffn_weights(dve):
            dve.wait_ge(loaded, 16 * len(loads))
            nc.vector.tensor_scalar(w1[:, 1, :], w1[:, 1, :], twist_sign[:, 0:1], None, ALU.mult)
            nc.vector.tensor_scalar(g1[:, 1, :], g1[:, 1, :], twist_sign[:, 0:1], None, ALU.mult)
            nc.vector.tensor_copy(w4_rep[:, :], w4[:, 0:1].broadcast_to([D3, P]))
            nc.vector.tensor_copy(g3_rep[:, :], g3[:, 0:1].broadcast_to([D3, P]))
            nc.vector.tensor_scalar(b4_half[:, :], b4_half[:, :], 0.5, None, ALU.mult)
            nc.vector.tensor_scalar(gb3_half[:, :], gb3_half[:, :], 0.5, None, ALU.mult)
            nc.vector.tensor_scalar(gain[:, :], rng[:, :], 0.3, None, ALU.mult)

        def layernorm(name, first, scale_half1, beside=None):
            with ExitStack() as scope:
                xn_tok = sb(name + "_xn_tok", [P, 2, G, DM], F32, scope)
                stats = sb(name + "_stats", [P, 2, G, 6], F32, scope)
                moments = sb(name + "_moments", [P, 2, G, 2], F32, scope)
                std = sb(name + "_std", [P, G], F32, scope)
                rstd = sb(name + "_rstd", [P, G], F32, scope)
                turned = [psum(f"{name}_turned{i}", [P, HALVES, 2, P], scope) for i in range(4)]
                stats_done = sem(name + "_stats_done", scope)
                moments_done = sem(name + "_moments_done", scope)
                std_done = sem(name + "_std_done", scope)
                rstd_done = sem(name + "_rstd_done", scope)
                xn_ready = sem(name + "_xn_ready", scope)
                turned_ready = sem(name + "_turned_ready", scope)
                turned_used = sem(name + "_turned_used", scope)
                with nc.Block() as block:
                    if beside:
                        @block.sync
                        def _(sp):
                            for dst, src in loads:
                                sp.dma_start(dst, src, allow_slow_non_contiguous=True).then_inc(loaded, 16)
                            beside["sync"](sp)

                        block.gpsimd(beside["gpsimd"])

                    @block.vector
                    def _(dve):
                        def rows(blk):
                            return x_tok[:, ds(blk, 1), :].rearrange("p a c -> p (a c)")

                        def statistics(par, blk):
                            for j in range(G):
                                s = nc.vector.bn_stats(stats[:, par, j, :], rows(blk + j))
                            s.then_inc(stats_done, 1)

                        def moments_of(par):
                            for j in range(G):
                                s = nc.vector.bn_aggr(moments[:, par, j, :], stats[:, par, j, :])
                            s.then_inc(moments_done, 1)

                        def normalise(i, par, blk, peeled):
                            dve.wait_ge(std_done, i + 1)
                            nc.vector.reciprocal(rstd[:, :], std[:, :]).then_inc(rstd_done, 1)
                            dve.wait_ge(rstd_done, i + 1)
                            if not peeled:
                                dve.wait_ge(turned_ready, (i - 1) * 2)
                            for j in range(G):
                                s = nc.vector.tensor_scalar(xn_tok[:, par, j, :], rows(blk + j), moments[:, par, j, 0:1],
                                                            rstd[:, j:j + 1], ALU.subtract, ALU.mult)
                            s.then_inc(xn_ready, 1)

                        def step(i, par, peeled):
                            if first:
                                dve.wait_ge(x_loaded[i], 16)
                            if not isinstance(i, int) or i >= 2:
                                dve.wait_ge(moments_done, i - 1)
                                dve.wait_ge(xn_ready, i - 1)
                            statistics(par, i * G)
                            dve.wait_ge(stats_done, i + 1)
                            normalise(i - 1, 1 - par, (i - 1) * G, peeled)
                            moments_of(par)

                        if first:
                            dve.wait_ge(x_loaded[0], 16)
                        statistics(0, 0)
                        dve.wait_ge(stats_done, 1)
                        moments_of(0)
                        if first:
                            for i in range(1, STEPS):
                                step(i, i % 2, i < 3)
                        else:
                            step(1, 1, True)
                            step(2, 0, True)
                            step(3, 1, False)
                            with dve.Fori(2, STEPS // 2) as k:
                                for par in range(2):
                                    step(k * 2 + par, par, False)
                        normalise(STEPS - 1, (STEPS - 1) % 2, (STEPS - 1) * G, False)
                        if beside:
                            ffn_weights(dve)
                            beside["vector"](dve)

                    @block.tensor
                    def _(pe):
                        def step(i, par, peeled):
                            pe.wait_ge(xn_ready, i + 1)
                            for pair in range(2):
                                bank = turned[2 * par + pair]
                                if not peeled:
                                    pe.wait_ge(turned_used, 4 * (i - 2) + 2 * pair + 2)
                                for j in range(2):
                                    for h in range(HALVES):
                                        t = nc.tensor.transpose(bank[:, h, j, :],
                                                                xn_tok[:, par, 2 * pair + j, h * P:(h + 1) * P],
                                                                ident[:, :])
                                t.then_inc(turned_ready, 1)

                        step(0, 0, True)
                        step(1, 1, True)
                        with pe.Fori(1, STEPS // 2) as k:
                            for par in range(2):
                                step(k * 2 + par, par, False)
                        if beside:
                            beside["tensor"](pe)

                    @block.scalar
                    def _(act):
                        scales = [ones_col, scale_half1]

                        def deviation(i, par):
                            act.wait_ge(moments_done, i + 1)
                            nc.scalar.activation(std[:, :], moments[:, par, :, 1], ACT.Sqrt,
                                                 bias=eps_col[:, 0:1]).then_inc(std_done, 1)

                        def keep_turned(i, par):
                            for pair in range(2):
                                act.wait_ge(turned_ready, i * 2 + pair + 1)
                                blk = i * G + 2 * pair
                                for h in range(HALVES):
                                    nc.scalar.activation(
                                        xn_ch[:, h, ds(blk * P, 2 * P)],
                                        turned[2 * par + pair][:, h, :, :].rearrange("p j c -> p (j c)"),
                                        ACT.Identity, scale=scales[h][:, 0:1],
                                        accum_out=block_sums[:, h, ds(blk, 1)]).then_inc(turned_used, 1)

                        deviation(0, 0)
                        deviation(1, 1)
                        keep_turned(0, 0)
                        with act.Fori(1, STEPS // 2) as k:
                            for par in range(2):
                                deviation(k * 2 + par, par)
                                keep_turned(k * 2 + par - 1, 1 - par)
                        keep_turned(STEPS - 1, 1)
                        if beside:
                            beside["scalar"](act)

        def ffn(name, last):
            JOBS_B = CYCLES * TILES_B
            JOBS = BATCH * JOBS_B
            TILES = BATCH * TILES_B
            jobs = [(b, c, s) for b in range(BATCH) for c in range(CYCLES) for s in range(TILES_B)]

            units_before = {s: [(s, 0)] for s in range(TILES_B)}
            units_behind = {s: [(s, 1)] for s in range(TILES_B)}
            for b in range(1, BATCH):
                for s in range(TILES_B):
                    units_behind[b * JOBS_B - TILES_B + s] = [(b * TILES_B + s, 0)]
                    units_behind[b * JOBS_B + s] = [(b * TILES_B + s, 1)]
            unit_order = [u for n in range(JOBS) for u in units_before.get(n, []) + units_behind.get(n, [])]

            def kept_count(tile, which):
                return MCH * (unit_order.index((tile, which)) + 1)

            def update_count(j):
                b, c, s = jobs[j]
                return (b * (CYCLES - 1) + c) * TILES_B + s + 1

            with ExitStack() as scope:
                w1_neg = sb(name + "_w1_neg", [P, D1], F32, scope)
                yz = sb(name + "_yz", [P, TILES_B, 2, MCH, TILE], F32, scope)
                y_now = sb(name + "_y_now", [P, 2, MCH, TILE], F32, scope)
                a_part = sb(name + "_a_part", [P, MCH, TILE], F32, scope)
                b_part = sb(name + "_b_part", [P, MCH, TILE], F32, scope)
                coef_a = sb(name + "_coef_a", [P, TILES_B, TILE], F32, scope)
                coef_b = sb(name + "_coef_b", [P, TILES_B, TILE], F32, scope)
                last_a = sb(name + "_last_a", [P, TILE], F32, scope)
                last_b = sb(name + "_last_b", [P, TILE], F32, scope)
                product_a = sb(name + "_product_a", [P, TILE], F32, scope)
                product_b = sb(name + "_product_b", [P, TILE], F32, scope)
                act1 = sb(name + "_act1", [P, MCH, TILE], F32, scope)
                act2 = sb(name + "_act2", [P, TILE], F32, scope)
                act3 = sb(name + "_act3", [D3, TILE], F32, scope)
                gate = sb(name + "_gate", [P, 2, TILE], F32, scope)
                coupling = sb(name + "_coupling", [P, 2, TILE], F32, scope)
                final = sb(name + "_final", [P, HALVES, TILE], F32, scope)
                mean = sb(name + "_mean", [P, HALVES, BATCH], F32, scope)
                gact1 = sb(name + "_gact1", [P, BATCH], F32, scope)
                gact2 = sb(name + "_gact2", [D3, BATCH], F32, scope)
                gtanh = sb(name + "_gtanh", [P, BATCH], F32, scope)
                base = sb(name + "_base", [P, BATCH], F32, scope)
                ps1 = psum(name + "_ps1", [P, MCH, TILE], scope)
                ps2 = psum(name + "_ps2", [P, TILE], scope)
                ps3 = psum(name + "_ps3", [P, TILE], scope)
                ps4 = psum(name + "_ps4", [P, TILE], scope)
                ps_out = psum(name + "_ps_out", [P, 2, 2, DM], scope)

                g_prod = sem(name + "_g_prod", scope)
                g_act = sem(name + "_g_act", scope)
                unit_done = sem(name + "_unit_done", scope)
                unit_kept = sem(name + "_unit_kept", scope)
                l2_done = sem(name + "_l2_done", scope)
                l3_done = sem(name + "_l3_done", scope)
                l4_done = sem(name + "_l4_done", scope)
                gelu1_done = sem(name + "_gelu1_done", scope)
                gelu2_done = sem(name + "_gelu2_done", scope)
                gelu3_done = sem(name + "_gelu3_done", scope)
                gate_done = sem(name + "_gate_done", scope)
                coupling_done = sem(name + "_coupling_done", scope)
                inner = sem(name + "_inner", scope)
                y_done = sem(name + "_y_done", scope)
                b_steps = sem(name + "_b_steps", scope)
                final_done = sem(name + "_final_done", scope)
                final_turned = sem(name + "_final_turned", scope)
                residual_done = sem(name + "_residual_done", scope)
                stored = sem(name + "_stored", scope) if last else None

                def state(h, tile):
                    return xn_ch[:, h, tile * TILE:(tile + 1) * TILE]

                def both_halves(tile):
                    return xn_ch[:, :, tile * TILE:(tile + 1) * TILE]

                def wide(row):
                    return row.unsqueeze(1).broadcast_to([P, 2, TILE])

                with nc.Block() as block:
                    @block.tensor
                    def _(pe):
                        pe.wait_ge(inner, BATCH + 2)
                        for h in range(HALVES):
                            m = nc.tensor.matmul(ps1[:, 0, 0:BATCH], g1[:, h, :], mean[:, h, :],
                                                 start=(h == 0), stop=(h == HALVES - 1))
                        m.then_inc(g_prod, 1)
                        pe.wait_ge(g_act, 1)
                        nc.tensor.matmul(ps2[0:D3, 0:BATCH], g2[:, :], gact1[:, :], start=True,
                                         stop=True).then_inc(g_prod, 1)
                        pe.wait_ge(g_act, 2)
                        nc.tensor.matmul(ps3[:, 0:BATCH], g3_rep[:, :], gact2[:, :], start=True,
                                         stop=True).then_inc(g_prod, 1)
                        pe.wait_ge(g_act, 3)

                        def unit(tile, which):
                            u = unit_order.index((tile, which))
                            terms = ([(w1[:, 0, :], 0), (w1[:, 1, :], 1)] if which == 0
                                     else [(w1[:, 0, :], 1), (w1_neg[:, :], 0)])
                            for m_ch in range(MCH):
                                if u > 0:
                                    pe.wait_ge(unit_kept, MCH * (u - 1) + m_ch + 1)
                                for i, (w, h) in enumerate(terms):
                                    m = nc.tensor.matmul(ps1[:, m_ch, :], w[:, m_ch * P:(m_ch + 1) * P],
                                                         state(h, tile), start=(i == 0), stop=(i == 1))
                                m.then_inc(unit_done, 1)

                        for n in range(JOBS + 4):
                            for u in units_before.get(n, []):
                                unit(*u)
                            if 3 <= n < JOBS + 3:
                                pe.wait_ge(gelu3_done, n - 3 + 1)
                                if n > 3:
                                    pe.wait_ge(gate_done, n - 3)
                                nc.tensor.matmul(ps4[:, :], w4_rep[:, :], act3[:, :], start=True,
                                                 stop=True).then_inc(l4_done, 1)
                            if 2 <= n < JOBS + 2:
                                pe.wait_ge(gelu2_done, n - 2 + 1)
                                nc.tensor.matmul(ps3[0:D3, :], w3[:, :], act2[:, :], start=True,
                                                 stop=True).then_inc(l3_done, 1)
                            if 1 <= n < JOBS + 1:
                                pe.wait_ge(gelu1_done, MCH * n)
                                for k in range(MCH):
                                    m = nc.tensor.matmul(ps2[:, :], w2[:, k, :], act1[:, k, :],
                                                         start=(k == 0), stop=(k == MCH - 1))
                                m.then_inc(l2_done, 1)
                            for u in units_behind.get(n, []):
                                unit(*u)
                            if n >= 4 and jobs[n - 4][1] == CYCLES - 1:
                                b, _, s = jobs[n - 4]
                                tile = b * TILES_B + s
                                pe.wait_ge(final_done, 2 * (tile + 1))
                                for pair in range(2):
                                    if tile > 0:
                                        pe.wait_ge(residual_done, (tile - 1) * 2 + pair + 1)
                                    for j in range(2):
                                        for h in range(HALVES):
                                            tok = (2 * pair + j) * P
                                            m = nc.tensor.transpose(ps_out[:, pair, j, h * P:(h + 1) * P],
                                                                    final[:, h, tok:tok + P], ident[:, :])
                                    m.then_inc(final_turned, 1)

                    @block.scalar
                    def _(act):
                        act.wait_ge(g_prod, 1)
                        nc.scalar.activation(gact1[:, :], ps1[:, 0, 0:BATCH], ACT.Gelu,
                                             bias=gb1[:, 0:1]).then_inc(g_act, 1)
                        act.wait_ge(g_prod, 2)
                        nc.scalar.activation(gact2[:, :], ps2[0:D3, 0:BATCH], ACT.Gelu,
                                             bias=gb2[:, 0:1]).then_inc(g_act, 1)
                        act.wait_ge(g_prod, 3)
                        nc.scalar.activation(gtanh[:, :], ps3[:, 0:BATCH], ACT.Tanh, bias=gb3_half[:, 0:1],
                                             scale=0.5).then_inc(g_act, 1)

                        def keep_unit(tile, which):
                            u = unit_order.index((tile, which))
                            if tile >= TILES_B:
                                act.wait_ge(y_done, update_count((tile // TILES_B - 1) * JOBS_B + TILES_B + tile % TILES_B))
                            for m_ch in range(MCH):
                                act.wait_ge(unit_done, MCH * u + m_ch + 1)
                                nc.scalar.activation(yz[:, tile % TILES_B, which, m_ch, :], ps1[:, m_ch, :], ACT.Copy)\
                                    .then_inc(unit_kept, 1)

                        for n in range(JOBS + 3):
                            for u in units_before.get(n, []):
                                keep_unit(*u)
                            if n >= 3:
                                j = n - 3
                                act.wait_ge(l4_done, j + 1)
                                if j >= 2:
                                    act.wait_ge(coupling_done, j - 1)
                                nc.scalar.activation(gate[:, j % 2, :], ps4[:, :], ACT.Tanh,
                                                     bias=b4_half[:, 0:1], scale=0.5).then_inc(gate_done, 1)
                            if 2 <= n < JOBS + 2:
                                act.wait_ge(l3_done, n - 1)
                                if n > 2:
                                    act.wait_ge(l4_done, n - 2)
                                nc.scalar.activation(act3[:, :], ps3[0:D3, :], ACT.Gelu,
                                                     bias=b3[:, 0:1]).then_inc(gelu3_done, 1)
                            if 1 <= n < JOBS + 1:
                                act.wait_ge(l2_done, n)
                                if n > 1:
                                    act.wait_ge(l3_done, n - 1)
                                nc.scalar.activation(act2[:, :], ps2[:, :], ACT.Gelu,
                                                     bias=b2[:, 0:1]).then_inc(gelu2_done, 1)
                            if n < JOBS:
                                b, c, s = jobs[n]
                                tile = b * TILES_B + s
                                if c == 0:
                                    act.wait_ge(unit_kept, kept_count(tile, 0))
                                else:
                                    act.wait_ge(y_done, update_count(n - TILES_B))
                                for m_ch in range(MCH):
                                    src = (yz[:, tile % TILES_B, 0, m_ch, :] if c == 0
                                           else y_now[:, (update_count(n - TILES_B) - 1) % 2, m_ch, :])
                                    if n > 0:
                                        act.wait_ge(l2_done, n)
                                    nc.scalar.activation(act1[:, m_ch, :], src, ACT.Gelu,
                                                         bias=b1[:, m_ch:m_ch + 1]).then_inc(gelu1_done, 1)
                            for u in units_behind.get(n, []):
                                keep_unit(*u)

                    @block.gpsimd
                    def _(pool):
                        for tile in range(TILES):
                            b, s = tile // TILES_B, tile % TILES_B
                            j = b * JOBS_B + (CYCLES - 1) * TILES_B + s
                            pool.wait_ge(coupling_done, j + 1)
                            nc.gpsimd.tensor_tensor(product_b[:, :], coupling[:, j % 2, :], coef_a[:, s, :], ALU.mult)\
                                .then_inc(b_steps, 1)
                            pool.wait_ge(b_steps, 3 * tile + 1)
                            nc.gpsimd.tensor_tensor(last_b[:, :], product_b[:, :], coef_b[:, s, :], ALU.add)\
                                .then_inc(b_steps, 1)
                            pool.wait_ge(b_steps, 3 * tile + 2)
                            pool.wait_ge(y_done, (b + 1) * (CYCLES - 1) * TILES_B)
                            if tile > 0:
                                pool.wait_ge(final_done, 2 * tile)
                            nc.gpsimd.tensor_tensor(b_part[:, :, :], both_halves(tile), wide(last_b[:, :]), ALU.mult)\
                                .then_inc(b_steps, 1)

                    @block.vector
                    def _(dve):
                        marks = [0]

                        def mark(ins):
                            marks[0] += 1
                            ins.then_inc(inner, 1)
                            return marks[0]

                        for b in range(BATCH):
                            sums = block_sums[:, :, b * BLK_B:(b + 1) * BLK_B].rearrange(
                                "p h (n two) -> p h n two", two=2)[:, :, :, 0]
                            summed = mark(nc.vector.tensor_reduce(mean[:, :, b:b + 1], sums, AX_X, ALU.add))
                        mark(nc.vector.tensor_scalar(w1_neg[:, :], w1[:, 1, :], -1.0, None, ALU.mult))
                        dve.wait_ge(inner, summed)
                        mark(nc.vector.tensor_scalar(mean[:, :, :], mean[:, :, :], 1.0 / SEQ, None, ALU.mult))

                        dve.wait_ge(g_act, 3)
                        ranged = mark(nc.vector.tensor_scalar(base[:, :], gtanh[:, :], rng[:, 0:1], 0.7, ALU.mult,
                                                              ALU.mult))
                        dve.wait_ge(inner, ranged)
                        based = mark(nc.vector.tensor_scalar(base[:, :], base[:, :], 0.1, None, ALU.add))
                        dve.wait_ge(inner, based)

                        def residual(tile):
                            for pair in range(2):
                                dve.wait_ge(final_turned, tile * 2 + pair + 1)
                                blk = tile * BLK_T + 2 * pair
                                kept = DM - P // 2
                                nc.vector.scalar_tensor_tensor(
                                    x_tok[:, blk:blk + 2, 0:kept], ps_out[:, pair, :, 0:kept], 0.5,
                                    x_tok[:, blk:blk + 2, 0:kept], ALU.mult, ALU.add)
                                nc.vector.scalar_tensor_tensor(
                                    x_tok[:, blk:blk + 2, kept:DM], ps_out[:, pair, :, kept:DM], -0.5,
                                    x_tok[:, blk:blk + 2, kept:DM], ALU.mult, ALU.add)\
                                    .then_inc(residual_done, 1)

                        for j, (b, c, s) in enumerate(jobs):
                            tile = b * TILES_B + s
                            dve.wait_ge(gate_done, j + 1)
                            if j >= 2 and jobs[j - 2][1] == CYCLES - 1:
                                before = jobs[j - 2][0] * TILES_B + jobs[j - 2][2]
                                dve.wait_ge(b_steps, 3 * before + 1)
                            c_now = coef_b[:, s, :] if c == 0 else coupling[:, j % 2, :]
                            nc.vector.tensor_scalar(c_now, gate[:, j % 2, :], gain[:, 0:1],
                                                    base[:, b:b + 1], ALU.mult, ALU.add)\
                                .then_inc(coupling_done, 1)
                            if c < CYCLES - 1:
                                slot = (update_count(j) - 1) % 2
                                dve.wait_ge(coupling_done, j + 1)
                                dve.wait_ge(unit_kept, kept_count(tile, 1))
                                if update_count(j) > 1:
                                    dve.wait_ge(y_done, update_count(j) - 1)
                                if b > 0:
                                    dve.wait_ge(final_done, 2 * b * TILES_B)
                            if c == 0:
                                added = mark(nc.vector.tensor_tensor(b_part[:, :, :], yz[:, tile % TILES_B, 1, :, :],
                                                                     wide(c_now), ALU.mult))
                                y_part = yz[:, tile % TILES_B, 0, :, :]
                            elif c == 1:
                                neg = mark(nc.vector.scalar_tensor_tensor(product_a[:, :], c_now, -1.0, coef_b[:, s, :],
                                                                          ALU.mult, ALU.mult))
                                dve.wait_ge(inner, neg)
                                summed = mark(nc.vector.tensor_tensor(coef_b[:, s, :], coef_b[:, s, :], c_now, ALU.add))
                                a_made = mark(nc.vector.tensor_scalar(coef_a[:, s, :], product_a[:, :], 1.0, None,
                                                                      ALU.add))
                                dve.wait_ge(inner, summed)
                                mark(nc.vector.tensor_tensor(b_part[:, :, :], yz[:, tile % TILES_B, 1, :, :],
                                                             wide(coef_b[:, s, :]), ALU.mult))
                                dve.wait_ge(inner, a_made)
                                added = mark(nc.vector.tensor_tensor(a_part[:, :, :], yz[:, tile % TILES_B, 0, :, :],
                                                                     wide(coef_a[:, s, :]), ALU.mult))
                                y_part = a_part[:, :, :]
                            if c < CYCLES - 1:
                                dve.wait_ge(inner, added)
                                if update_count(j) > 2:
                                    read_by = next(k + TILES_B for k in range(j)
                                                   if jobs[k][1] < CYCLES - 1 and update_count(k) == update_count(j) - 2)
                                    dve.wait_ge(gelu1_done, MCH * (read_by + 1))
                                nc.vector.tensor_tensor(y_now[:, slot, :, :], y_part, b_part[:, :, :], ALU.add)\
                                    .then_inc(y_done, 1)
                            else:
                                dve.wait_ge(coupling_done, j + 1)
                                neg = mark(nc.vector.scalar_tensor_tensor(product_a[:, :], c_now, -1.0, coef_b[:, s, :],
                                                                          ALU.mult, ALU.mult))
                                dve.wait_ge(inner, neg)
                                a_made = mark(nc.vector.tensor_tensor(last_a[:, :], product_a[:, :], coef_a[:, s, :],
                                                                      ALU.add))
                                dve.wait_ge(inner, a_made)
                                dve.wait_ge(y_done, (b + 1) * (CYCLES - 1) * TILES_B)
                                a_scaled = mark(nc.vector.tensor_tensor(a_part[:, :, :], both_halves(tile),
                                                                      wide(last_a[:, :]), ALU.mult))
                                if s > 0:
                                    residual(tile - 1)
                                dve.wait_ge(inner, a_scaled)
                                dve.wait_ge(b_steps, 3 * (tile + 1))
                                nc.vector.tensor_tensor(final[:, 0, :], a_part[:, 0, :], b_part[:, 1, :], ALU.add)\
                                    .then_inc(final_done, 1)
                                nc.vector.tensor_tensor(final[:, 1, :], a_part[:, 1, :], b_part[:, 0, :], ALU.subtract)\
                                    .then_inc(final_done, 1)
                            if c == 0 and s == 0 and b > 0:
                                residual(b * TILES_B - 1)
                        residual(TILES - 1)

                    if last:
                        @block.sync
                        def _(sp):
                            for k in range(TILES):
                                sp.wait_ge(residual_done, k * 2 + 2)
                                sp.dma_start(out_blocks[:, k * BLK_T:(k + 1) * BLK_T, :],
                                             x_tok[:, k * BLK_T:(k + 1) * BLK_T, :]).then_inc(stored, 16)
                            sp.wait_ge(stored, 16 * TILES)

        HEADS, DH = 16, DM // 16
        FEAT = proj.shape[0]
        STRIP = 32
        PER_G = P // STRIP
        GROUPS = HEADS // PER_G
        HALF_HEADS = HEADS // 2
        SCALE = DH ** -0.5
        X_SCALE = sqrt(SCALE)
        FSCALE = 4096.0
        UNSCALE = 1.0 / (FSCALE * FSCALE)
        WSCALE = 64.0
        LOCAL_SHARE = 1.0 - SCALE
        assert DH == 16 and FEAT == 24 and GROUPS == 4 and PER_G == 4

        def up_to_attention():
            with ExitStack() as scope:
                wq_s = [sb(f"wq_s_{part}", [P, HALVES, HEADS * STRIP], F16, scope) for part in ("high", "low")]
                wk_s = [sb(f"wk_s_{part}", [P, HALVES, HEADS * STRIP], F16, scope) for part in ("high", "low")]
                w_vq = [sb(f"w_vq_{part}", [P, HALVES, 2 * DM], F16, scope) for part in ("high", "low")]
                w_qf = [sb(f"w_qf_{part}", [P, HALVES, HEADS * FEAT], F16, scope) for part in ("high", "low")]
                w_o = sb("w_o", [P, HALVES, DM], F32, scope)
                bq_s = sb("bq_s", [P, GROUPS], F32, scope)
                bk_s = sb("bk_s", [P, GROUPS], F32, scope)
                b_vq = sb("b_vq", [P, 2 * DM], F32, scope)
                b_qf = sb("b_qf", [P, HEADS * FEAT], F32, scope)
                b_o = sb("b_o", [P, DM], F32, scope)
                log_k = nc.dram_tensor("log_k", (NBLK + 2, P, GROUPS, P), F32, kind="Internal").ap()
                neg_kmax = sb("neg_kmax", [P, NBLK + 1, GROUPS], F32, scope)
                kmax_tok = sb("kmax_tok", [P, NBLK + 1, HEADS], F32, scope)
                penalty = sb("penalty", [P, NBLK + 1], F32, scope)
                has_prev = sb("has_prev", [P, NBLK + 1], F32, scope)
                keep_state = sb("keep_state", [P, NBLK + 1], F32, scope)
                low_rows = sb("low_rows", [P, 1], F32, scope)
                ident16 = sb("ident16", [P, P], BF16, scope)
                mask_q = sb("mask_q", [P, 2, 2, P], BF16, scope)
                stair_own_l = sb("stair_own_l", [P, P], BF16, scope)
                stair_prev_l = sb("stair_prev_l", [P, P], BF16, scope)
                stair_own_r = sb("stair_own_r", [P, HEADS, P], BF16, scope)
                stair_prev_r = sb("stair_prev_r", [P, HEADS, P], BF16, scope)
                gmask = sb("gmask", [P, 2, P], F32, scope)
                diag_strips = sb("diag_strips", [P, PER_G, STRIP], F32, scope)

                def attention_weights(scope):
                    rows = sb("qkv_rows", [P, 3 * HALVES, DM], F32, scope)
                    o_rows = sb("o_rows", [P, HALVES, DM], F32, scope)
                    bq_col = sb("bq_col", [P, HALVES], F32, scope)
                    bq_rep = sb("bq_rep", [P, HALVES, P], F32, scope)
                    BANKS = 4
                    ps = [psum(f"prep_ps{i}", [P, 512], scope) for i in range(BANKS)]
                    loaded = sem("prep_loaded", scope)
                    blank = sem("prep_blank", scope)
                    drawn = sem("prep_drawn", scope)
                    tables = sem("prep_tables", scope)
                    product = sem("prep_product", scope)
                    evacuated = sem("prep_evacuated", scope)
                    reps = sem("prep_reps", scope)
                    high_kept = sem("prep_high_kept", scope)

                    row = lambda v, n: v.rearrange("(a n) -> a n", a=1).broadcast_to([P, n])
                    loads = [
                        (rows[:, :, :], wqkv.rearrange("(k p) n -> p k n", p=P)),
                        (o_rows[:, :, :], wout.rearrange("(k p) n -> p k n", p=P)),
                        (bq_col[:, :], bqkv[0:DM].rearrange("(k p) -> p k", p=P)),
                        (bk_col[:, :], bqkv[DM:2 * DM].rearrange("(k p) -> p k", p=P)),
                        (b_vq[:, 0:DM], row(bqkv[2 * DM:3 * DM], DM)),
                        (b_vq[:, DM:2 * DM], row(bqkv[0:DM], DM)),
                        (b_o[:, :], row(bout, DM)),
                    ]
                    for j in range(HALF_HEADS):
                        loads.append((proj_bd[j * DH:(j + 1) * DH, j, :], proj.rearrange("m d -> d m")))
                    for which, dst in ((0, bq_s), (1, bk_s)):
                        src = bqkv[which * DM:(which + 1) * DM].rearrange("(g r d) -> r d g", g=GROUPS, r=PER_G)
                        for r in range(PER_G):
                            for dup in range(2):
                                at = r * STRIP + dup * DH
                                loads.append((dst[at:at + DH, :], src[r]))

                    jobs = []
                    for k in range(HALVES):
                        for i in range(HALVES):
                            def strips(w, dup, k=k, i=i):
                                return [part[:, k, i * HALF_HEADS * STRIP:(i + 1) * HALF_HEADS * STRIP].rearrange(
                                    "p (h s) -> p h s", s=STRIP)[:, :, dup * DH:(dup + 1) * DH] for part in w]

                            def halves(w, at, k=k):
                                return [part[:, k, at] for part in w]
                            heads = "p (h d) -> p h d"
                            jobs.append((("turn", rows, i, k), [(strips(wq_s, 0), SCALE, heads), (strips(wq_s, 1), SCALE, heads),
                                                                (halves(w_vq, slice(DM + i * P, DM + (i + 1) * P)), 1.0, None)]))
                            jobs.append((("turn", rows, 2 + i, k), [(strips(wk_s, 0), 1.0, heads), (strips(wk_s, 1), 1.0, heads),
                                                                    (w_k[:, k, i * P:(i + 1) * P], 1.0, None)]))
                            jobs.append((("turn", rows, 4 + i, k), [(halves(w_vq, slice(i * P, (i + 1) * P)), 1.0, None)]))
                            jobs.append((("turn", o_rows, i, k), [(w_o[:, k, i * P:(i + 1) * P], 1.0, None)]))
                            jobs.append((("feat", rows, i, k), [(halves(w_qf, slice(i * HALF_HEADS * FEAT, (i + 1) * HALF_HEADS * FEAT)),
                                                                 X_SCALE, None)]))
                    for i in range(HALVES):
                        jobs.append((("bias", bq_rep, i, 0), [(b_qf[:, i * HALF_HEADS * FEAT:(i + 1) * HALF_HEADS * FEAT],
                                                               X_SCALE, None)]))

                    def evacuations(n):
                        (kind, *_), views = jobs[n]
                        src = ps[n % BANKS][:, 0:P if kind == "turn" else HALF_HEADS * FEAT]
                        return [(view, scale, src.rearrange(split, d=DH) if split else src)
                                for view, scale, split in views]

                    highs_until = [sum(isinstance(view, list) for _, views in jobs[:n + 1] for view, *_ in views)
                                   for n in range(len(jobs))]

                    def on_sync(sp):
                        sp.wait_ge(blank, 1)
                        for dst, src in loads:
                            sp.dma_start(dst, src, allow_slow_non_contiguous=True).then_inc(loaded, 16)

                    def on_gpsimd(pool):
                        nc.gpsimd.memset(proj_bd[:, :, :], 0.0).then_inc(blank, 1)
                        zero = [(ident16, 0.0), (mask_q, 0.0), (stair_own_l, 1.0), (stair_prev_l, 1.0),
                                (stair_own_r, 0.0), (stair_prev_r, 0.0), (gmask[:, 0, :], LOCAL_SHARE),
                                (gmask[:, 1, :], 1.0), (diag_strips, 1.0), (low_rows, 1.0),
                                (penalty, 0.0), (has_prev, 1.0), (keep_state, 1.0),
                                ]
                        for buf, value in zero:
                            last = nc.gpsimd.memset(buf if isinstance(buf, bass.AP) else buf[tuple([slice(None)] * len(buf.shape))], value)
                        last.then_inc(blank, 1)
                        pool.wait_ge(blank, 2)

                        selected = [0]

                        def select(view, op, fill, base, pattern, mult):
                            selected[0] += 1
                            nc.gpsimd.affine_select(out=view, in_=view, compare_op=op, fill=fill, base=base,
                                                    pattern=pattern, channel_multiplier=mult)\
                                .then_inc(drawn, 1)
                            pool.wait_ge(drawn, selected[0])

                        select(ident16[:, :], ALU.not_equal, 1.0, 0, [[-1, P]], 1)
                        for order in range(2):
                            own, prev = 1 - order, order
                            select(mask_q[:, order, own, :], ALU.is_ge, MASKED, 0, [[-1, P]], 1)
                            select(mask_q[:, order, prev, :], ALU.is_ge, MASKED, 0, [[1, P]], -1)
                        select(stair_own_l[:, :], ALU.is_ge, 0.0, 0, [[1, P]], -1)
                        select(stair_prev_l[:, :], ALU.is_ge, 0.0, 0, [[-1, P]], 1)
                        select(stair_own_r[:, :, :], ALU.not_equal, MASKED, -1, [[0, HEADS], [-1, P]], 1)
                        select(stair_prev_r[:, :, :], ALU.not_equal, MASKED, 1, [[0, HEADS], [-1, P]], 1)
                        select(gmask[:, 0, :], ALU.is_ge, 0.0, 0, [[1, P]], -1)
                        select(gmask[:, 1, :], ALU.is_gt, LOCAL_SHARE, 0, [[1, P]], -1)
                        select(diag_strips[:, :, :], ALU.is_ge, 0.0, 0, [[-STRIP, PER_G], [0, STRIP]], 1)
                        select(diag_strips[:, :, :], ALU.is_ge, 0.0, STRIP - 1, [[STRIP, PER_G], [0, STRIP]], -1)
                        first_of_batch = [b * BLK_B for b in range(BATCH + 1)]
                        for blk in first_of_batch:
                            nc.gpsimd.memset(penalty[:, blk:blk + 1], MASKED)
                            nc.gpsimd.memset(has_prev[:, blk:blk + 1], 0.0)
                            nc.gpsimd.memset(keep_state[:, blk:blk + 1], 0.0)
                            if blk:
                                nc.gpsimd.memset(keep_state[:, blk - 1:blk], 0.0)
                        nc.gpsimd.memset(ident16[0:1, 0:1], 1.0).then_inc(tables, 1)

                    def on_vector(dve):
                        dve.wait_ge(loaded, 16 * len(loads))
                        nc.vector.tensor_copy(bq_rep[:, :, :], bq_col[:, :].unsqueeze(2).broadcast_to([P, HALVES, P]))\
                            .then_inc(reps, 1)
                        dve.wait_ge(tables, 1)
                        nc.vector.tensor_reduce(
                            low_rows[:, :],
                            ident16[:, :].rearrange("p (r two d) -> p r two d", two=2, d=DH)[:, :, 1, :],
                            mybir.AxisListType.XY, ALU.add)
                        nc.vector.tensor_scalar(bq_s[:, :], bq_s[:, :], SCALE, None, ALU.mult)
                        for n in range(len(jobs)):
                            dve.wait_ge(product, n + 1)
                            if highs_until[n] > (highs_until[n - 1] if n else 0):
                                dve.wait_ge(high_kept, highs_until[n])
                            for view, scale, src in evacuations(n):
                                if isinstance(view, list):
                                    last = nc.vector.scalar_tensor_tensor(view[1], src, scale * WSCALE, view[0],
                                                                          ALU.mult, ALU.subtract)
                                else:
                                    last = nc.vector.tensor_scalar(view, src, scale, None, ALU.mult)
                            last.then_inc(evacuated, 1)

                    def on_scalar(act):
                        for n in range(len(jobs)):
                            parted = [e for e in evacuations(n) if isinstance(e[0], list)]
                            if parted:
                                act.wait_ge(product, n + 1)
                            for view, scale, src in parted:
                                nc.scalar.activation(view[0], src, ACT.Copy, scale=scale * WSCALE)\
                                    .then_inc(high_kept, 1)

                    def on_tensor(pe):
                        pe.wait_ge(loaded, 16 * len(loads))
                        for n, ((kind, src, i, k), _) in enumerate(jobs):
                            if n >= BANKS:
                                pe.wait_ge(evacuated, n - BANKS + 1)
                            bank = ps[n % BANKS]
                            if kind == "turn":
                                last = nc.tensor.transpose(bank[:, 0:P], src[:, i, k * P:(k + 1) * P], ident[:, :])
                            else:
                                if kind == "bias":
                                    pe.wait_ge(reps, 1)
                                left = src[:, i, k * P:(k + 1) * P] if kind == "feat" else src[:, i, :]
                                last = nc.tensor.matmul(bank[:, 0:HALF_HEADS * FEAT], left,
                                                        proj_bd[:, :, :].rearrange("p h m -> p (h m)"),
                                                        start=True, stop=True)
                            last.then_inc(product, 1)

                    return {"sync": on_sync, "gpsimd": on_gpsimd, "vector": on_vector, "scalar": on_scalar,
                            "tensor": on_tensor}

                def key_features(outer):
                    TILES = NBLK // BLK_T
                    with ExitStack() as scope:
                        lift = sb("lift", [P, 2, PER_G, STRIP], F32, scope)
                        halve = sb("halve", [P, HALF_HEADS, STRIP], F32, scope)
                        ones_sq = sb("ones_sq", [P, P], F32, scope)
                        strip_head = sb("strip_head", [P, PER_G], F32, scope)
                        k_and_sq = sb("k_and_sq", [P, 2, GROUPS, TILE], F32, scope)
                        logs_sb = sb("logs_sb", [P, 2, GROUPS, TILE], F32, scope)
                        no_logs = sb("no_logs", [P, GROUPS, P], F32, scope)
                        tile_max = sb("tile_max", [P, BATCH, GROUPS, TILES_B], F32, scope)
                        row_max = sb("row_max", [P, STRIP], F32, scope)
                        row_max_t = sb("row_max_t", [P, STRIP], F32, scope)
                        head_max = sb("head_max", [P, 1], F32, scope)
                        head_max_b = sb("head_max_b", [P, STRIP], F32, scope)
                        kmax = sb("kmax", [P, STRIP], F32, scope)
                        one_row = sb("one_row", [P, BATCH, GROUPS, PER_G], F32, scope)
                        ps_k = psum("ps_k", [P, HALVES, TILE], scope)
                        ps_log = psum("ps_log", [P, GROUPS, TILE], scope)
                        ps_spread = psum("ps_spread", [P, 512], scope)
                        patterns = sem("kf_patterns", scope)
                        lift_ready = sem("lift_ready", scope)
                        k_product = sem("k_product", scope)
                        k_ready = sem("k_ready", scope)
                        k_sq_ready = sem("k_sq_ready", scope)
                        log_product = sem("log_product", scope)
                        log_kept = sem("log_kept", scope)
                        log_max = sem("log_max", scope)
                        log_stored = [sem(f"log_stored{i}", scope) for i in range(2)]
                        pad_stored = sem("pad_stored", scope)
                        chain = sem("kmax_chain", scope)
                        spread = sem("kmax_spread", scope)
                        with nc.Block() as block:
                            @block.gpsimd
                            def _(pool):
                                nc.gpsimd.memset(halve[:, :, :], -SCALE / 2)
                                nc.gpsimd.memset(strip_head[:, :], 0.0)
                                nc.gpsimd.memset(row_max[:, :], 0.0)
                                nc.gpsimd.memset(no_logs[:, :, :], 0.0)
                                nc.gpsimd.memset(ones_sq[:, :], 1.0).then_inc(patterns, 1)
                                pool.wait_ge(patterns, 1)
                                nc.gpsimd.affine_select(out=halve[:, :, :], in_=halve[:, :, :], compare_op=ALU.is_ge, fill=0.0,
                                                        base=0, pattern=[[-DH, HALF_HEADS], [0, STRIP]], channel_multiplier=1)\
                                    .then_inc(patterns, 1)
                                pool.wait_ge(patterns, 2)
                                nc.gpsimd.affine_select(out=halve[:, :, :], in_=halve[:, :, :], compare_op=ALU.is_ge, fill=0.0,
                                                        base=DH - 1, pattern=[[DH, HALF_HEADS], [0, STRIP]], channel_multiplier=-1)
                                nc.gpsimd.affine_select(out=strip_head[:, :], in_=strip_head[:, :], compare_op=ALU.not_equal,
                                                        fill=1.0, base=0, pattern=[[-STRIP, PER_G]], channel_multiplier=1)\
                                    .then_inc(patterns, 1)

                            @block.tensor
                            def _(pe):
                                def keys(n):
                                    for i in range(HALVES):
                                        for k in range(HALVES):
                                            m = nc.tensor.matmul(ps_k[:, i, :], w_k[:, k, i * P:(i + 1) * P],
                                                                 xn_ch[:, k, ds(n * TILE, TILE)], start=(k == 0),
                                                                 stop=(k == HALVES - 1))
                                    m.then_inc(k_product, 1)

                                def logs(n, par, peeled):
                                    pe.wait_ge(k_sq_ready, n + 1)
                                    for g in range(GROUPS):
                                        if not peeled:
                                            pe.wait_ge(log_kept, (n - 1) * GROUPS + g + 1)
                                            pe.wait_ge(log_max, (n - 1) * GROUPS + g + 1)
                                        nc.tensor.matmul(ps_log[:, g, :], lift[:, g % 2, :, :].rearrange("p h m -> p (h m)"),
                                                         k_and_sq[:, par, g, :], start=True, stop=True)\
                                            .then_inc(log_product, 1)

                                pe.wait_ge(patterns, 3)
                                pe.wait_ge(lift_ready, 1)
                                keys(0)
                                for n in range(2):
                                    pe.wait_ge(k_ready, n + 1)
                                    keys(n + 1)
                                    logs(n, n, n == 0)
                                with pe.Fori(1, TILES // 2 - 1) as j:
                                    for par in range(2):
                                        n = j * 2 + par
                                        pe.wait_ge(k_ready, n + 1)
                                        keys(n + 1)
                                        logs(n, par, False)
                                for n in range(TILES - 2, TILES):
                                    pe.wait_ge(k_ready, n + 1)
                                    if n + 1 < TILES:
                                        keys(n + 1)
                                    logs(n, n % 2, False)
                                pe.wait_ge(chain, 7)
                                nc.tensor.matmul(ps_spread[:, 0:BATCH * HEADS], ones_sq[:, :],
                                                 one_row[:, :, :, :].rearrange("p b g r -> p (b g r)"), start=True,
                                                 stop=True).then_inc(spread, 1)

                            @block.scalar
                            def _(act):
                                def tile(n, par, peeled):
                                    act.wait_ge(k_ready, n + 1)
                                    if not peeled:
                                        act.wait_ge(log_product, (n - 1) * GROUPS)
                                    for q in range(2):
                                        own, other = slice(q * P // 2, (q + 1) * P // 2), slice((1 - q) * P // 2, (2 - q) * P // 2)
                                        a = nc.scalar.activation(k_and_sq[other, par, q::2, :], k_and_sq[own, par, q::2, :],
                                                                 ACT.Square)
                                    a.then_inc(k_sq_ready, 1)

                                def keep_logs(n, par, before):
                                    if before is not None:
                                        act.wait_ge(log_stored[par], 16 * before)
                                    for g in range(GROUPS):
                                        act.wait_ge(log_product, n * GROUPS + g + 1)
                                        act.wait_ge(log_max, n * GROUPS + g + 1)
                                        nc.scalar.activation(logs_sb[:, par, g, :], ps_log[:, g, :],
                                                             ACT.Identity).then_inc(log_kept, 1)

                                tile(0, 0, True)
                                tile(1, 1, True)
                                keep_logs(0, 0, None)
                                tile(2, 0, False)
                                keep_logs(1, 1, None)
                                tile(3, 1, False)
                                keep_logs(2, 0, 1)
                                with act.Fori(2, TILES // 2) as j:
                                    tile(j * 2, 0, False)
                                    keep_logs(j * 2 - 1, 1, j - 1)
                                    tile(j * 2 + 1, 1, False)
                                    keep_logs(j * 2, 0, j)
                                keep_logs(TILES - 1, 1, TILES // 2 - 1)

                            @block.sync
                            def _(sp):
                                for n in range(TILES):
                                    sp.wait_ge(log_kept, (n + 1) * GROUPS)
                                    sp.dma_start(log_k[n * BLK_T:(n + 1) * BLK_T, :, :, :].rearrange("a p g q -> p g a q"),
                                                 logs_sb[:, n % 2, :, :].rearrange("p g (a q) -> p g a q", q=P))\
                                        .then_inc(log_stored[n % 2], 16)
                                sp.wait_ge(patterns, 3)
                                for pad in range(2):
                                    sp.dma_start(log_k[NBLK + pad, :, :, :], no_logs[:, :, :]).then_inc(pad_stored, 16)
                                for stored in log_stored:
                                    sp.wait_ge(stored, 16 * (TILES // 2))
                                sp.wait_ge(pad_stored, 32)

                            @block.vector
                            def _(dve):
                                dve.wait_ge(patterns, 3)
                                for q in range(2):
                                    own, other = slice(q * P // 2, (q + 1) * P // 2), slice((1 - q) * P // 2, (2 - q) * P // 2)
                                    mine, theirs = slice(q * PER_G, (q + 1) * PER_G), slice((1 - q) * PER_G, (2 - q) * PER_G)
                                    nc.vector.tensor_scalar(lift[own, q, :, 0:FEAT], proj_bd[own, mine, :], X_SCALE, None,
                                                            ALU.mult)
                                    nc.vector.tensor_scalar(lift[own, q, :, FEAT:STRIP],
                                                            proj_bd[own, mine, 0:1].broadcast_to([P // 2, PER_G, STRIP - FEAT]),
                                                            X_SCALE, None, ALU.mult)
                                    last = nc.vector.tensor_copy(lift[other, q, :, :], halve[other, theirs, :])
                                last.then_inc(lift_ready, 1)

                                def keys(n):
                                    dve.wait_ge(k_product, n + 1)
                                    if n >= 2:
                                        dve.wait_ge(log_product, (n - 1) * GROUPS)
                                    for q in range(2):
                                        own = slice(q * P // 2, (q + 1) * P // 2)
                                        k = nc.vector.tensor_tensor(
                                            k_and_sq[own, n % 2, q::2, :], ps_k[own, :, :],
                                            bk_col[own, :].unsqueeze(2).broadcast_to([P // 2, HALVES, TILE]), ALU.add)
                                    k.then_inc(k_ready, 1)

                                keys(0)
                                for b in range(BATCH):
                                    for s in range(TILES_B):
                                        if b * TILES_B + s + 1 < TILES:
                                            keys(b * TILES_B + s + 1)
                                        for g in range(GROUPS):
                                            n = (b * TILES_B + s) * GROUPS + g
                                            dve.wait_ge(log_product, n + 1)
                                            nc.vector.tensor_reduce(tile_max[:, b, g, s:s + 1], ps_log[:, g, :], AX_X,
                                                                    ALU.max).then_inc(log_max, 1)
                                dve.wait_ge(log_max, NBLK // BLK_T * GROUPS)
                                dve.wait_ge(patterns, 3)

                                steps = [0]

                                def link(ins):
                                    steps[0] += 1
                                    ins.then_inc(chain, 1)
                                    dve.wait_ge(chain, steps[0])

                                link(nc.vector.tensor_reduce(row_max[:, 0:BATCH * GROUPS],
                                                             tile_max[:, :, :, :].rearrange("p b g s -> p (b g) s"), AX_X, ALU.max))
                                link(nc.vector.transpose(row_max_t[:, :], row_max[:, :]))
                                link(nc.vector.tensor_reduce(head_max[:, :], row_max_t[:, :], AX_X, ALU.max))
                                link(nc.vector.tensor_copy(head_max_b[:, :], head_max[:, :].broadcast_to([P, STRIP])))
                                link(nc.vector.transpose(kmax[:, :], head_max_b[:, :]))
                                km = kmax[:, 0:BATCH * GROUPS].rearrange("p (b g) -> p b g", b=BATCH)
                                link(nc.vector.memset(neg_kmax[:, NBLK:, :], 0.0))
                                link(nc.vector.tensor_tensor(
                                    one_row[:, :, :, :].rearrange("p b g r -> p (b g) r"),
                                    kmax[:, 0:BATCH * GROUPS].unsqueeze(2).broadcast_to([P, BATCH * GROUPS, PER_G]),
                                    strip_head[:, :].unsqueeze(1).broadcast_to([P, BATCH * GROUPS, PER_G]), ALU.mult))
                                for b in range(BATCH):
                                    nc.vector.tensor_scalar(neg_kmax[:, b * BLK_B:(b + 1) * BLK_B, :],
                                                            km[:, b:b + 1, :].broadcast_to([P, BLK_B, GROUPS]), -1.0, None,
                                                            ALU.mult)
                                dve.wait_ge(spread, 1)
                                nc.vector.memset(kmax_tok[:, NBLK:, :], 0.0)
                                for b in range(BATCH):
                                    nc.vector.tensor_copy(
                                        kmax_tok[:, b * BLK_B:(b + 1) * BLK_B, :],
                                        ps_spread[:, b * HEADS:(b + 1) * HEADS].unsqueeze(1).broadcast_to([P, BLK_B, HEADS]))

                def attention_blocks(outer):
                    RING = 4
                    FEATURE_ITEMS = (5, 7, 9, 12)
                    with ExitStack() as scope:
                        x_high = sb("x_high", [P, 2, HALVES, P], F16, scope)
                        x_low = sb("x_low", [P, 2, HALVES, P], F16, scope)
                        q32 = sb("q32", [P, GROUPS, P], F32, scope)
                        k32 = sb("k32", [P, GROUPS, P], F32, scope)
                        q_high = sb("q_high", [P, GROUPS, P], F16, scope)
                        q_low = sb("q_low", [P, GROUPS, P], F16, scope)
                        k_lowhigh = sb("k_lowhigh", [P, GROUPS, P], F16, scope)
                        q_bd = sb("q_bd", [P, 2, 2, GROUPS, PER_G, P], F16, scope)
                        k_mix = sb("k_mix", [P, GROUPS, RING, P], F16, scope)
                        v_ext = sb("v_ext", [P, RING, HEADS, STRIP], F32, scope)
                        q_tok = sb("q_tok", [P, DM], F32, scope)
                        qf_tok = sb("qf_tok", [P, HEADS, FEAT], F32, scope)
                        qf_pad = sb("qf_pad", [P, HEADS, STRIP], F32, scope)
                        q_norm = sb("q_norm", [P, HEADS], F32, scope)
                        qf_max = sb("qf_max", [P, HEADS], F32, scope)
                        q_scale = sb("q_scale", [P, HEADS], F32, scope)
                        g_scale = sb("g_scale", [P, 2, HEADS], F32, scope)
                        log_blk = sb("log_blk", [P, GROUPS, P], F32, scope)
                        scaled_eps = sb("scaled_eps", [P, 1], F32, scope)
                        kf32 = sb("kf32", [P, GROUPS, P], F32, scope)
                        kf_high = sb("kf_high", [P, RING, GROUPS, P], F16, scope)
                        kf_low = sb("kf_low", [P, RING, GROUPS, P], F16, scope)
                        kf_tok = sb("kf_tok", [P, 2, HEADS * STRIP], F32, scope)
                        qf32 = sb("qf32", [P, 2, GROUPS, P], F32, scope)
                        qf_high = sb("qf_high", [P, GROUPS, P], F16, scope)
                        qf_low = sb("qf_low", [P, GROUPS, P], F16, scope)
                        qf_bd = sb("qf_bd", [P, 2, 1, GROUPS, PER_G, P], F16, scope)
                        block_max = sb("block_max", [P, GROUPS, PER_G, 2], F32, scope)
                        row_top = sb("row_top", [P, HEADS], F32, scope)
                        neg_max = sb("neg_max", [P, 2, HEADS], BF16, scope)
                        max_rows = sb("max_rows", [2 * HEADS, P], BF16, scope)
                        lift_arg = sb("lift_arg", [P, HEADS], F32, scope)
                        lift_exp = sb("lift_exp", [P, 2, HEADS], F32, scope)
                        probs = sb("probs", [P, 2, 2, PER_G, P], F32, scope)
                        feats = sb("feats", [P, 2, 2, PER_G, P], F32, scope)
                        state = sb("kv_state", [P, GROUPS, P], F32, scope)
                        state_inc = sb("kv_state_inc", [P, GROUPS, P], F32, scope)
                        sums = sb("sums", [P, 2, GROUPS * P], F32, scope)
                        r_local = sb("r_local", [P, HEADS], F32, scope)
                        norm_a = sb("norm_a", [P, HEADS], F32, scope)
                        norm_b = sb("norm_b", [P, HEADS], F32, scope)
                        norm_c = sb("norm_c", [P, HEADS], F32, scope)
                        norm_r = sb("norm_r", [P, HEADS], F32, scope)
                        r_global = sb("r_global", [P, HEADS], F32, scope)
                        ctx_a = sb("ctx_a", [P, HEADS, DH], F32, scope)
                        ctx = sb("ctx", [P, DM], F32, scope)
                        ctx_ch = sb("ctx_ch", [P, HALVES, P], F32, scope)

                        pairs = [psum(f"pair{i}", [P, 2, 512], scope) for i in range(3)]
                        ps_local = psum("ps_local", [P, GROUPS * P], scope)
                        ps_global = psum("ps_global", [P, GROUPS * P], scope)

                        def pair(item):
                            return pairs[item % 3]

                        PASSES = ((0, x_high), (1, x_high), (0, x_low))

                        def S(name):
                            return sem("a_" + name, scope)

                        cleared, cleared_dve = S("cleared"), S("cleared_dve")
                        x_high_ready, x_ready = S("x_high_ready"), S("x_ready")
                        qk_product, q32_ready, k32_ready = S("qk_product"), S("q32_ready"), S("k32_ready")
                        q_high_ready, k_lowhigh_ready = S("q_high_ready"), S("k_lowhigh_ready")
                        q_low_ready, k_mix_ready, q_bd_ready = S("q_low_ready"), S("k_mix_ready"), S("q_bd_ready")
                        vq_product, v_ready, q_tok_ready, qf_ready = S("vq_product"), S("v_ready"), S("q_tok_ready"), S("qf_ready")
                        q_sq_ready, q_norm_ready, qf_max_ready, qf_shifted = S("q_sq_ready"), S("q_norm_ready"), S("qf_max_ready"), S("qf_shifted")
                        q_scale_ready, g_scale_ready = S("q_scale_ready"), S("g_scale_ready")
                        qf_exp_ready, qf_pad_ready = S("qf_exp_ready"), S("qf_pad_ready")
                        log_loaded = S("log_loaded")
                        kf_exp_ready, kf32_ready, kf_high_ready, kf_low_ready = S("kf_exp_ready"), S("kf32_ready"), S("kf_high_ready"), S("kf_low_ready")
                        turned, qf32_ready, kf_tok_ready = S("turned"), S("qf32_ready"), S("kf_tok_ready")
                        qf_high_ready, qf_low_ready, qf_bd_ready = S("qf_high_ready"), S("qf_low_ready"), S("qf_bd_ready")
                        qs_product, qs_max = S("qs_product"), S("qs_max")
                        row_top_ready, neg_max_ready, penal_ready = S("row_top_ready"), S("neg_max_ready"), S("penal_ready")
                        lift_arg_ready, lift_exp_ready = S("lift_arg_ready"), S("lift_exp_ready")
                        max_turned, max_rows_ready, max_placed = S("max_turned"), S("max_rows_ready"), S("max_placed")
                        f_product, f_ready = S("f_product"), S("f_ready")
                        ks_product, p_ready = S("ks_product"), S("p_ready")
                        global_done, local_done = S("global_done"), S("local_done")
                        state_read, inc_product, inc_ready, state_ready = S("state_read"), S("inc_product"), S("inc_ready"), S("state_ready")
                        sums_ready, sums_turned = S("sums_ready"), S("sums_turned")
                        norm_parts, norm_ready = S("norm_parts"), S("norm_ready")
                        r_ready, ctx_parts, ctx_ready = S("r_ready"), S("ctx_parts"), S("ctx_ready")
                        ctx_turned, ctx_ch_ready = S("ctx_turned"), S("ctx_ch_ready")
                        y_product, y_ready, x_biased = S("y_product"), S("y_ready"), S("x_biased")

                        def wait(eng, signal, count):
                            if not isinstance(count, int) or count > 0:
                                eng.wait_ge(signal, count)

                        def flat(v):
                            return v.rearrange("p a b -> p (a b)")

                        def scheduled(eng, one_block):
                            for par in range(RING):
                                one_block(par, par)
                            with eng.Fori(1, NBLK // RING) as i:
                                for par in range(RING):
                                    one_block(i * RING + par, par)

                        with nc.Block() as block:
                            @block.gpsimd
                            def _(pool):
                                nc.gpsimd.memset(scaled_eps[:, :], FEATURE_EPS * FSCALE).then_inc(cleared, 1)
                                for view in (v_ext[:, :, :, :], kf_tok[:, 1, :], qf_pad[:, :, :], state[:, :, :]):
                                    last = nc.gpsimd.memset(view, 0.0)
                                last.then_inc(cleared, 1)
                                pool.wait_ge(cleared, 2)
                                nc.gpsimd.memset(v_ext[:, :, :, DH:DH + 1], 1.0).then_inc(cleared, 1)

                                def low_x(f, par):
                                    pool.wait_ge(x_high_ready, f + 1)
                                    nc.gpsimd.tensor_tensor(x_low[:, par % 2, :, :], xn_ch[:, :, ds(f * P, P)],
                                                            x_high[:, par % 2, :, :], ALU.subtract).then_inc(x_ready, 1)

                                def front(f, par):
                                    pool.wait_ge(kf32_ready, f + 1)
                                    pool.wait_ge(kf_high_ready, f + 1)
                                    nc.gpsimd.tensor_tensor(kf_low[:, par, :, :], kf32[:, :, :], kf_high[:, par, :, :],
                                                            ALU.subtract).then_inc(kf_low_ready, 1)
                                    pool.wait_ge(q_high_ready, f + 1)
                                    wait(pool, q_bd_ready, 2 * f)
                                    nc.gpsimd.tensor_tensor(q_low[:, :, :], q32[:, :, :], q_high[:, :, :], ALU.subtract)\
                                        .then_inc(q_low_ready, 1)
                                    pool.wait_ge(k_lowhigh_ready, f + 1)
                                    nc.gpsimd.tensor_tensor(k_mix[:, :, par, :], k32[:, :, :], k_lowhigh[:, :, :],
                                                            ALU.subtract).then_inc(k_mix_ready, 1)
                                    pool.wait_ge(qf_max_ready, f + 1)
                                    nc.gpsimd.tensor_tensor(qf_tok[:, :, :], qf_tok[:, :, :],
                                                            qf_max[:, :].unsqueeze(2).broadcast_to([P, HEADS, FEAT]),
                                                            ALU.subtract).then_inc(qf_shifted, 1)
                                    pool.wait_ge(qf_high_ready, f + 1)
                                    wait(pool, qf_bd_ready, 2 * f)
                                    nc.gpsimd.tensor_tensor(qf_low[:, :, :], qf32[:, par % 2, :, :], qf_high[:, :, :],
                                                            ALU.subtract).then_inc(qf_low_ready, 1)

                                low_x(0, 0)
                                nc.gpsimd.memset(qf_bd[:, :, :, :, :, :], 0.0).then_inc(cleared, 1)
                                pool.wait_ge(cleared_dve, 1)
                                front(0, 0)

                                def output_bias(n):
                                    x_row = x_tok[:, ds(n, 1), :].rearrange("p a c -> p (a c)")
                                    nc.gpsimd.tensor_tensor(x_row, x_row, b_o[:, :], ALU.add).then_inc(x_biased, 1)

                                def one_block(n, par):
                                    low_x(n + 1, (par + 1) % RING)
                                    output_bias(n)
                                    front(n + 1, (par + 1) % RING)

                                scheduled(pool, one_block)

                            @block.sync
                            def _(sp):
                                def one_block(n, par):
                                    sp.wait_ge(max_rows_ready, n + 1)
                                    sp.dma_start(stair_own_r[0:1, :, :], max_rows[0:HEADS, :]).then_inc(max_placed, 16)
                                    sp.dma_start(stair_prev_r[P - 1:P, :, :], max_rows[HEADS:, :]).then_inc(max_placed, 16)

                                scheduled(sp, one_block)

                            @block.tensor
                            def _(pe):
                                def queries_keys(f, par):
                                    pe.wait_ge(x_ready, f + 1)
                                    wait(pe, qs_max, GROUPS * (f - 1) + 1)
                                    dst = pair(3)
                                    for which, w in ((0, wq_s), (1, wk_s)):
                                        for g in range(GROUPS):
                                            for k in range(HALVES):
                                                for i, (part, x_part) in enumerate(PASSES):
                                                    m = nc.tensor.matmul(dst[:, which, g * P:(g + 1) * P],
                                                                         w[part][:, k, g * P:(g + 1) * P],
                                                                         x_part[:, par % 2, k, :],
                                                                         start=(k == 0 and i == 0),
                                                                         stop=(k == HALVES - 1 and i == 2))
                                    m.then_inc(qk_product, 1)

                                def values(f, par):
                                    wait(pe, f_ready, 2 * GROUPS * (f - 1) + 2)
                                    dst = pair(8)
                                    for k in range(HALVES):
                                        for i, (part, x_part) in enumerate(PASSES):
                                            ends = dict(start=(k == 0 and i == 0), stop=(k == HALVES - 1 and i == 2))
                                            nc.tensor.matmul(dst[:, 0, :], x_part[:, par % 2, k, :], w_vq[part][:, k, :],
                                                             **ends)
                                            m = nc.tensor.matmul(dst[:, 1, 0:HEADS * FEAT], x_part[:, par % 2, k, :],
                                                                 w_qf[part][:, k, :], **ends)
                                    m.then_inc(vq_product, 1)

                                def turn_features(f):
                                    pe.wait_ge(qf_pad_ready, f + 1)
                                    pe.wait_ge(kf32_ready, f + 1)
                                    wait(pe, max_rows_ready, f)
                                    wait(pe, inc_ready, f)
                                    dst = pair(13)
                                    for g in range(GROUPS):
                                        nc.tensor.transpose(dst[:, 0, g * P:(g + 1) * P],
                                                            flat(qf_pad[:, g * PER_G:(g + 1) * PER_G, :]), ident[:, :])
                                    for g in range(GROUPS):
                                        m = nc.tensor.transpose(dst[:, 1, g * P:(g + 1) * P], kf32[:, g, :], ident[:, :])
                                    m.then_inc(turned, 1)

                                def query_scores(n, par, g):
                                    item = g if g < 3 else 4
                                    if g == 0:
                                        pe.wait_ge(q_bd_ready, 2 * n + 2)
                                        pe.wait_ge(k_mix_ready, n + 1)
                                        if isinstance(n, int) and n == 0:
                                            pe.wait_ge(qf_ready, 1)
                                        wait(pe, p_ready, GROUPS * (n - 1) + 2)
                                    if g == 1:
                                        if isinstance(n, int) and n == 0:
                                            pe.wait_ge(kf_tok_ready, 1)
                                        wait(pe, p_ready, GROUPS * (n - 1) + 3)
                                    if g == 2:
                                        wait(pe, p_ready, GROUPS * n)
                                    if g == 3:
                                        pe.wait_ge(qs_max, GROUPS * n + 2)
                                    dst = pair(item)
                                    order, keys = key_pair(par)
                                    for bank in range(2):
                                        nc.tensor.matmul(dst[:, bank, :], ident16[:, :],
                                                         mask_q[:, order, :, :].rearrange("p s k -> p (s k)").unsqueeze(1)
                                                         .broadcast_to([P, 2, 2 * P]),
                                                         start=True, stop=False)
                                        for h in range(2):
                                            m = nc.tensor.matmul(dst[:, bank, h * 2 * P:(h + 1) * 2 * P],
                                                                 q_bd[:, 0, par % 2, g, 2 * bank + h, :],
                                                                 k_mix[:, g, keys, :], start=False, stop=(h == 1))
                                    m.then_inc(qs_product, 1)

                                def maxima_state(n, par):
                                    pe.wait_ge(f_ready, 2 * GROUPS * n + 4)
                                    pe.wait_ge(penal_ready, n + 1)
                                    dst = pair(10)
                                    nc.tensor.transpose(dst[:, 1, :].bitcast(BF16)[0:2 * HEADS, 0:P],
                                                        neg_max[:, :, :].rearrange("p a h -> p (a h)"), ident16[:, :])\
                                        .then_inc(max_turned, 1)
                                    if isinstance(n, int) and n == 0:
                                        pe.wait_ge(cleared, 3)
                                    before = (par - 1) % RING
                                    for g in range(GROUPS):
                                        m = nc.tensor.matmul(dst[:, 0, g * P:(g + 1) * P],
                                                             kf_tok[:, before % 2, g * P:(g + 1) * P],
                                                             flat(v_ext[:, before, g * PER_G:(g + 1) * PER_G, :]),
                                                             start=True, stop=True)
                                    m.then_inc(inc_product, 1)

                                def feature_scores(n, par, g):
                                    item = FEATURE_ITEMS[g]
                                    if g == 0:
                                        pe.wait_ge(qf_bd_ready, 2 * n + 2)
                                        pe.wait_ge(kf_low_ready, n + 1)
                                        pe.wait_ge(qs_max, GROUPS * n + 3)
                                    if g == 1:
                                        pe.wait_ge(qs_max, GROUPS * (n + 1))
                                    if g == 2:
                                        wait(pe, ctx_ready, n)
                                        if isinstance(n, int) and n == 0:
                                            pe.wait_ge(k32_ready, 2)
                                    if g == 3:
                                        pe.wait_ge(f_ready, 2 * GROUPS * n + 6)
                                    dst = pair(item)
                                    for side in range(2):
                                        at = (par - side) % RING
                                        parts = ((kf_high, 0), (kf_high, 1), (kf_low, 0))
                                        for i, (kf, part) in enumerate(parts):
                                            m = nc.tensor.matmul(dst[:, side, :], kf[:, at, g, :],
                                                                 flat(qf_bd[:, part, 0, g, :, :]),
                                                                 start=(i == 0), stop=(i == 2))
                                        m.then_inc(f_product, 1)

                                def state_part(n, par):
                                    wait(pe, sums_ready, 2 * n)
                                    wait(pe, state_ready, n)
                                    if isinstance(n, int) and n == 0:
                                        pe.wait_ge(cleared, 3)
                                    for g in range(GROUPS):
                                        m = nc.tensor.matmul(ps_global[:, g * P:(g + 1) * P], state[:, g, :],
                                                             qf32[:, par % 2, g, :], start=(g == 0), stop=False,
                                                             skip_group_check=True)
                                    m.then_inc(state_read, 1)

                                def weighted(n, par, g, bank, weights, ready, done, unit, first):
                                    pe.wait_ge(ready, unit * (GROUPS * n + g + 1))
                                    if g == 0:
                                        pe.wait_ge(v_ready, n + 1)
                                    for side in range(2):
                                        at = (par - side) % RING
                                        for h in range(PER_G):
                                            m = nc.tensor.matmul(bank[h * STRIP:(h + 1) * STRIP, g * P:(g + 1) * P],
                                                                 v_ext[:, at, g * PER_G + h, :], weights[:, g % 2, side, h, :],
                                                                 start=(first and side == 0), stop=(side == 1),
                                                                 skip_group_check=True)
                                    m.then_inc(done, 1)

                                def weighted_features(n, par, g):
                                    weighted(n, par, g, ps_global, feats, f_ready, global_done, 2, False)

                                def weighted_probs(n, par, g):
                                    weighted(n, par, g, ps_local, probs, p_ready, local_done, 1, True)

                                def key_scores(n, par, g):
                                    item = 14 + g
                                    if g == 0:
                                        pe.wait_ge(max_placed, 32 * (n + 1))
                                        wait(pe, y_ready, n)
                                        if isinstance(n, int) and n == 0:
                                            pe.wait_ge(qf_ready, 2)
                                    if g == 1:
                                        pe.wait_ge(f_ready, 2 * GROUPS * (n + 1))
                                    if g == 2:
                                        pe.wait_ge(kf_tok_ready, n + 2)
                                    if g == 3:
                                        pe.wait_ge(p_ready, GROUPS * n + 1)
                                    dst = pair(item)
                                    for side, (left, right) in enumerate(((stair_own_l, stair_own_r),
                                                                          (stair_prev_l, stair_prev_r))):
                                        at = (par - side) % RING
                                        nc.tensor.matmul(dst[:, side, :], left[:, :], flat(right[:, g * PER_G:(g + 1) * PER_G, :]),
                                                         start=True, stop=False)
                                        for part in range(2):
                                            m = nc.tensor.matmul(dst[:, side, :], k_mix[:, g, at, :],
                                                                 flat(q_bd[:, part, par % 2, g, :, :]), start=False,
                                                                 stop=(part == 1))
                                    m.then_inc(ks_product, 1)

                                def turn_sums(n):
                                    pe.wait_ge(sums_ready, 2 * n + 2)
                                    pe.wait_ge(k32_ready, n + 3)
                                    dst = pair(6)
                                    for which in range(2):
                                        for g in range(GROUPS):
                                            m = nc.tensor.transpose(dst[:, which, g * P:(g + 1) * P],
                                                                    sums[:, which, g * P:(g + 1) * P], ident[:, :])
                                    m.then_inc(sums_turned, 1)

                                def turn_context(n, last=False):
                                    pe.wait_ge(ctx_ready, n + 1)
                                    if not last:
                                        pe.wait_ge(qf_ready, n + 3)
                                    dst = pair(11)
                                    for k in range(HALVES):
                                        m = nc.tensor.transpose(dst[:, 0, k * P:(k + 1) * P], ctx[:, k * P:(k + 1) * P],
                                                                ident[:, :])
                                    m.then_inc(ctx_turned, 1)

                                def output_product(n):
                                    pe.wait_ge(ctx_ch_ready, n + 1)
                                    dst = pair(11)
                                    for k in range(HALVES):
                                        m = nc.tensor.matmul(dst[:, 1, 0:DM], ctx_ch[:, k, :], w_o[:, k, :],
                                                             start=(k == 0), stop=(k == HALVES - 1))
                                    m.then_inc(y_product, 1)

                                queries_keys(0, 0)
                                values(0, 0)
                                turn_features(0)

                                def one_block(n, par):
                                    tail = not (isinstance(n, int) and n == 0)
                                    nxt = (par + 1) % RING
                                    query_scores(n, par, 0)
                                    query_scores(n, par, 1)
                                    query_scores(n, par, 2)
                                    queries_keys(n + 1, nxt)
                                    state_part(n, par)
                                    query_scores(n, par, 3)
                                    feature_scores(n, par, 0)
                                    if tail:
                                        turn_sums(n - 1)
                                    feature_scores(n, par, 1)
                                    values(n + 1, nxt)
                                    weighted_features(n, par, 0)
                                    feature_scores(n, par, 2)
                                    maxima_state(n, par)
                                    weighted_features(n, par, 1)
                                    if tail:
                                        turn_context(n - 1)
                                    feature_scores(n, par, 3)
                                    if tail:
                                        output_product(n - 1)
                                    weighted_features(n, par, 2)
                                    turn_features(n + 1)
                                    key_scores(n, par, 0)
                                    key_scores(n, par, 1)
                                    weighted_probs(n, par, 0)
                                    key_scores(n, par, 2)
                                    weighted_probs(n, par, 1)
                                    key_scores(n, par, 3)
                                    weighted_features(n, par, 3)
                                    weighted_probs(n, par, 2)
                                    weighted_probs(n, par, 3)

                                scheduled(pe, one_block)
                                pe.wait_ge(p_ready, GROUPS * NBLK)
                                pe.wait_ge(sums_ready, 2 * NBLK)
                                dst = pair(6)
                                for which in range(2):
                                    for g in range(GROUPS):
                                        m = nc.tensor.transpose(dst[:, which, g * P:(g + 1) * P],
                                                                sums[:, which, g * P:(g + 1) * P], ident[:, :])
                                m.then_inc(sums_turned, 1)
                                turn_context(NBLK - 1, last=True)
                                output_product(NBLK - 1)

                            @block.scalar
                            def _(act):
                                def high_x(f, par):
                                    wait(act, vq_product, f - 1)
                                    nc.scalar.activation(x_high[:, par % 2, :, :], xn_ch[:, :, ds(f * P, P)], ACT.Copy)\
                                        .then_inc(x_high_ready, 1)

                                def load_logs(f):
                                    wait(act, kf32_ready, f)
                                    act.dma_start(log_blk[:, :, :],
                                                  log_k[ds(f, 1), :, :, :].rearrange("a p g q -> (a p) g q"))\
                                        .then_inc(log_loaded, 16)

                                def key_exponentials(f):
                                    act.wait_ge(log_loaded, 16 * (f + 1))
                                    for g in range(GROUPS):
                                        a = nc.scalar.activation(log_blk[:, g, :], log_blk[:, g, :], ACT.Exp,
                                                                 bias=neg_kmax[:, ds(f, 1), g:g + 1].rearrange("p a b -> p (a b)"))
                                    a.then_inc(kf_exp_ready, 1)
                                    act.wait_ge(kf_exp_ready, f + 1)
                                    if isinstance(f, int) and f == 0:
                                        act.wait_ge(cleared, 1)
                                    wait(act, kf_low_ready, f)
                                    wait(act, turned, f)
                                    nc.scalar.activation(kf32[:, :, :], log_blk[:, :, :], ACT.Identity,
                                                         bias=scaled_eps[:, 0:1], scale=FSCALE).then_inc(kf32_ready, 1)

                                def splits(f, par):
                                    act.wait_ge(q32_ready, f + 1)
                                    wait(act, q_bd_ready, 2 * f)
                                    wait(act, q_low_ready, f)
                                    nc.scalar.activation(q_high[:, :, :], q32[:, :, :], ACT.Copy).then_inc(q_high_ready, 1)
                                    act.wait_ge(k32_ready, f + 1)
                                    wait(act, k_mix_ready, f)
                                    nc.scalar.activation(k_lowhigh[:, :, :], k32[:, :, :], ACT.Copy, scale=low_rows[:, 0:1])\
                                        .then_inc(k_lowhigh_ready, 1)
                                    act.wait_ge(kf32_ready, f + 1)
                                    wait(act, f_product, 2 * GROUPS * (f - 2))
                                    nc.scalar.activation(kf_high[:, par, :, :], kf32[:, :, :], ACT.Copy)\
                                        .then_inc(kf_high_ready, 1)

                                def query_squares(f):
                                    act.wait_ge(q_tok_ready, f + 1)
                                    nc.scalar.activation(q_tok[:, :], q_tok[:, :], ACT.Square).then_inc(q_sq_ready, 1)

                                def feature_exponentials(f):
                                    act.wait_ge(qf_shifted, f + 1)
                                    nc.scalar.activation(qf_tok[:, :, :], qf_tok[:, :, :], ACT.Exp).then_inc(qf_exp_ready, 1)

                                def turned_features(f, par):
                                    act.wait_ge(turned, f + 1)
                                    wait(act, state_read, f - 1)
                                    dst = pair(13)
                                    nc.scalar.activation(flat(qf32[:, par % 2, :, :]), dst[:, 0, :], ACT.Copy)\
                                        .then_inc(qf32_ready, 1)
                                    nc.scalar.activation(kf_tok[:, par % 2, :], dst[:, 1, :], ACT.Copy).then_inc(kf_tok_ready, 1)
                                    act.wait_ge(qf32_ready, f + 1)
                                    wait(act, qf_bd_ready, 2 * f)
                                    wait(act, qf_low_ready, f)
                                    nc.scalar.activation(qf_high[:, :, :], qf32[:, par % 2, :, :], ACT.Copy)\
                                        .then_inc(qf_high_ready, 1)

                                def context_turned(n):
                                    act.wait_ge(ctx_turned, n + 1)
                                    wait(act, y_product, n)
                                    nc.scalar.activation(flat(ctx_ch[:, :, :]), pair(11)[:, 0, 0:DM], ACT.Copy)\
                                        .then_inc(ctx_ch_ready, 1)

                                high_x(0, 0)
                                load_logs(0)
                                key_exponentials(0)
                                act.wait_ge(cleared, 3)
                                act.wait_ge(cleared_dve, 1)
                                splits(0, 0)
                                query_squares(0)
                                feature_exponentials(0)
                                load_logs(1)
                                turned_features(0, 0)

                                def one_block(n, par):
                                    tail = not (isinstance(n, int) and n == 0)
                                    nxt = (par + 1) % RING
                                    high_x(n + 1, nxt)
                                    key_exponentials(n + 1)
                                    splits(n + 1, nxt)
                                    load_logs(n + 2)
                                    act.wait_ge(lift_arg_ready, n + 1)
                                    nc.scalar.activation(lift_exp[:, par % 2, :], lift_arg[:, :], ACT.Exp)\
                                        .then_inc(lift_exp_ready, 1)
                                    query_squares(n + 1)
                                    act.wait_ge(max_turned, n + 1)
                                    wait(act, max_placed, 32 * n)
                                    nc.scalar.activation(max_rows[:, :], pair(10)[:, 1, :].bitcast(BF16)[0:2 * HEADS, 0:P],
                                                         ACT.Copy).then_inc(max_rows_ready, 1)
                                    if tail:
                                        context_turned(n - 1)
                                    feature_exponentials(n + 1)
                                    turned_features(n + 1, nxt)
                                    for g in range(GROUPS):
                                        act.wait_ge(ks_product, GROUPS * n + g + 1)
                                        wait(act, local_done, GROUPS * n + g - 1)
                                        nc.scalar.activation(probs[:, g % 2, :, :, :].rearrange("p s h q -> p (s h q)"),
                                                             pair(14 + g)[:, :, :].rearrange("p s c -> p (s c)"), ACT.Exp)\
                                            .then_inc(p_ready, 1)
                                    wait(act, sums_turned, n)
                                    act.wait_ge(global_done, GROUPS * (n + 1))
                                    nc.scalar.activation(sums[:, 1, :], ps_global[:, :], ACT.Copy).then_inc(sums_ready, 1)
                                    act.wait_ge(local_done, GROUPS * (n + 1))
                                    nc.scalar.activation(sums[:, 0, :], ps_local[:, :], ACT.Copy).then_inc(sums_ready, 1)

                                scheduled(act, one_block)
                                context_turned(NBLK - 1)
                                act.wait_ge(log_loaded, 16 * (NBLK + 2))

                            @block.vector
                            def _(dve):
                                def queries_keys(f):
                                    src = pair(3)
                                    dve.wait_ge(qk_product, f + 1)
                                    wait(dve, q_low_ready, f)
                                    wait(dve, k_mix_ready, f)
                                    for which, bias, dst, ready in ((0, bq_s, q32, q32_ready), (1, bk_s, k32, k32_ready)):
                                        nc.vector.scalar_tensor_tensor(
                                            dst[:, :, :], src[:, which, :].rearrange("p (g q) -> p g q", q=P), 1.0 / WSCALE,
                                            bias[:, :].unsqueeze(2).broadcast_to([P, GROUPS, P]), ALU.mult, ALU.add)\
                                            .then_inc(ready, 1)

                                def values(f, par):
                                    src = pair(8)
                                    dve.wait_ge(vq_product, f + 1)
                                    wait(dve, local_done, GROUPS * (f - 2))
                                    nc.vector.scalar_tensor_tensor(v_ext[:, par, :, 0:DH],
                                                                   src[:, 0, 0:DM].rearrange("p (h d) -> p h d", d=DH), 1.0 / WSCALE,
                                                                   b_vq[:, 0:DM].rearrange("p (h d) -> p h d", d=DH),
                                                                   ALU.mult, ALU.add)\
                                        .then_inc(v_ready, 1)
                                    wait(dve, q_norm_ready, f)
                                    nc.vector.scalar_tensor_tensor(q_tok[:, :], src[:, 0, DM:], 1.0 / WSCALE, b_vq[:, DM:],
                                                                   ALU.mult, ALU.add)\
                                        .then_inc(q_tok_ready, 1)
                                    wait(dve, qf_pad_ready, f)
                                    nc.vector.scalar_tensor_tensor(
                                        qf_tok[:, :, :], src[:, 1, 0:HEADS * FEAT].rearrange("p (h m) -> p h m", m=FEAT),
                                        1.0 / WSCALE, b_qf[:, :].rearrange("p (h m) -> p h m", m=FEAT), ALU.mult, ALU.add)\
                                        .then_inc(qf_ready, 1)

                                def feature_maxima(f, par):
                                    dve.wait_ge(qf_ready, f + 1)
                                    nc.vector.tensor_reduce(qf_max[:, :], qf_tok[:, :, :], AX_X, ALU.max).then_inc(qf_max_ready, 1)
                                    dve.wait_ge(q_sq_ready, f + 1)
                                    nc.vector.tensor_reduce(q_norm[:, :], q_tok[:, :].rearrange("p (h d) -> p h d", d=DH), AX_X,
                                                            ALU.add).then_inc(q_norm_ready, 1)
                                    dve.wait_ge(q_norm_ready, f + 1)
                                    dve.wait_ge(qf_max_ready, f + 1)
                                    nc.vector.scalar_tensor_tensor(q_scale[:, :], q_norm[:, :], -SCALE / 2, qf_max[:, :],
                                                                   ALU.mult, ALU.add).then_inc(q_scale_ready, 1)
                                    dve.wait_ge(q_scale_ready, f + 1)
                                    nc.vector.tensor_tensor(g_scale[:, par % 2, :], q_scale[:, :],
                                                            kmax_tok[:, ds(f, 1), :].rearrange("p a h -> p (a h)"), ALU.add)\
                                        .then_inc(g_scale_ready, 1)

                                def place(f, slot, bd, high, low, high_ready, low_ready, placed):
                                    for part, src, ready in ((0, high, high_ready), (1, low, low_ready)):
                                        dve.wait_ge(ready, f + 1)
                                        for r in range(PER_G):
                                            rows = slice(r * STRIP, (r + 1) * STRIP)
                                            c = nc.vector.tensor_copy(bd[rows, part, slot, :, r, :], src[rows, :, :])
                                        c.then_inc(placed, 1)

                                def place_queries(f, par):
                                    wait(dve, ks_product, GROUPS * (f - 1))
                                    place(f, par % 2, q_bd, q_high, q_low, q_high_ready, q_low_ready, q_bd_ready)

                                def place_features(f, par):
                                    wait(dve, f_product, 2 * GROUPS * f)
                                    place(f, 0, qf_bd, qf_high, qf_low, qf_high_ready, qf_low_ready, qf_bd_ready)

                                def pad_features(f):
                                    dve.wait_ge(qf_exp_ready, f + 1)
                                    wait(dve, turned, f)
                                    nc.vector.tensor_scalar(qf_pad[:, :, 0:FEAT], qf_tok[:, :, :], FEATURE_EPS, FSCALE,
                                                            ALU.add, ALU.mult).then_inc(qf_pad_ready, 1)

                                def maximum(n, par, g):
                                    dve.wait_ge(qs_product, GROUPS * n + g + 1)
                                    if g == 0:
                                        wait(dve, row_top_ready, n)
                                    nc.vector.tensor_reduce(
                                        block_max[:, g, :, :],
                                        pair(g if g < 3 else 4)[:, :, :].rearrange("p b (h s k) -> p (b h s) k", h=2, s=2),
                                        AX_X, ALU.max).then_inc(qs_max, 1)

                                def maxima(n, par):
                                    order, _ = key_pair(par)
                                    own, prev = 1 - order, order
                                    bm = block_max[:, :, :, :].rearrange("p g h s -> p (g h) s")
                                    dve.wait_ge(qs_max, GROUPS * (n + 1))
                                    nc.vector.scalar_tensor_tensor(row_top[:, :], bm[:, :, prev], penalty[:, ds(n, 1)],
                                                                   bm[:, :, own], ALU.add, ALU.max).then_inc(row_top_ready, 1)
                                    dve.wait_ge(row_top_ready, n + 1)
                                    wait(dve, max_turned, n)
                                    wait(dve, lift_arg_ready, n)
                                    nc.vector.tensor_scalar(neg_max[:, 0, :], row_top[:, :], -1.0, None, ALU.mult)\
                                        .then_inc(neg_max_ready, 1)
                                    dve.wait_ge(neg_max_ready, n + 1)
                                    nc.vector.tensor_scalar(neg_max[:, 1, :], neg_max[:, 0, :], penalty[:, ds(n, 1)], None,
                                                            ALU.add).then_inc(penal_ready, 1)
                                    dve.wait_ge(g_scale_ready, n + 1)
                                    wait(dve, lift_exp_ready, n)
                                    nc.vector.scalar_tensor_tensor(lift_arg[:, :], neg_max[:, 0, :], -1.0,
                                                                   g_scale[:, par % 2, :], ALU.mult, ALU.subtract)\
                                        .then_inc(lift_arg_ready, 1)

                                def masked_features(n, par, g):
                                    src = pair(FEATURE_ITEMS[g])
                                    for side in range(2):
                                        dve.wait_ge(f_product, 2 * (GROUPS * n + g) + side + 1)
                                        wait(dve, global_done, GROUPS * n + g - 1)
                                        s = src[:, side, :].rearrange("p (h q) -> p h q", q=P)
                                        mask = gmask[:, side:side + 1, :].broadcast_to([P, PER_G, P])
                                        if side == 0:
                                            m = nc.vector.tensor_tensor(feats[:, g % 2, side, :, :], s, mask, ALU.mult)
                                        else:
                                            m = nc.vector.scalar_tensor_tensor(feats[:, g % 2, side, :, :], s,
                                                                               has_prev[:, ds(n, 1)], mask, ALU.mult, ALU.mult)
                                        m.then_inc(f_ready, 1)

                                def new_state(n):
                                    src = pair(10)[:, 0, :]
                                    dve.wait_ge(inc_product, n + 1)
                                    nc.vector.scalar_tensor_tensor(
                                        state_inc[:, :, :], src.rearrange("p (g c) -> p g c", c=P), keep_state[:, ds(n, 1)],
                                        flat(diag_strips[:, :, :]).unsqueeze(1).broadcast_to([P, GROUPS, P]),
                                        ALU.mult, ALU.mult).then_inc(inc_ready, 1)
                                    dve.wait_ge(inc_ready, n + 1)
                                    dve.wait_ge(state_read, n + 1)
                                    nc.vector.scalar_tensor_tensor(state[:, :, :], state[:, :, :], keep_state[:, ds(n, 1)],
                                                                   state_inc[:, :, :], ALU.mult, ALU.add)\
                                        .then_inc(state_ready, 1)

                                def normalise(n, par):
                                    src = pair(6)
                                    local = src[:, 0, :].rearrange("p (h d) -> p h d", d=STRIP)
                                    whole = src[:, 1, :].rearrange("p (h d) -> p h d", d=STRIP)
                                    dve.wait_ge(sums_turned, n + 1)
                                    dve.wait_ge(lift_exp_ready, n + 1)
                                    nc.vector.tensor_tensor(norm_a[:, :], lift_exp[:, par % 2, :], local[:, :, DH], ALU.mult)\
                                        .then_inc(norm_parts, 1)
                                    nc.vector.tensor_scalar(norm_b[:, :], whole[:, :, DH], UNSCALE, 1e-24, ALU.mult, ALU.max)\
                                        .then_inc(norm_parts, 1)
                                    nc.vector.reciprocal(r_local[:, :], local[:, :, DH]).then_inc(r_ready, 1)
                                    dve.wait_ge(norm_parts, 2 * n + 2)
                                    nc.vector.tensor_tensor(norm_c[:, :], norm_a[:, :], norm_b[:, :], ALU.add).then_inc(norm_ready, 1)
                                    dve.wait_ge(r_ready, 2 * n + 1)
                                    nc.vector.tensor_tensor(ctx_a[:, :, :], local[:, :, 0:DH],
                                                            r_local[:, :].unsqueeze(2).broadcast_to([P, HEADS, DH]), ALU.mult)\
                                        .then_inc(ctx_parts, 1)
                                    dve.wait_ge(norm_ready, 2 * n + 1)
                                    nc.vector.reciprocal(norm_r[:, :], norm_c[:, :]).then_inc(norm_ready, 1)
                                    dve.wait_ge(norm_ready, 2 * n + 2)
                                    nc.vector.tensor_scalar(r_global[:, :], norm_r[:, :], UNSCALE, None, ALU.mult)\
                                        .then_inc(r_ready, 1)
                                    dve.wait_ge(r_ready, 2 * n + 2)
                                    wait(dve, ctx_turned, n)
                                    nc.vector.tensor_tensor(ctx[:, :].rearrange("p (h d) -> p h d", d=DH), whole[:, :, 0:DH],
                                                            r_global[:, :].unsqueeze(2).broadcast_to([P, HEADS, DH]), ALU.mult)\
                                        .then_inc(ctx_parts, 1)
                                    dve.wait_ge(ctx_parts, 2 * n + 2)
                                    wait(dve, ctx_turned, n)
                                    nc.vector.tensor_tensor(ctx[:, :], flat(ctx_a[:, :, :]), ctx[:, :], ALU.add)\
                                        .then_inc(ctx_ready, 1)

                                def add_output(n):
                                    dve.wait_ge(y_product, n + 1)
                                    dve.wait_ge(x_biased, n + 1)
                                    x_row = x_tok[:, ds(n, 1), :].rearrange("p a c -> p (a c)")
                                    nc.vector.tensor_tensor(x_row, pair(11)[:, 1, 0:DM], x_row, ALU.add)\
                                        .then_inc(y_ready, 1)

                                for view in (q_bd[:, :, :, :, :, :], k_mix[:, :, RING - 1, :], kf_high[:, RING - 1, :, :],
                                             kf_low[:, RING - 1, :, :]):
                                    last = nc.vector.memset(view, 0.0)
                                last.then_inc(cleared_dve, 1)
                                dve.wait_ge(cleared_dve, 1)
                                dve.wait_ge(cleared, 3)
                                queries_keys(0)
                                values(0, 0)
                                feature_maxima(0, 0)
                                place_queries(0, 0)
                                pad_features(0)
                                dve.wait_ge(cleared, 4)
                                place_features(0, 0)

                                def one_block(n, par):
                                    tail = not (isinstance(n, int) and n == 0)
                                    nxt = (par + 1) % RING
                                    for g in range(3):
                                        maximum(n, par, g)
                                    queries_keys(n + 1)
                                    maximum(n, par, 3)
                                    maxima(n, par)
                                    masked_features(n, par, 0)
                                    if tail:
                                        normalise(n - 1, (par - 1) % RING)
                                    masked_features(n, par, 1)
                                    values(n + 1, nxt)
                                    masked_features(n, par, 2)
                                    feature_maxima(n + 1, nxt)
                                    new_state(n)
                                    pad_features(n + 1)
                                    masked_features(n, par, 3)
                                    if tail:
                                        add_output(n - 1)
                                    place_queries(n + 1, nxt)
                                    place_features(n + 1, nxt)

                                scheduled(dve, one_block)
                                normalise(NBLK - 1, (NBLK - 1) % RING)
                                add_output(NBLK - 1)

                def key_pair(par):
                    return (0, slice(par - 1, par + 1)) if par else (1, slice(0, 4, 3))

                with ExitStack() as prep:
                    proj_bd = sb("proj_bd", [P, HALF_HEADS, FEAT], F32, prep)
                    w_k = sb("w_k", [P, HALVES, DM], F32, prep)
                    bk_col = sb("bk_col", [P, HALVES], F32, prep)
                    with ExitStack() as early:
                        layernorm("ln1", True, twist_sign, attention_weights(early))
                    ffn("ffn1", False)
                    layernorm("ln2", False, ones_col)
                    key_features(prep)
                attention_blocks(scope)

        up_to_attention()
        layernorm("ln3", False, twist_sign)
        ffn("ffn2", True)


_INS = ["L0_attn_x", "L0_attn_Wqkv_w", "L0_attn_Wqkv_b", "L0_attn_proj", "L0_attn_out_w", "L0_attn_out_b",
        "L0_ffn_cn_w1", "L0_ffn_cn_b1", "L0_ffn_cn_w2", "L0_ffn_cn_b2", "L0_ffn_cn_w3", "L0_ffn_cn_b3",
        "L0_ffn_cn_w4", "L0_ffn_cn_b4", "L0_ffn_gc_w1", "L0_ffn_gc_b1", "L0_ffn_gc_w2", "L0_ffn_gc_b2",
        "L0_ffn_gc_w3", "L0_ffn_gc_b3", "L0_ffn_adaptive_range"]


def kernel(**inputs):
    import numpy as _np
    import concourse.bacc as _bacc
    from concourse.bass_utils import run_bass_kernel_spmd as _run

    nc = _bacc.Bacc("TRN2", target_bir_lowering=False, num_devices=1)
    arrays, args = {}, []
    for name in _INS:
        a = _np.ascontiguousarray(inputs[name])
        arrays[name + "_dram"] = a
        args.append(nc.dram_tensor(name + "_dram", a.shape, mybir.dt.from_np(a.dtype),
                                   kind="ExternalInput").ap())
    x = inputs["L0_attn_x"]
    out = nc.dram_tensor("out_dram", tuple(x.shape), F32, kind="ExternalOutput").ap()
    macaron_kernel(nc, *args, out)
    r = _run(nc, [arrays], core_ids=[0])
    return r.results[0]["out_dram"]
```

```python
from contextlib import ExitStack
from math import sqrt

import concourse.bass as bass
from concourse import mybir

ds = bass.ds
ALU = mybir.AluOpType
ACT = mybir.ActivationFunctionType
F32 = mybir.dt.float32
F16 = mybir.dt.float16
BF16 = mybir.dt.bfloat16
AX_X = mybir.AxisListType.X

P = 128
LN_EPS = 1e-5
FEATURE_EPS = 1e-4
MASKED = -30000.0


def macaron_kernel(nc, x_in, wqkv, bqkv, proj, wout, bout, cn_w1, cn_b1, cn_w2, cn_b2, cn_w3, cn_b3,
                   cn_w4, cn_b4, gc_w1, gc_b1, gc_w2, gc_b2, gc_w3, gc_b3, adaptive_range, out):
    BATCH, SEQ, DM = x_in.shape
    NBLK = BATCH * SEQ // P
    BLK_B = SEQ // P
    HALVES = DM // P
    TILE = 512
    TILES_B = SEQ // TILE
    BLK_T = TILE // P
    CYCLES = 3
    D1, D2, D3 = cn_w1.shape[1], cn_w2.shape[1], cn_w3.shape[1]
    MCH = D1 // P
    assert HALVES == 2 and DM == 256 and D2 == P and D3 == 64 and SEQ % TILE == 0

    x_blocks = x_in.rearrange("b (n p) c -> p (b n) c", p=P)
    out_blocks = out.rearrange("b (n p) c -> p (b n) c", p=P)

    with ExitStack() as keep:
        def sb(name, shape, dt, scope=keep):
            return scope.enter_context(nc.sbuf_tensor(name, shape, dt))

        def psum(name, shape, scope, dt=F32):
            return scope.enter_context(nc.psum_tensor(name, shape, dt))

        def sem(name, scope):
            return scope.enter_context(nc.semaphore(name))

        x_tok = sb("x_tok", [P, NBLK, DM], F32)
        xn_ch = sb("xn_ch", [P, HALVES, (NBLK + 1) * P], F32)
        ident = sb("ident", [P, P], F32)
        twist_sign = sb("twist_sign", [P, 1], F32)
        ones_col = sb("ones_col", [P, 1], F32)
        eps_col = sb("eps_col", [P, 1], F32)
        stats = sb("stats", [P, NBLK, 6], F32)

        w1 = sb("w1", [P, HALVES, D1], F32)
        w2 = sb("w2", [P, MCH, D2], F32)
        w3 = sb("w3", [P, D3], F32)
        w4 = sb("w4", [D3, 1], F32)
        w4_rep = sb("w4_rep", [D3, P], F32)
        b1 = sb("b1", [P, MCH], F32)
        b2 = sb("b2", [P, 1], F32)
        b3 = sb("b3", [D3, 1], F32)
        b4_half = sb("b4_half", [P, 1], F32)
        g1 = sb("g1", [P, HALVES, P], F32)
        g2 = sb("g2", [P, D3], F32)
        g3 = sb("g3", [D3, 1], F32)
        g3_rep = sb("g3_rep", [D3, P], F32)
        gb1 = sb("gb1", [P, 1], F32)
        gb2 = sb("gb2", [D3, 1], F32)
        gb3_half = sb("gb3_half", [P, 1], F32)
        rng = sb("rng", [P, 1], F32)
        gain = sb("gain", [P, 1], F32)

        G = 4
        STEPS = NBLK // G
        x_loaded = [sem(f"x_loaded{i}", keep) for i in range(STEPS)]
        loaded = sem("loaded", keep)
        with ExitStack() as scope:
            constants = sem("constants", scope)
            col = lambda v: v.rearrange("(p a) -> p a", a=1)
            spread = lambda v, n: v.rearrange("(a p) -> a p", a=1).broadcast_to([n, 1])
            with nc.Block() as block:
                loads = [
                    (w1[:, :, :], cn_w1.rearrange("(k p) n -> p k n", p=P)),
                    (w2[:, :, :], cn_w2.rearrange("(k p) n -> p k n", p=P)),
                    (w3[:, :], cn_w3),
                    (w4[:, :], cn_w4),
                    (b1[:, :], cn_b1.rearrange("(k p) -> p k", p=P)),
                    (b2[:, :], col(cn_b2)),
                    (b3[:, :], col(cn_b3)),
                    (b4_half[:, :], spread(cn_b4, P)),
                    (g1[:, :, :], gc_w1.rearrange("(k p) n -> p k n", p=P)),
                    (g2[:, :], gc_w2),
                    (g3[:, :], gc_w3),
                    (gb1[:, :], col(gc_b1)),
                    (gb2[:, :], col(gc_b2)),
                    (gb3_half[:, :], spread(gc_b3, P)),
                    (rng[:, :], spread(adaptive_range, P)),
                ]

                @block.sync
                def _(sp):
                    for i in range(STEPS):
                        sp.dma_start(x_tok[:, i * G:(i + 1) * G, :],
                                     x_blocks[:, i * G:(i + 1) * G, :]).then_inc(x_loaded[i], 16)

                @block.gpsimd
                def _(pool):
                    nc.gpsimd.memset(ident[:, :], 0.0).then_inc(constants, 1)
                    nc.gpsimd.memset(twist_sign[:, :], 1.0).then_inc(constants, 1)
                    nc.gpsimd.memset(ones_col[:, :], 1.0)
                    nc.gpsimd.memset(eps_col[:, :], LN_EPS)
                    nc.gpsimd.memset(xn_ch[:, :, NBLK * P:], 0.0)
                    pool.wait_ge(constants, 2)
                    nc.gpsimd.affine_select(out=ident[:, :], in_=ident[:, :], compare_op=ALU.not_equal,
                                            fill=1.0, base=0, pattern=[[-1, P]], channel_multiplier=1)
                    nc.gpsimd.affine_select(out=twist_sign[:, :], in_=twist_sign[:, :], compare_op=ALU.is_gt,
                                            fill=-1.0, base=P // 2, pattern=[[0, 1]],
                                            channel_multiplier=-1).then_inc(constants, 1)

        def ffn_weights(dve):
            dve.wait_ge(loaded, 16 * len(loads))
            nc.vector.tensor_scalar(w1[:, 1, :], w1[:, 1, :], twist_sign[:, 0:1], None, ALU.mult)
            nc.vector.tensor_scalar(g1[:, 1, :], g1[:, 1, :], twist_sign[:, 0:1], None, ALU.mult)
            nc.vector.tensor_copy(w4_rep[:, :], w4[:, 0:1].broadcast_to([D3, P]))
            nc.vector.tensor_copy(g3_rep[:, :], g3[:, 0:1].broadcast_to([D3, P]))
            nc.vector.tensor_scalar(b4_half[:, :], b4_half[:, :], 0.5, None, ALU.mult)
            nc.vector.tensor_scalar(gb3_half[:, :], gb3_half[:, :], 0.5, None, ALU.mult)
            return nc.vector.tensor_scalar(gain[:, :], rng[:, :], 0.3, None, ALU.mult)

        def layernorm(name, weights):
            with ExitStack() as scope:
                xn_tok = sb(name + "_xn_tok", [P, 2, G, DM], F32, scope)
                moments = sb(name + "_moments", [P, NBLK, 2], F32, scope)
                std = sb(name + "_std", [P, NBLK], F32, scope)
                rstd = sb(name + "_rstd", [P, NBLK], F32, scope)
                turned = [psum(f"{name}_turned{i}", [P, HALVES, 2, P], scope) for i in range(4)]
                weights["banks"] += [psum(f"{name}_weights{i}", [P, 512], scope) for i in range(4)]
                moments_done = sem(name + "_moments_done", scope)
                std_done = sem(name + "_std_done", scope)
                rstd_done = sem(name + "_rstd_done", scope)
                xn_ready = sem(name + "_xn_ready", scope)
                turned_ready = sem(name + "_turned_ready", scope)
                turned_used = sem(name + "_turned_used", scope)
                with nc.Block() as block:
                    @block.vector
                    def _(dve):
                        def rows(blk):
                            return x_tok[:, ds(blk, 1), :].rearrange("p a c -> p (a c)")

                        def normalise(i, par):
                            if not isinstance(i, int) or i >= 2:
                                dve.wait_ge(turned_ready, (i - 1) * 2)
                            for j in range(G):
                                blk = i * G + j
                                s = nc.vector.tensor_scalar(xn_tok[:, par, j, :], rows(blk),
                                                            moments[:, ds(blk, 1), 0:1].rearrange("p a c -> p (a c)"),
                                                            rstd[:, ds(blk, 1)], ALU.subtract, ALU.mult)
                            s.then_inc(xn_ready, 1)

                        for blk in range(NBLK):
                            nc.vector.bn_aggr(moments[:, blk, :], stats[:, blk, :]).then_inc(moments_done, 1)
                        dve.wait_ge(std_done, 1)
                        nc.vector.reciprocal(rstd[:, :], std[:, :]).then_inc(rstd_done, 1)
                        dve.wait_ge(rstd_done, 1)
                        normalise(0, 0)
                        normalise(1, 1)
                        with dve.Fori(1, STEPS // 2) as k:
                            for par in range(2):
                                normalise(k * 2 + par, par)
                        weights["vector"](dve)

                    @block.tensor
                    def _(pe):
                        def step(i, par, peeled):
                            pe.wait_ge(xn_ready, i + 1)
                            for pair in range(2):
                                bank = turned[2 * par + pair]
                                if not peeled:
                                    pe.wait_ge(turned_used, 2 * (i - 2) + pair + 1)
                                for j in range(2):
                                    for h in range(HALVES):
                                        t = nc.tensor.transpose(bank[:, h, j, :],
                                                                xn_tok[:, par, 2 * pair + j, h * P:(h + 1) * P],
                                                                ident[:, :])
                                t.then_inc(turned_ready, 1)

                        step(0, 0, True)
                        step(1, 1, True)
                        with pe.Fori(1, STEPS // 2) as k:
                            for par in range(2):
                                step(k * 2 + par, par, False)
                        weights["tensor"](pe)

                    @block.scalar
                    def _(act):
                        def keep_turned(i, par):
                            for pair in range(2):
                                act.wait_ge(turned_ready, i * 2 + pair + 1)
                                nc.scalar.activation(
                                    xn_ch[:, :, ds((i * G + 2 * pair) * P, 2 * P)],
                                    turned[2 * par + pair][:, :, :, :].rearrange("p h j c -> p h (j c)"),
                                    ACT.Copy).then_inc(turned_used, 1)

                        act.wait_ge(moments_done, NBLK)
                        nc.scalar.activation(std[:, :], moments[:, :, 1], ACT.Sqrt,
                                             bias=eps_col[:, 0:1]).then_inc(std_done, 1)
                        with act.Fori(0, STEPS // 2) as k:
                            for par in range(2):
                                keep_turned(k * 2 + par, par)
                        weights["scalar"](act)

        def ffn(name, first, last, weights=None):
            JOBS_B = CYCLES * TILES_B
            JOBS = BATCH * JOBS_B
            TILES = BATCH * TILES_B
            jobs = [(b, c, s) for b in range(BATCH) for c in range(CYCLES) for s in range(TILES_B)]

            units_before = {s: [(s, 0)] for s in range(TILES_B)}
            units_behind = {s: [(s, 1)] for s in range(TILES_B)}
            for b in range(1, BATCH):
                for s in range(TILES_B):
                    units_behind[b * JOBS_B - TILES_B + s] = [(b * TILES_B + s, 0)]
                    units_behind[b * JOBS_B + s] = [(b * TILES_B + s, 1)]
            unit_order = [u for n in range(JOBS) for u in units_before.get(n, []) + units_behind.get(n, [])]

            moment_parts = [(0, 2 * BLK_T), (2 * BLK_T, NBLK)] if first else [(0, NBLK)]
            norm_first = [0, 1]
            norm_between = {n: [2 * n + 2] for n in range(TILES // 2 - 1)}
            norm_behind = {n: [2 * n + 3] for n in range(TILES // 2 - 1)}
            GLOBAL_STEP = 3
            MEAN_STEPS = (2 if first else 1) + BATCH + 1
            assert TILES // 2 - 1 <= GLOBAL_STEP

            def kept_count(tile, which):
                return MCH * (unit_order.index((tile, which)) + 1)

            def final_count(j):
                b, c, s = jobs[j]
                return 2 * (b * TILES_B + (s if c == CYCLES - 1 else 0))

            def update_count(j):
                b, c, s = jobs[j]
                return (b * (CYCLES - 1) + c) * TILES_B + s + 1

            with ExitStack() as scope:
                w1_neg = sb(name + "_w1_neg", [P, D1], F32, scope)
                yz = sb(name + "_yz", [P, TILES_B, 2, MCH, TILE], F32, scope)
                y_second = sb(name + "_y_second", [P, TILES_B, MCH, TILE], F32, scope)
                c_first = sb(name + "_c_first", [P, TILES_B, TILE], F32, scope)
                c_y = sb(name + "_c_y", [P, MCH, TILE], F32, scope)
                c_state_first = sb(name + "_c_state_first", [P, HALVES, TILE], F32, scope)
                c_times = sb(name + "_c_times", [P, 2, TILE], F32, scope)
                assert MCH == HALVES == 2
                act1 = sb(name + "_act1", [P, MCH, TILE], F32, scope)
                act2 = sb(name + "_act2", [P, TILE], F32, scope)
                act3 = sb(name + "_act3", [D3, TILE], F32, scope)
                gate = sb(name + "_gate", [P, 2, TILE], F32, scope)
                coupling = sb(name + "_coupling", [P, TILE], F32, scope)
                final = sb(name + "_final", [P, HALVES, TILE], F32, scope)
                mean = sb(name + "_mean", [P, HALVES, BATCH], F32, scope)
                gact1 = sb(name + "_gact1", [P, BATCH], F32, scope)
                gact2 = sb(name + "_gact2", [D3, BATCH], F32, scope)
                gtanh = sb(name + "_gtanh", [P, BATCH], F32, scope)
                base = sb(name + "_base", [P, BATCH], F32, scope)
                block_sums = sb(name + "_block_sums", [P, HALVES, NBLK], F32, scope)
                moments = sb(name + "_moments", [P, NBLK, 2], F32, scope)
                std = sb(name + "_std", [P, NBLK], F32, scope)
                rstd = sb(name + "_rstd", [P, NBLK], F32, scope)
                ps1 = psum(name + "_ps1", [P, MCH, TILE], scope)
                ps2 = psum(name + "_ps2", [P, TILE], scope)
                ps3 = psum(name + "_ps3", [P, TILE], scope)
                ps4 = psum(name + "_ps4", [P, TILE], scope)
                ps_out = psum(name + "_ps_out", [P, 2, 2, DM], scope)

                stats_done = sem(name + "_stats_done", scope)
                std_done = sem(name + "_std_done", scope)
                xn_ready = sem(name + "_xn_ready", scope)
                xn_turned = sem(name + "_xn_turned", scope)
                xn_kept = sem(name + "_xn_kept", scope)
                g_prod = sem(name + "_g_prod", scope)
                g_act = sem(name + "_g_act", scope)
                unit_done = sem(name + "_unit_done", scope)
                unit_kept = sem(name + "_unit_kept", scope)
                l2_done = sem(name + "_l2_done", scope)
                l3_done = sem(name + "_l3_done", scope)
                l4_done = sem(name + "_l4_done", scope)
                gelu1_done = sem(name + "_gelu1_done", scope)
                gelu2_done = sem(name + "_gelu2_done", scope)
                gelu3_done = sem(name + "_gelu3_done", scope)
                gate_done = sem(name + "_gate_done", scope)
                coupling_done = sem(name + "_coupling_done", scope)
                inner = sem(name + "_inner", scope)
                y_done = sem(name + "_y_done", scope)
                z_steps = sem(name + "_z_steps", scope)
                first_state = sem(name + "_first_state", scope)
                second_state = sem(name + "_second_state", scope)
                final_done = sem(name + "_final_done", scope)
                final_turned = sem(name + "_final_turned", scope)
                residual_done = sem(name + "_residual_done", scope)
                stored = sem(name + "_stored", scope) if last else None

                def state(h, tile):
                    return xn_ch[:, h, tile * TILE:(tile + 1) * TILE]

                def xn_tok(tile):
                    return y_second[:, tile % 2, :, :].rearrange("p m (i c) -> p (m i) c", c=DM)

                def both_halves(tile):
                    return xn_ch[:, :, tile * TILE:(tile + 1) * TILE]

                def wide(row):
                    return row.unsqueeze(1).broadcast_to([P, 2, TILE])

                with nc.Block() as block:
                    @block.tensor
                    def _(pe):
                        def turn_normed(tile):
                            pe.wait_ge(xn_ready, tile + 1)
                            for pair in range(2):
                                if tile > 0:
                                    pe.wait_ge(xn_kept, 4 * (tile - 1) + 2 * pair + 2)
                                for j in range(2):
                                    for h in range(HALVES):
                                        m = nc.tensor.transpose(ps_out[:, pair, j, h * P:(h + 1) * P],
                                                                xn_tok(tile)[:, 2 * pair + j, h * P:(h + 1) * P],
                                                                ident[:, :])
                                m.then_inc(xn_turned, 1)

                        def global_layer(layer):
                            if layer == 0:
                                pe.wait_ge(inner, MEAN_STEPS)
                                for h in range(HALVES):
                                    m = nc.tensor.matmul(ps_out[:, 0, 0, 0:BATCH], g1[:, h, :], mean[:, h, :],
                                                         start=(h == 0), stop=(h == HALVES - 1))
                            else:
                                pe.wait_ge(g_act, layer)
                                m = (nc.tensor.matmul(ps_out[0:D3, 1, 0, 0:BATCH], g2[:, :], gact1[:, :], start=True,
                                                      stop=True) if layer == 1 else
                                     nc.tensor.matmul(ps_out[:, 0, 0, 0:BATCH], g3_rep[:, :], gact2[:, :], start=True,
                                                      stop=True))
                            m.then_inc(g_prod, 1)

                        def unit(tile, which):
                            u = unit_order.index((tile, which))
                            terms = ([(w1[:, 0, :], 0), (w1[:, 1, :], 1)] if which == 0
                                     else [(w1[:, 0, :], 1), (w1_neg[:, :], 0)])
                            pe.wait_ge(xn_kept, 4 * (tile + 1))
                            for m_ch in range(MCH):
                                if u > 0:
                                    pe.wait_ge(unit_kept, MCH * (u - 1) + m_ch + 1)
                                for i, (w, h) in enumerate(terms):
                                    m = nc.tensor.matmul(ps1[:, m_ch, :], w[:, m_ch * P:(m_ch + 1) * P],
                                                         state(h, tile), start=(i == 0), stop=(i == 1))
                                m.then_inc(unit_done, 1)

                        for tile in norm_first:
                            turn_normed(tile)
                        if first:
                            pe.wait_ge(loaded, 16 * len(loads))
                        pe.wait_ge(inner, 2 if first else 1)
                        for n in range(JOBS + 4):
                            for u in units_before.get(n, []):
                                unit(*u)
                            if n == GLOBAL_STEP:
                                global_layer(0)
                            if 3 <= n < JOBS + 3:
                                pe.wait_ge(gelu3_done, n - 3 + 1)
                                if n > 3:
                                    pe.wait_ge(gate_done, n - 3)
                                nc.tensor.matmul(ps4[:, :], w4_rep[:, :], act3[:, :], start=True,
                                                 stop=True).then_inc(l4_done, 1)
                            if 2 <= n < JOBS + 2:
                                pe.wait_ge(gelu2_done, n - 2 + 1)
                                nc.tensor.matmul(ps3[0:D3, :], w3[:, :], act2[:, :], start=True,
                                                 stop=True).then_inc(l3_done, 1)
                            if n == GLOBAL_STEP:
                                global_layer(1)
                            if 1 <= n < JOBS + 1:
                                for k in range(MCH):
                                    pe.wait_ge(gelu1_done, MCH * (n - 1) + k + 1)
                                    if k == 0 and n > 1:
                                        pe.wait_ge(gelu2_done, n - 1)
                                    nc.tensor.matmul(ps2[:, :], w2[:, k, :], act1[:, k, :], start=(k == 0),
                                                     stop=(k == MCH - 1)).then_inc(l2_done, 1)
                            if n == GLOBAL_STEP:
                                global_layer(2)
                            for tile in norm_between.get(n, []):
                                turn_normed(tile)
                            for u in units_behind.get(n, []):
                                unit(*u)
                            for tile in norm_behind.get(n, []):
                                turn_normed(tile)
                            if n >= 4 and jobs[n - 4][1] == CYCLES - 1:
                                b, _, s = jobs[n - 4]
                                tile = b * TILES_B + s
                                pe.wait_ge(final_done, 2 * (tile + 1))
                                for pair in range(2):
                                    if tile > 0:
                                        pe.wait_ge(residual_done, (tile - 1) * 2 + pair + 1)
                                    for j in range(2):
                                        for h in range(HALVES):
                                            tok = (2 * pair + j) * P
                                            m = nc.tensor.transpose(ps_out[:, pair, j, h * P:(h + 1) * P],
                                                                    final[:, h, tok:tok + P], ident[:, :])
                                    m.then_inc(final_turned, 1)

                    @block.scalar
                    def _(act):
                        def keep_normed(tile):
                            for pair in range(2):
                                act.wait_ge(xn_turned, tile * 2 + pair + 1)
                                blk = tile * BLK_T + 2 * pair
                                for h, scale in ((0, ones_col), (1, twist_sign)):
                                    nc.scalar.activation(
                                        xn_ch[:, h, blk * P:(blk + 2) * P].rearrange("p (j c) -> p j c", j=2),
                                        ps_out[:, pair, :, h * P:(h + 1) * P], ACT.Identity, scale=scale[:, 0:1],
                                        accum_out=block_sums[:, h, blk:blk + 1]).then_inc(xn_kept, 1)

                        def global_activation(layer):
                            act.wait_ge(g_prod, layer + 1)
                            if layer == 0:
                                a = nc.scalar.activation(gact1[:, :], ps_out[:, 0, 0, 0:BATCH], ACT.Gelu,
                                                         bias=gb1[:, 0:1])
                            elif layer == 1:
                                a = nc.scalar.activation(gact2[:, :], ps_out[0:D3, 1, 0, 0:BATCH], ACT.Gelu,
                                                         bias=gb2[:, 0:1])
                            else:
                                a = nc.scalar.activation(gtanh[:, :], ps_out[:, 0, 0, 0:BATCH], ACT.Tanh,
                                                         bias=gb3_half[:, 0:1], scale=0.5)
                            a.then_inc(g_act, 1)

                        def deviations(part):
                            low, high = moment_parts[part]
                            act.wait_ge(stats_done, 2 * high if first else high)
                            if part > 0:
                                act.wait_ge(std_done, 2 * part)
                            nc.scalar.activation(std[:, low:high], moments[:, low:high, 1], ACT.Sqrt,
                                                 bias=eps_col[:, 0:1]).then_inc(std_done, 1)

                        deviations(0)
                        for tile in norm_first:
                            keep_normed(tile)

                        def keep_unit(tile, which):
                            u = unit_order.index((tile, which))
                            if tile >= TILES_B:
                                before = (tile // TILES_B - 1) * JOBS_B + TILES_B + tile % TILES_B
                                act.wait_ge(y_done, update_count(before))
                                if which == 0:
                                    act.wait_ge(gelu1_done, MCH * (before + TILES_B + 1))
                            for m_ch in range(MCH):
                                act.wait_ge(unit_done, MCH * u + m_ch + 1)
                                nc.scalar.activation(yz[:, tile % TILES_B, which, m_ch, :], ps1[:, m_ch, :], ACT.Copy)\
                                    .then_inc(unit_kept, 1)

                        def first_gelu(n, m_ch):
                            b, c, s = jobs[n]
                            if c == 0:
                                act.wait_ge(unit_kept, kept_count(b * TILES_B + s, 0))
                            else:
                                act.wait_ge(y_done, update_count(n - TILES_B))
                            if n > 0:
                                act.wait_ge(l2_done, MCH * (n - 1) + m_ch + 1)
                            src = y_second[:, s, m_ch, :] if c == 1 else yz[:, s, 0, m_ch, :]
                            nc.scalar.activation(act1[:, m_ch, :], src, ACT.Gelu,
                                                 bias=b1[:, m_ch:m_ch + 1]).then_inc(gelu1_done, 1)

                        for n in range(JOBS + 3):
                            for u in units_before.get(n, []):
                                keep_unit(*u)
                            if n == 0 and first:
                                deviations(1)
                            if n == GLOBAL_STEP:
                                global_activation(0)
                            if n >= 3:
                                j = n - 3
                                act.wait_ge(l4_done, j + 1)
                                if j >= 2:
                                    act.wait_ge(coupling_done, j - 1)
                                nc.scalar.activation(gate[:, j % 2, :], ps4[:, :], ACT.Tanh,
                                                     bias=b4_half[:, 0:1], scale=0.5).then_inc(gate_done, 1)
                            if 2 <= n < JOBS + 2:
                                act.wait_ge(l3_done, n - 1)
                                if n > 2:
                                    act.wait_ge(l4_done, n - 2)
                                nc.scalar.activation(act3[:, :], ps3[0:D3, :], ACT.Gelu,
                                                     bias=b3[:, 0:1]).then_inc(gelu3_done, 1)
                            if n == GLOBAL_STEP:
                                global_activation(1)
                            if n < JOBS:
                                first_gelu(n, 0)
                            if 1 <= n < JOBS + 1:
                                act.wait_ge(l2_done, MCH * n)
                                if n > 1:
                                    act.wait_ge(l3_done, n - 1)
                                nc.scalar.activation(act2[:, :], ps2[:, :], ACT.Gelu,
                                                     bias=b2[:, 0:1]).then_inc(gelu2_done, 1)
                            if n == GLOBAL_STEP:
                                global_activation(2)
                            if n < JOBS:
                                for m_ch in range(1, MCH):
                                    first_gelu(n, m_ch)
                            for tile in norm_between.get(n, []):
                                keep_normed(tile)
                            for u in units_behind.get(n, []):
                                keep_unit(*u)
                            for tile in norm_behind.get(n, []):
                                keep_normed(tile)

                    @block.gpsimd
                    def _(pool):
                        if first:
                            weights["gpsimd"](pool)
                        for tile in range(TILES):
                            b, s = tile // TILES_B, tile % TILES_B
                            j = b * JOBS_B + s
                            pool.wait_ge(coupling_done, j + 1)
                            pool.wait_ge(unit_kept, max(kept_count(tile, 0), kept_count(tile, 1)))
                            if tile > 0:
                                pool.wait_ge(z_steps, 2 * tile)
                            nc.gpsimd.tensor_tensor(c_y[:, :, :], yz[:, s, 0, :, :], wide(c_first[:, s, :]), ALU.mult)\
                                .then_inc(z_steps, 1)
                            pool.wait_ge(z_steps, 2 * tile + 1)
                            pool.wait_ge(y_done, update_count(j))
                            nc.gpsimd.tensor_tensor(yz[:, s, 1, :, :], yz[:, s, 1, :, :], c_y[:, :, :], ALU.subtract)\
                                .then_inc(z_steps, 1)
                            if tile > 0:
                                pool.wait_ge(first_state, 3 * tile)
                            nc.gpsimd.tensor_tensor(c_state_first[:, :, :], both_halves(tile), wide(c_first[:, s, :]), ALU.mult)\
                                .then_inc(first_state, 1)
                            pool.wait_ge(first_state, 3 * tile + 1)
                            nc.gpsimd.tensor_tensor(state(0, tile), state(0, tile), c_state_first[:, 1, :], ALU.add)\
                                .then_inc(first_state, 1)
                            nc.gpsimd.tensor_tensor(state(1, tile), state(1, tile), c_state_first[:, 0, :], ALU.subtract)\
                                .then_inc(first_state, 1)

                    @block.vector
                    def _(dve):
                        def row(blk):
                            return x_tok[:, ds(blk, 1), :].rearrange("p a c -> p (a c)")

                        marks = [0]

                        def mark(ins):
                            marks[0] += 1
                            ins.then_inc(inner, 1)
                            return marks[0]

                        for part, (low, high) in enumerate(moment_parts):
                            if first:
                                for blk in range(low, high):
                                    if blk % G == 0:
                                        dve.wait_ge(x_loaded[blk // G], 16)
                                    nc.vector.bn_stats(stats[:, blk, :], row(blk)).then_inc(stats_done, 1)
                                if part == len(moment_parts) - 1:
                                    dve.wait_ge(inner, mark(ffn_weights(dve)))
                                    mark(nc.vector.tensor_scalar(w1_neg[:, :], w1[:, 1, :], -1.0, None, ALU.mult))
                                dve.wait_ge(stats_done, low + high)
                            for blk in range(low, high):
                                nc.vector.bn_aggr(moments[:, blk, :], stats[:, blk, :]).then_inc(stats_done, 1)
                            if not first:
                                mark(nc.vector.tensor_scalar(w1_neg[:, :], w1[:, 1, :], -1.0, None, ALU.mult))
                            dve.wait_ge(std_done, 2 * part + 1)
                            nc.vector.reciprocal(rstd[:, low:high], std[:, low:high]).then_inc(std_done, 1)
                            dve.wait_ge(std_done, 2 * part + 2)
                            for tile in range(low // BLK_T, high // BLK_T):
                                if tile >= 2:
                                    dve.wait_ge(xn_turned, 2 * (tile - 1))
                                for i in range(BLK_T):
                                    blk = tile * BLK_T + i
                                    t = nc.vector.tensor_scalar(xn_tok(tile)[:, i, :], row(blk), moments[:, blk, 0:1],
                                                                rstd[:, blk:blk + 1], ALU.subtract, ALU.mult)
                                t.then_inc(xn_ready, 1)
                        dve.wait_ge(xn_kept, 4 * TILES)

                        for b in range(BATCH):
                            sums = block_sums[:, :, b * BLK_B:(b + 1) * BLK_B].rearrange(
                                "p h (n two) -> p h n two", two=2)[:, :, :, 0]
                            summed = mark(nc.vector.tensor_reduce(mean[:, :, b:b + 1], sums, AX_X, ALU.add))
                        dve.wait_ge(inner, summed)
                        mark(nc.vector.tensor_scalar(mean[:, :, :], mean[:, :, :], 1.0 / SEQ, None, ALU.mult))

                        dve.wait_ge(g_act, 3)
                        ranged = mark(nc.vector.tensor_scalar(base[:, :], gtanh[:, :], rng[:, 0:1], 0.7, ALU.mult,
                                                              ALU.mult))
                        dve.wait_ge(inner, ranged)
                        based = mark(nc.vector.tensor_scalar(base[:, :], base[:, :], 0.1, None, ALU.add))
                        dve.wait_ge(inner, based)

                        def residual(tile):
                            for pair in range(2):
                                dve.wait_ge(final_turned, tile * 2 + pair + 1)
                                blk = tile * BLK_T + 2 * pair
                                kept = DM - P // 2
                                nc.vector.scalar_tensor_tensor(
                                    x_tok[:, blk:blk + 2, 0:kept], ps_out[:, pair, :, 0:kept], 0.5,
                                    x_tok[:, blk:blk + 2, 0:kept], ALU.mult, ALU.add)
                                nc.vector.scalar_tensor_tensor(
                                    x_tok[:, blk:blk + 2, kept:DM], ps_out[:, pair, :, kept:DM], -0.5,
                                    x_tok[:, blk:blk + 2, kept:DM], ALU.mult, ALU.add)\
                                    .then_inc(residual_done, 1)

                        def statistics(tile):
                            if first:
                                dve.wait_ge(residual_done, 2 * (tile + 1))
                                for blk in range(tile * BLK_T, (tile + 1) * BLK_T):
                                    nc.vector.bn_stats(stats[:, blk, :], row(blk))

                        for j, (b, c, s) in enumerate(jobs):
                            tile = b * TILES_B + s
                            dve.wait_ge(gate_done, j + 1)
                            c_now = c_first[:, s, :] if c == 0 else coupling[:, :]
                            nc.vector.tensor_scalar(c_now, gate[:, j % 2, :], gain[:, 0:1],
                                                    base[:, b:b + 1], ALU.mult, ALU.add)\
                                .then_inc(coupling_done, 1)
                            dve.wait_ge(coupling_done, j + 1)
                            if c < CYCLES - 1:
                                if update_count(j) > 1:
                                    dve.wait_ge(y_done, update_count(j) - 1)
                                if j > 0 and jobs[j - 1][1] == 1:
                                    dve.wait_ge(second_state, 2 * tile)
                                if final_count(j) > 0:
                                    dve.wait_ge(final_done, final_count(j))
                                dve.wait_ge(unit_kept, kept_count(tile, 1))
                                if c == 1:
                                    dve.wait_ge(z_steps, 2 * (tile + 1))
                                moved = mark(nc.vector.tensor_tensor(c_times[:, :, :], yz[:, s, 1, :, :], wide(c_now), ALU.mult))
                                dve.wait_ge(inner, moved)
                                old, new = yz[:, s, 0, :, :], y_second[:, s, :, :]
                                if c == 1:
                                    old, new = new, old
                                nc.vector.tensor_tensor(new, old, c_times[:, :, :], ALU.add).then_inc(y_done, 1)
                            if c > 0:
                                if c == 1:
                                    dve.wait_ge(first_state, 3 * (tile + 1))
                                else:
                                    dve.wait_ge(second_state, 2 * (tile + 1))
                                dve.wait_ge(y_done, update_count(j) if c == 1 else (b + 1) * (CYCLES - 1) * TILES_B)
                                if final_count(j) > 0:
                                    dve.wait_ge(final_done, final_count(j))
                                moved = mark(nc.vector.tensor_tensor(c_times[:, :, :], both_halves(tile), wide(c_now),
                                                                     ALU.mult))
                                if c == CYCLES - 1 and s > 0:
                                    residual(tile - 1)
                                dve.wait_ge(inner, moved)
                                done = second_state if c == 1 else final_done
                                new_state = ([state(0, tile), state(1, tile)] if c == 1
                                             else [final[:, 0, :], final[:, 1, :]])
                                nc.vector.tensor_tensor(new_state[0], state(0, tile), c_times[:, 1, :], ALU.add)\
                                    .then_inc(done, 1)
                                nc.vector.tensor_tensor(new_state[1], state(1, tile), c_times[:, 0, :], ALU.subtract)\
                                    .then_inc(done, 1)
                                if c == CYCLES - 1 and s > 0:
                                    statistics(tile - 1)
                            if c == 0 and s == 0 and b > 0:
                                residual(b * TILES_B - 1)
                                statistics(b * TILES_B - 1)
                        residual(TILES - 1)
                        statistics(TILES - 1)

                    if first:
                        @block.sync
                        def _(sp):
                            for dst, src in loads:
                                sp.dma_start(dst, src, allow_slow_non_contiguous=True).then_inc(loaded, 16)
                            weights["sync"](sp)

                    if last:
                        @block.sync
                        def _(sp):
                            for k in range(TILES):
                                sp.wait_ge(residual_done, k * 2 + 2)
                                sp.dma_start(out_blocks[:, k * BLK_T:(k + 1) * BLK_T, :],
                                             x_tok[:, k * BLK_T:(k + 1) * BLK_T, :]).then_inc(stored, 16)
                            sp.wait_ge(stored, 16 * TILES)

        HEADS, DH = 16, DM // 16
        FEAT = proj.shape[0]
        STRIP = 32
        PER_G = P // STRIP
        GROUPS = HEADS // PER_G
        HALF_HEADS = HEADS // 2
        SCALE = DH ** -0.5
        X_SCALE = sqrt(SCALE)
        FSCALE = 4096.0
        UNSCALE = 1.0 / (FSCALE * FSCALE)
        WSCALE = 64.0
        LOCAL_SHARE = 1.0 - SCALE
        assert DH == 16 and FEAT == 24 and GROUPS == 4 and PER_G == 4

        def first_ffn_and_attention():
            with ExitStack() as scope:
                wq_s = [sb(f"wq_s_{part}", [P, HALVES, HEADS * STRIP], F16, scope) for part in ("high", "low")]
                wk_s = [sb(f"wk_s_{part}", [P, HALVES, HEADS * STRIP], F16, scope) for part in ("high", "low")]
                w_vq = [sb(f"w_vq_{part}", [P, HALVES, 2 * DM], F16, scope) for part in ("high", "low")]
                w_qf = [sb(f"w_qf_{part}", [P, HALVES, HEADS * FEAT], F16, scope) for part in ("high", "low")]
                w_o = sb("w_o", [P, HALVES, DM], F32, scope)
                bq_s = sb("bq_s", [P, GROUPS], F32, scope)
                bk_s = sb("bk_s", [P, GROUPS], F32, scope)
                b_vq = sb("b_vq", [P, 2 * DM], F32, scope)
                b_qf = sb("b_qf", [P, HEADS * FEAT], F32, scope)
                b_o = sb("b_o", [P, DM], F32, scope)
                log_k = nc.dram_tensor("log_k", (NBLK + 2, P, GROUPS, P), F32, kind="Internal").ap()
                neg_kmax = sb("neg_kmax", [P, NBLK + 1, GROUPS], F32, scope)
                kmax_tok = sb("kmax_tok", [P, NBLK + 1, HEADS], F32, scope)
                penalty = sb("penalty", [P, NBLK + 1], F32, scope)
                has_prev = sb("has_prev", [P, NBLK + 1], F32, scope)
                keep_state = sb("keep_state", [P, NBLK + 1], F32, scope)
                low_rows = sb("low_rows", [P, 1], F32, scope)
                ident16 = sb("ident16", [P, P], BF16, scope)
                mask_q = sb("mask_q", [P, 2, 2, P], BF16, scope)
                stair_own_l = sb("stair_own_l", [P, P], BF16, scope)
                stair_prev_l = sb("stair_prev_l", [P, P], BF16, scope)
                stair_own_r = sb("stair_own_r", [P, HEADS, P], BF16, scope)
                stair_prev_r = sb("stair_prev_r", [P, HEADS, P], BF16, scope)
                gmask = sb("gmask", [P, 2, P], BF16, scope)
                diag_strips = sb("diag_strips", [P, PER_G, STRIP], F32, scope)

                def attention_weights(scope):
                    rows = sb("qkv_rows", [P, 3 * HALVES, DM], F32, scope)
                    o_rows = sb("o_rows", [P, HALVES, DM], F32, scope)
                    bq_col = sb("bq_col", [P, HALVES], F32, scope)
                    bq_rep = sb("bq_rep", [P, HALVES, P], F32, scope)
                    BANKS = 4
                    ps = []
                    loaded = sem("prep_loaded", scope)
                    blank = sem("prep_blank", scope)
                    drawn = sem("prep_drawn", scope)
                    tables = sem("prep_tables", scope)
                    product = sem("prep_product", scope)
                    evacuated = sem("prep_evacuated", scope)
                    reps = sem("prep_reps", scope)
                    high_kept = sem("prep_high_kept", scope)

                    row = lambda v, n: v.rearrange("(a n) -> a n", a=1).broadcast_to([P, n])
                    loads = [
                        (rows[:, :, :], wqkv.rearrange("(k p) n -> p k n", p=P)),
                        (o_rows[:, :, :], wout.rearrange("(k p) n -> p k n", p=P)),
                        (bq_col[:, :], bqkv[0:DM].rearrange("(k p) -> p k", p=P)),
                        (bk_col[:, :], bqkv[DM:2 * DM].rearrange("(k p) -> p k", p=P)),
                        (b_vq[:, 0:DM], row(bqkv[2 * DM:3 * DM], DM)),
                        (b_vq[:, DM:2 * DM], row(bqkv[0:DM], DM)),
                        (b_o[:, :], row(bout, DM)),
                    ]
                    for j in range(HALF_HEADS):
                        loads.append((proj_bd[j * DH:(j + 1) * DH, j, :], proj.rearrange("m d -> d m")))
                    for which, dst in ((0, bq_s), (1, bk_s)):
                        src = bqkv[which * DM:(which + 1) * DM].rearrange("(g r d) -> r d g", g=GROUPS, r=PER_G)
                        for r in range(PER_G):
                            for dup in range(2):
                                at = r * STRIP + dup * DH
                                loads.append((dst[at:at + DH, :], src[r]))

                    jobs = []
                    for k in range(HALVES):
                        for i in range(HALVES):
                            def strips(w, dup, k=k, i=i):
                                return [part[:, k, i * HALF_HEADS * STRIP:(i + 1) * HALF_HEADS * STRIP].rearrange(
                                    "p (h s) -> p h s", s=STRIP)[:, :, dup * DH:(dup + 1) * DH] for part in w]

                            def halves(w, at, k=k):
                                return [part[:, k, at] for part in w]
                            heads = "p (h d) -> p h d"
                            jobs.append((("turn", rows, i, k), [(strips(wq_s, 0), SCALE, heads), (strips(wq_s, 1), SCALE, heads),
                                                                (halves(w_vq, slice(DM + i * P, DM + (i + 1) * P)), 1.0, None)]))
                            jobs.append((("turn", rows, 2 + i, k), [(strips(wk_s, 0), 1.0, heads), (strips(wk_s, 1), 1.0, heads),
                                                                    (w_k[:, k, i * P:(i + 1) * P], 1.0, None)]))
                            jobs.append((("turn", rows, 4 + i, k), [(halves(w_vq, slice(i * P, (i + 1) * P)), 1.0, None)]))
                            jobs.append((("turn", o_rows, i, k), [(w_o[:, k, i * P:(i + 1) * P], 1.0, None)]))
                            jobs.append((("feat", rows, i, k), [(halves(w_qf, slice(i * HALF_HEADS * FEAT, (i + 1) * HALF_HEADS * FEAT)),
                                                                 X_SCALE, None)]))
                    for i in range(HALVES):
                        jobs.append((("bias", bq_rep, i, 0), [(b_qf[:, i * HALF_HEADS * FEAT:(i + 1) * HALF_HEADS * FEAT],
                                                               X_SCALE, None)]))

                    def evacuations(n):
                        (kind, *_), views = jobs[n]
                        src = ps[n % BANKS][:, 0:P if kind == "turn" else HALF_HEADS * FEAT]
                        return [(view, scale, src.rearrange(split, d=DH) if split else src)
                                for view, scale, split in views]

                    highs_until = [sum(isinstance(view, list) for _, views in jobs[:n + 1] for view, *_ in views)
                                   for n in range(len(jobs))]

                    def on_sync(sp):
                        sp.wait_ge(blank, 1)
                        for dst, src in loads:
                            sp.dma_start(dst, src, allow_slow_non_contiguous=True).then_inc(loaded, 16)

                    def on_gpsimd(pool):
                        nc.gpsimd.memset(proj_bd[:, :, :], 0.0).then_inc(blank, 1)
                        zero = [(ident16, 0.0), (mask_q, 0.0), (stair_own_l, 1.0), (stair_prev_l, 1.0),
                                (stair_own_r, 0.0), (stair_prev_r, 0.0), (gmask[:, 0, :], LOCAL_SHARE),
                                (gmask[:, 1, :], 1.0), (diag_strips, 1.0), (low_rows, 1.0),
                                (penalty, 0.0), (has_prev, 1.0), (keep_state, 1.0),
                                ]
                        for buf, value in zero:
                            last = nc.gpsimd.memset(buf if isinstance(buf, bass.AP) else buf[tuple([slice(None)] * len(buf.shape))], value)
                        last.then_inc(blank, 1)
                        pool.wait_ge(blank, 2)

                        selected = [0]

                        def select(view, op, fill, base, pattern, mult):
                            selected[0] += 1
                            nc.gpsimd.affine_select(out=view, in_=view, compare_op=op, fill=fill, base=base,
                                                    pattern=pattern, channel_multiplier=mult)\
                                .then_inc(drawn, 1)
                            pool.wait_ge(drawn, selected[0])

                        select(ident16[:, :], ALU.not_equal, 1.0, 0, [[-1, P]], 1)
                        for order in range(2):
                            own, prev = 1 - order, order
                            select(mask_q[:, order, own, :], ALU.is_ge, MASKED, 0, [[-1, P]], 1)
                            select(mask_q[:, order, prev, :], ALU.is_ge, MASKED, 0, [[1, P]], -1)
                        select(stair_own_l[:, :], ALU.is_ge, 0.0, 0, [[1, P]], -1)
                        select(stair_prev_l[:, :], ALU.is_ge, 0.0, 0, [[-1, P]], 1)
                        select(stair_own_r[:, :, :], ALU.not_equal, MASKED, -1, [[0, HEADS], [-1, P]], 1)
                        select(stair_prev_r[:, :, :], ALU.not_equal, MASKED, 1, [[0, HEADS], [-1, P]], 1)
                        select(gmask[:, 0, :], ALU.is_ge, 0.0, 0, [[1, P]], -1)
                        select(gmask[:, 1, :], ALU.is_gt, LOCAL_SHARE, 0, [[1, P]], -1)
                        select(diag_strips[:, :, :], ALU.is_ge, 0.0, 0, [[-STRIP, PER_G], [0, STRIP]], 1)
                        select(diag_strips[:, :, :], ALU.is_ge, 0.0, STRIP - 1, [[STRIP, PER_G], [0, STRIP]], -1)
                        first_of_batch = [b * BLK_B for b in range(BATCH + 1)]
                        for blk in first_of_batch:
                            nc.gpsimd.memset(penalty[:, blk:blk + 1], MASKED)
                            nc.gpsimd.memset(has_prev[:, blk:blk + 1], 0.0)
                            nc.gpsimd.memset(keep_state[:, blk:blk + 1], 0.0)
                            if blk:
                                nc.gpsimd.memset(keep_state[:, blk - 1:blk], 0.0)
                        nc.gpsimd.memset(ident16[0:1, 0:1], 1.0).then_inc(tables, 1)

                    def on_vector(dve):
                        dve.wait_ge(loaded, 16 * len(loads))
                        nc.vector.tensor_copy(bq_rep[:, :, :], bq_col[:, :].unsqueeze(2).broadcast_to([P, HALVES, P]))\
                            .then_inc(reps, 1)
                        dve.wait_ge(tables, 1)
                        nc.vector.tensor_reduce(
                            low_rows[:, :],
                            ident16[:, :].rearrange("p (r two d) -> p r two d", two=2, d=DH)[:, :, 1, :],
                            mybir.AxisListType.XY, ALU.add)
                        nc.vector.tensor_scalar(bq_s[:, :], bq_s[:, :], SCALE, None, ALU.mult)
                        for n in range(len(jobs)):
                            dve.wait_ge(product, n + 1)
                            if highs_until[n] > (highs_until[n - 1] if n else 0):
                                dve.wait_ge(high_kept, highs_until[n])
                            for view, scale, src in evacuations(n):
                                if isinstance(view, list):
                                    last = nc.vector.scalar_tensor_tensor(view[1], src, scale * WSCALE, view[0],
                                                                          ALU.mult, ALU.subtract)
                                else:
                                    last = nc.vector.tensor_scalar(view, src, scale, None, ALU.mult)
                            last.then_inc(evacuated, 1)

                    def on_scalar(act):
                        for n in range(len(jobs)):
                            parted = [e for e in evacuations(n) if isinstance(e[0], list)]
                            if parted:
                                act.wait_ge(product, n + 1)
                            for view, scale, src in parted:
                                nc.scalar.activation(view[0], src, ACT.Copy, scale=scale * WSCALE)\
                                    .then_inc(high_kept, 1)

                    def on_tensor(pe):
                        pe.wait_ge(loaded, 16 * len(loads))
                        for n, ((kind, src, i, k), _) in enumerate(jobs):
                            if n >= BANKS:
                                pe.wait_ge(evacuated, n - BANKS + 1)
                            bank = ps[n % BANKS]
                            if kind == "turn":
                                last = nc.tensor.transpose(bank[:, 0:P], src[:, i, k * P:(k + 1) * P], ident[:, :])
                            else:
                                if kind == "bias":
                                    pe.wait_ge(reps, 1)
                                left = src[:, i, k * P:(k + 1) * P] if kind == "feat" else src[:, i, :]
                                last = nc.tensor.matmul(bank[:, 0:HALF_HEADS * FEAT], left,
                                                        proj_bd[:, :, :].rearrange("p h m -> p (h m)"),
                                                        start=True, stop=True)
                            last.then_inc(product, 1)

                    return {"sync": on_sync, "gpsimd": on_gpsimd, "vector": on_vector, "scalar": on_scalar,
                            "tensor": on_tensor, "banks": ps}

                def key_features(outer):
                    TILES = NBLK // BLK_T
                    with ExitStack() as scope:
                        lift = sb("lift", [P, 2, PER_G, STRIP], F32, scope)
                        halve = sb("halve", [P, HALF_HEADS, STRIP], F32, scope)
                        ones_sq = sb("ones_sq", [P, P], F32, scope)
                        strip_head = sb("strip_head", [P, PER_G], F32, scope)
                        k_and_sq = sb("k_and_sq", [P, 2, GROUPS, TILE], F32, scope)
                        logs_sb = sb("logs_sb", [P, 2, GROUPS, TILE], F32, scope)
                        no_logs = sb("no_logs", [P, GROUPS, P], F32, scope)
                        tile_max = sb("tile_max", [P, BATCH, GROUPS, TILES_B], F32, scope)
                        row_max = sb("row_max", [P, STRIP], F32, scope)
                        row_max_t = sb("row_max_t", [P, STRIP], F32, scope)
                        head_max = sb("head_max", [P, 1], F32, scope)
                        head_max_b = sb("head_max_b", [P, STRIP], F32, scope)
                        kmax = sb("kmax", [P, STRIP], F32, scope)
                        one_row = sb("one_row", [P, BATCH, GROUPS, PER_G], F32, scope)
                        ps_k = psum("ps_k", [P, HALVES, TILE], scope)
                        ps_log = psum("ps_log", [P, GROUPS, TILE], scope)
                        ps_spread = psum("ps_spread", [P, 512], scope)
                        patterns = sem("kf_patterns", scope)
                        lift_ready = sem("lift_ready", scope)
                        k_product = sem("k_product", scope)
                        k_ready = sem("k_ready", scope)
                        k_sq_ready = sem("k_sq_ready", scope)
                        log_product = sem("log_product", scope)
                        log_kept = sem("log_kept", scope)
                        log_max = sem("log_max", scope)
                        log_stored = [sem(f"log_stored{i}", scope) for i in range(2)]
                        pad_stored = sem("pad_stored", scope)
                        chain = sem("kmax_chain", scope)
                        spread = sem("kmax_spread", scope)
                        with nc.Block() as block:
                            @block.gpsimd
                            def _(pool):
                                nc.gpsimd.memset(halve[:, :, :], -SCALE / 2)
                                nc.gpsimd.memset(strip_head[:, :], 0.0)
                                nc.gpsimd.memset(row_max[:, :], 0.0)
                                nc.gpsimd.memset(no_logs[:, :, :], 0.0)
                                nc.gpsimd.memset(ones_sq[:, :], 1.0).then_inc(patterns, 1)
                                pool.wait_ge(patterns, 1)
                                nc.gpsimd.affine_select(out=halve[:, :, :], in_=halve[:, :, :], compare_op=ALU.is_ge, fill=0.0,
                                                        base=0, pattern=[[-DH, HALF_HEADS], [0, STRIP]], channel_multiplier=1)\
                                    .then_inc(patterns, 1)
                                pool.wait_ge(patterns, 2)
                                nc.gpsimd.affine_select(out=halve[:, :, :], in_=halve[:, :, :], compare_op=ALU.is_ge, fill=0.0,
                                                        base=DH - 1, pattern=[[DH, HALF_HEADS], [0, STRIP]], channel_multiplier=-1)
                                nc.gpsimd.affine_select(out=strip_head[:, :], in_=strip_head[:, :], compare_op=ALU.not_equal,
                                                        fill=1.0, base=0, pattern=[[-STRIP, PER_G]], channel_multiplier=1)\
                                    .then_inc(patterns, 1)

                            @block.tensor
                            def _(pe):
                                def keys(n):
                                    for i in range(HALVES):
                                        for k in range(HALVES):
                                            m = nc.tensor.matmul(ps_k[:, i, :], w_k[:, k, i * P:(i + 1) * P],
                                                                 xn_ch[:, k, ds(n * TILE, TILE)], start=(k == 0),
                                                                 stop=(k == HALVES - 1))
                                    m.then_inc(k_product, 1)

                                def logs(n, par, peeled):
                                    pe.wait_ge(k_sq_ready, n + 1)
                                    for g in range(GROUPS):
                                        if not peeled:
                                            pe.wait_ge(log_kept, (n - 1) * GROUPS + g + 1)
                                            pe.wait_ge(log_max, (n - 1) * GROUPS + g + 1)
                                        nc.tensor.matmul(ps_log[:, g, :], lift[:, g % 2, :, :].rearrange("p h m -> p (h m)"),
                                                         k_and_sq[:, par, g, :], start=True, stop=True)\
                                            .then_inc(log_product, 1)

                                pe.wait_ge(patterns, 3)
                                pe.wait_ge(lift_ready, 1)
                                keys(0)
                                for n in range(2):
                                    pe.wait_ge(k_ready, n + 1)
                                    keys(n + 1)
                                    logs(n, n, n == 0)
                                with pe.Fori(1, TILES // 2 - 1) as j:
                                    for par in range(2):
                                        n = j * 2 + par
                                        pe.wait_ge(k_ready, n + 1)
                                        keys(n + 1)
                                        logs(n, par, False)
                                for n in range(TILES - 2, TILES):
                                    pe.wait_ge(k_ready, n + 1)
                                    if n + 1 < TILES:
                                        keys(n + 1)
                                    logs(n, n % 2, False)
                                pe.wait_ge(chain, 7)
                                nc.tensor.matmul(ps_spread[:, 0:BATCH * HEADS], ones_sq[:, :],
                                                 one_row[:, :, :, :].rearrange("p b g r -> p (b g r)"), start=True,
                                                 stop=True).then_inc(spread, 1)

                            @block.scalar
                            def _(act):
                                def tile(n, par, peeled):
                                    act.wait_ge(k_ready, n + 1)
                                    if not peeled:
                                        act.wait_ge(log_product, (n - 1) * GROUPS)
                                    for q in range(2):
                                        own, other = slice(q * P // 2, (q + 1) * P // 2), slice((1 - q) * P // 2, (2 - q) * P // 2)
                                        a = nc.scalar.activation(k_and_sq[other, par, q::2, :], k_and_sq[own, par, q::2, :],
                                                                 ACT.Square)
                                    a.then_inc(k_sq_ready, 1)

                                def keep_logs(n, par, before):
                                    if before is not None:
                                        act.wait_ge(log_stored[par], 16 * before)
                                    for g in range(GROUPS):
                                        act.wait_ge(log_product, n * GROUPS + g + 1)
                                        act.wait_ge(log_max, n * GROUPS + g + 1)
                                        nc.scalar.activation(logs_sb[:, par, g, :], ps_log[:, g, :],
                                                             ACT.Identity).then_inc(log_kept, 1)

                                tile(0, 0, True)
                                tile(1, 1, True)
                                keep_logs(0, 0, None)
                                tile(2, 0, False)
                                keep_logs(1, 1, None)
                                tile(3, 1, False)
                                keep_logs(2, 0, 1)
                                with act.Fori(2, TILES // 2) as j:
                                    tile(j * 2, 0, False)
                                    keep_logs(j * 2 - 1, 1, j - 1)
                                    tile(j * 2 + 1, 1, False)
                                    keep_logs(j * 2, 0, j)
                                keep_logs(TILES - 1, 1, TILES // 2 - 1)

                            @block.sync
                            def _(sp):
                                sp.wait_ge(patterns, 3)
                                for pad in range(2):
                                    sp.dma_start(log_k[NBLK + pad, :, :, :], no_logs[:, :, :]).then_inc(pad_stored, 16)
                                for n in range(TILES):
                                    sp.wait_ge(log_kept, (n + 1) * GROUPS)
                                    sp.dma_start(log_k[n * BLK_T:(n + 1) * BLK_T, :, :, :].rearrange("a p g q -> p g a q"),
                                                 logs_sb[:, n % 2, :, :].rearrange("p g (a q) -> p g a q", q=P))\
                                        .then_inc(log_stored[n % 2], 16)
                                for stored in log_stored:
                                    sp.wait_ge(stored, 16 * (TILES // 2))
                                sp.wait_ge(pad_stored, 32)

                            @block.vector
                            def _(dve):
                                dve.wait_ge(patterns, 3)
                                for q in range(2):
                                    own, other = slice(q * P // 2, (q + 1) * P // 2), slice((1 - q) * P // 2, (2 - q) * P // 2)
                                    mine, theirs = slice(q * PER_G, (q + 1) * PER_G), slice((1 - q) * PER_G, (2 - q) * PER_G)
                                    nc.vector.tensor_scalar(lift[own, q, :, 0:FEAT], proj_bd[own, mine, :], X_SCALE, None,
                                                            ALU.mult)
                                    nc.vector.tensor_scalar(lift[own, q, :, FEAT:STRIP],
                                                            proj_bd[own, mine, 0:1].broadcast_to([P // 2, PER_G, STRIP - FEAT]),
                                                            X_SCALE, None, ALU.mult)
                                    last = nc.vector.tensor_copy(lift[other, q, :, :], halve[other, theirs, :])
                                last.then_inc(lift_ready, 1)

                                def keys(n):
                                    dve.wait_ge(k_product, n + 1)
                                    if n >= 2:
                                        dve.wait_ge(log_product, (n - 1) * GROUPS)
                                    for q in range(2):
                                        own = slice(q * P // 2, (q + 1) * P // 2)
                                        k = nc.vector.tensor_tensor(
                                            k_and_sq[own, n % 2, q::2, :], ps_k[own, :, :],
                                            bk_col[own, :].unsqueeze(2).broadcast_to([P // 2, HALVES, TILE]), ALU.add)
                                    k.then_inc(k_ready, 1)

                                keys(0)
                                for b in range(BATCH):
                                    for s in range(TILES_B):
                                        if b * TILES_B + s + 1 < TILES:
                                            keys(b * TILES_B + s + 1)
                                        for g in range(GROUPS):
                                            n = (b * TILES_B + s) * GROUPS + g
                                            dve.wait_ge(log_product, n + 1)
                                            nc.vector.tensor_reduce(tile_max[:, b, g, s:s + 1], ps_log[:, g, :], AX_X,
                                                                    ALU.max).then_inc(log_max, 1)
                                dve.wait_ge(log_max, NBLK // BLK_T * GROUPS)
                                dve.wait_ge(patterns, 3)

                                steps = [0]

                                def link(ins):
                                    steps[0] += 1
                                    ins.then_inc(chain, 1)
                                    dve.wait_ge(chain, steps[0])

                                link(nc.vector.tensor_reduce(row_max[:, 0:BATCH * GROUPS],
                                                             tile_max[:, :, :, :].rearrange("p b g s -> p (b g) s"), AX_X, ALU.max))
                                link(nc.vector.transpose(row_max_t[:, :], row_max[:, :]))
                                link(nc.vector.tensor_reduce(head_max[:, :], row_max_t[:, :], AX_X, ALU.max))
                                link(nc.vector.tensor_copy(head_max_b[:, :], head_max[:, :].broadcast_to([P, STRIP])))
                                link(nc.vector.transpose(kmax[:, :], head_max_b[:, :]))
                                km = kmax[:, 0:BATCH * GROUPS].rearrange("p (b g) -> p b g", b=BATCH)
                                link(nc.vector.memset(neg_kmax[:, NBLK:, :], 0.0))
                                link(nc.vector.tensor_tensor(
                                    one_row[:, :, :, :].rearrange("p b g r -> p (b g) r"),
                                    kmax[:, 0:BATCH * GROUPS].unsqueeze(2).broadcast_to([P, BATCH * GROUPS, PER_G]),
                                    strip_head[:, :].unsqueeze(1).broadcast_to([P, BATCH * GROUPS, PER_G]), ALU.mult))
                                for b in range(BATCH):
                                    nc.vector.tensor_scalar(neg_kmax[:, b * BLK_B:(b + 1) * BLK_B, :],
                                                            km[:, b:b + 1, :].broadcast_to([P, BLK_B, GROUPS]), -1.0, None,
                                                            ALU.mult)
                                dve.wait_ge(spread, 1)
                                nc.vector.memset(kmax_tok[:, NBLK:, :], 0.0)
                                for b in range(BATCH):
                                    nc.vector.tensor_copy(
                                        kmax_tok[:, b * BLK_B:(b + 1) * BLK_B, :],
                                        ps_spread[:, b * HEADS:(b + 1) * HEADS].unsqueeze(1).broadcast_to([P, BLK_B, HEADS]))

                def attention_blocks(outer):
                    RING = 4
                    FEATURE_ITEMS = (5, 7, 9, 12)
                    with ExitStack() as scope:
                        x_high = sb("x_high", [P, 2, HALVES, P], F16, scope)
                        x_low = sb("x_low", [P, 2, HALVES, P], F16, scope)
                        q32 = sb("q32", [P, GROUPS, P], F32, scope)
                        k32 = sb("k32", [P, GROUPS, P], F32, scope)
                        q_high = sb("q_high", [P, GROUPS, P], F16, scope)
                        q_low = sb("q_low", [P, GROUPS, P], F16, scope)
                        k_lowhigh = sb("k_lowhigh", [P, GROUPS, P], F16, scope)
                        q_bd = sb("q_bd", [P, 2, 2, GROUPS, PER_G, P], F16, scope)
                        k_mix = sb("k_mix", [P, GROUPS, RING, P], F16, scope)
                        v_ext = sb("v_ext", [P, RING, HEADS, STRIP], F32, scope)
                        q_tok = sb("q_tok", [P, DM], F32, scope)
                        qf_tok = sb("qf_tok", [P, HEADS, FEAT], F32, scope)
                        qf_pad = sb("qf_pad", [P, HEADS, STRIP], F32, scope)
                        q_norm = sb("q_norm", [P, HEADS], F32, scope)
                        qf_max = sb("qf_max", [P, HEADS], F32, scope)
                        q_scale = sb("q_scale", [P, HEADS], F32, scope)
                        g_scale = sb("g_scale", [P, 2, HEADS], F32, scope)
                        log_blk = sb("log_blk", [P, GROUPS, P], F32, scope)
                        scaled_eps = sb("scaled_eps", [P, 1], F32, scope)
                        kf32 = sb("kf32", [P, GROUPS, P], F32, scope)
                        kf_high = sb("kf_high", [P, RING, GROUPS, P], F16, scope)
                        kf_low = sb("kf_low", [P, RING, GROUPS, P], F16, scope)
                        kf_tok = sb("kf_tok", [P, 2, HEADS * STRIP], F32, scope)
                        qf32 = sb("qf32", [P, 2, GROUPS, P], F32, scope)
                        qf_high = sb("qf_high", [P, GROUPS, P], F16, scope)
                        qf_low = sb("qf_low", [P, GROUPS, P], F16, scope)
                        qf_bd = sb("qf_bd", [P, 2, 1, GROUPS, PER_G, P], F16, scope)
                        block_max = sb("block_max", [P, GROUPS, PER_G, 2], F32, scope)
                        row_top = sb("row_top", [P, HEADS], F32, scope)
                        neg_max = sb("neg_max", [P, 2, HEADS], BF16, scope)
                        max_rows = sb("max_rows", [2 * HEADS, P], BF16, scope)
                        lift_arg = sb("lift_arg", [P, HEADS], F32, scope)
                        lift_exp = sb("lift_exp", [P, 2, HEADS], F32, scope)
                        probs = sb("probs", [P, 2, 2, PER_G, P], F32, scope)
                        feats = sb("feats", [P, 2, 2, PER_G, P], F32, scope)
                        state = sb("kv_state", [P, GROUPS, P], F32, scope)
                        state_inc = sb("kv_state_inc", [P, GROUPS, P], F32, scope)
                        sums = sb("sums", [P, 2, GROUPS * P], F32, scope)
                        r_local = sb("r_local", [P, HEADS], F32, scope)
                        norm_a = sb("norm_a", [P, HEADS], F32, scope)
                        norm_b = sb("norm_b", [P, HEADS], F32, scope)
                        norm_c = sb("norm_c", [P, HEADS], F32, scope)
                        norm_r = sb("norm_r", [P, HEADS], F32, scope)
                        r_global = sb("r_global", [P, HEADS], F32, scope)
                        ctx_a = sb("ctx_a", [P, HEADS, DH], F32, scope)
                        ctx = sb("ctx", [P, DM], F32, scope)
                        ctx_ch = sb("ctx_ch", [P, HALVES, P], F32, scope)

                        pairs = [psum(f"pair{i}", [P, 2, 512], scope) for i in range(3)]
                        ps_local = psum("ps_local", [P, GROUPS * P], scope)
                        ps_global = psum("ps_global", [P, GROUPS * P], scope)

                        def pair(item):
                            return pairs[item % 3]

                        PASSES = ((0, x_high), (1, x_high), (0, x_low))

                        def S(name):
                            return sem("a_" + name, scope)

                        cleared, cleared_dve = S("cleared"), S("cleared_dve")
                        x_high_ready, x_ready = S("x_high_ready"), S("x_ready")
                        qk_product, q32_ready, k32_ready = S("qk_product"), S("q32_ready"), S("k32_ready")
                        q_high_ready, k_lowhigh_ready = S("q_high_ready"), S("k_lowhigh_ready")
                        q_low_ready, k_mix_ready, q_bd_ready = S("q_low_ready"), S("k_mix_ready"), S("q_bd_ready")
                        vq_product, v_ready, q_tok_ready, qf_ready = S("vq_product"), S("v_ready"), S("q_tok_ready"), S("qf_ready")
                        q_sq_ready, q_norm_ready, qf_max_ready, qf_shifted = S("q_sq_ready"), S("q_norm_ready"), S("qf_max_ready"), S("qf_shifted")
                        q_scale_ready, g_scale_ready = S("q_scale_ready"), S("g_scale_ready")
                        qf_exp_ready, qf_pad_ready = S("qf_exp_ready"), S("qf_pad_ready")
                        log_loaded = S("log_loaded")
                        kf_exp_ready, kf32_ready, kf_high_ready, kf_low_ready = S("kf_exp_ready"), S("kf32_ready"), S("kf_high_ready"), S("kf_low_ready")
                        turned, qf32_ready, kf_tok_ready = S("turned"), S("qf32_ready"), S("kf_tok_ready")
                        qf_high_ready, qf_low_ready, qf_bd_ready = S("qf_high_ready"), S("qf_low_ready"), S("qf_bd_ready")
                        qs_product, qs_max = S("qs_product"), S("qs_max")
                        row_top_ready, neg_max_ready, penal_ready = S("row_top_ready"), S("neg_max_ready"), S("penal_ready")
                        lift_arg_ready, lift_exp_ready = S("lift_arg_ready"), S("lift_exp_ready")
                        max_turned, max_rows_ready, max_placed = S("max_turned"), S("max_rows_ready"), S("max_placed")
                        f_product, f_ready = S("f_product"), S("f_ready")
                        ks_product, p_ready = S("ks_product"), S("p_ready")
                        global_done, local_done = S("global_done"), S("local_done")
                        state_read, inc_product, inc_ready, state_ready = S("state_read"), S("inc_product"), S("inc_ready"), S("state_ready")
                        sums_ready, sums_turned = S("sums_ready"), S("sums_turned")
                        norm_parts, norm_ready = S("norm_parts"), S("norm_ready")
                        r_ready, ctx_parts, ctx_ready = S("r_ready"), S("ctx_parts"), S("ctx_ready")
                        ctx_turned, ctx_ch_ready = S("ctx_turned"), S("ctx_ch_ready")
                        y_product, y_ready, x_biased = S("y_product"), S("y_ready"), S("x_biased")

                        def wait(eng, signal, count):
                            if not isinstance(count, int) or count > 0:
                                eng.wait_ge(signal, count)

                        def flat(v):
                            return v.rearrange("p a b -> p (a b)")

                        def scheduled(eng, one_block):
                            for par in range(RING):
                                one_block(par, par)
                            with eng.Fori(1, NBLK // RING) as i:
                                for par in range(RING):
                                    one_block(i * RING + par, par)

                        with nc.Block() as block:
                            @block.gpsimd
                            def _(pool):
                                def low_x(f, par):
                                    pool.wait_ge(x_high_ready, f + 1)
                                    nc.gpsimd.tensor_tensor(x_low[:, par % 2, :, :], xn_ch[:, :, ds(f * P, P)],
                                                            x_high[:, par % 2, :, :], ALU.subtract).then_inc(x_ready, 1)

                                nc.gpsimd.memset(scaled_eps[:, :], FEATURE_EPS * FSCALE).then_inc(cleared, 1)
                                low_x(0, 0)
                                for view in (v_ext[:, :, :, :], kf_tok[:, 1, :], qf_pad[:, :, :], state[:, :, :]):
                                    last = nc.gpsimd.memset(view, 0.0)
                                last.then_inc(cleared, 1)
                                pool.wait_ge(cleared, 2)
                                nc.gpsimd.memset(v_ext[:, :, :, DH:DH + 1], 1.0).then_inc(cleared, 1)

                                def front(f, par):
                                    pool.wait_ge(kf32_ready, f + 1)
                                    pool.wait_ge(kf_high_ready, f + 1)
                                    nc.gpsimd.tensor_tensor(kf_low[:, par, :, :], kf32[:, :, :], kf_high[:, par, :, :],
                                                            ALU.subtract).then_inc(kf_low_ready, 1)
                                    pool.wait_ge(q_high_ready, f + 1)
                                    wait(pool, q_bd_ready, 2 * f)
                                    nc.gpsimd.tensor_tensor(q_low[:, :, :], q32[:, :, :], q_high[:, :, :], ALU.subtract)\
                                        .then_inc(q_low_ready, 1)
                                    pool.wait_ge(k_lowhigh_ready, f + 1)
                                    nc.gpsimd.tensor_tensor(k_mix[:, :, par, :], k32[:, :, :], k_lowhigh[:, :, :],
                                                            ALU.subtract).then_inc(k_mix_ready, 1)
                                    pool.wait_ge(qf_max_ready, f + 1)
                                    nc.gpsimd.tensor_tensor(qf_tok[:, :, :], qf_tok[:, :, :],
                                                            qf_max[:, :].unsqueeze(2).broadcast_to([P, HEADS, FEAT]),
                                                            ALU.subtract).then_inc(qf_shifted, 1)
                                    pool.wait_ge(qf_high_ready, f + 1)
                                    wait(pool, qf_bd_ready, 2 * f)
                                    nc.gpsimd.tensor_tensor(qf_low[:, :, :], qf32[:, par % 2, :, :], qf_high[:, :, :],
                                                            ALU.subtract).then_inc(qf_low_ready, 1)

                                nc.gpsimd.memset(qf_bd[:, :, :, :, :, :], 0.0).then_inc(cleared, 1)
                                pool.wait_ge(cleared_dve, 1)
                                front(0, 0)

                                def output_bias(n):
                                    x_row = x_tok[:, ds(n, 1), :].rearrange("p a c -> p (a c)")
                                    nc.gpsimd.tensor_tensor(x_row, x_row, b_o[:, :], ALU.add).then_inc(x_biased, 1)

                                def one_block(n, par):
                                    low_x(n + 1, (par + 1) % RING)
                                    output_bias(n)
                                    front(n + 1, (par + 1) % RING)

                                scheduled(pool, one_block)

                            @block.sync
                            def _(sp):
                                def one_block(n, par):
                                    sp.wait_ge(max_rows_ready, n + 1)
                                    sp.dma_start(stair_own_r[0:1, :, :], max_rows[0:HEADS, :]).then_inc(max_placed, 16)
                                    sp.dma_start(stair_prev_r[P - 1:P, :, :], max_rows[HEADS:, :]).then_inc(max_placed, 16)

                                scheduled(sp, one_block)

                            @block.tensor
                            def _(pe):
                                def queries_keys(f, par):
                                    pe.wait_ge(x_ready, f + 1)
                                    wait(pe, qs_max, GROUPS * (f - 1) + 1)
                                    dst = pair(3)
                                    for which, w in ((0, wq_s), (1, wk_s)):
                                        for g in range(GROUPS):
                                            for k in range(HALVES):
                                                for i, (part, x_part) in enumerate(PASSES):
                                                    m = nc.tensor.matmul(dst[:, which, g * P:(g + 1) * P],
                                                                         w[part][:, k, g * P:(g + 1) * P],
                                                                         x_part[:, par % 2, k, :],
                                                                         start=(k == 0 and i == 0),
                                                                         stop=(k == HALVES - 1 and i == 2))
                                    m.then_inc(qk_product, 1)

                                def values(f, par):
                                    wait(pe, f_ready, 2 * GROUPS * (f - 1) + 2)
                                    dst = pair(8)
                                    for k in range(HALVES):
                                        for i, (part, x_part) in enumerate(PASSES):
                                            ends = dict(start=(k == 0 and i == 0), stop=(k == HALVES - 1 and i == 2))
                                            nc.tensor.matmul(dst[:, 0, :], x_part[:, par % 2, k, :], w_vq[part][:, k, :],
                                                             **ends)
                                            m = nc.tensor.matmul(dst[:, 1, 0:HEADS * FEAT], x_part[:, par % 2, k, :],
                                                                 w_qf[part][:, k, :], **ends)
                                    m.then_inc(vq_product, 1)

                                def turn_features(f):
                                    pe.wait_ge(qf_pad_ready, f + 1)
                                    pe.wait_ge(kf32_ready, f + 1)
                                    wait(pe, max_rows_ready, f)
                                    wait(pe, inc_ready, f)
                                    dst = pair(13)
                                    for g in range(GROUPS):
                                        nc.tensor.transpose(dst[:, 0, g * P:(g + 1) * P],
                                                            flat(qf_pad[:, g * PER_G:(g + 1) * PER_G, :]), ident[:, :])
                                    for g in range(GROUPS):
                                        m = nc.tensor.transpose(dst[:, 1, g * P:(g + 1) * P], kf32[:, g, :], ident[:, :])
                                    m.then_inc(turned, 1)

                                def query_scores(n, par, g):
                                    item = g if g < 3 else 4
                                    if g == 0:
                                        pe.wait_ge(q_bd_ready, 2 * n + 2)
                                        pe.wait_ge(k_mix_ready, n + 1)
                                        if isinstance(n, int) and n == 0:
                                            pe.wait_ge(qf_ready, 1)
                                        wait(pe, p_ready, GROUPS * (n - 1) + 2)
                                    if g == 1:
                                        if isinstance(n, int) and n == 0:
                                            pe.wait_ge(kf_tok_ready, 1)
                                        wait(pe, p_ready, GROUPS * (n - 1) + 3)
                                    if g == 2:
                                        wait(pe, p_ready, GROUPS * n)
                                    if g == 3:
                                        pe.wait_ge(qs_max, GROUPS * n + 2)
                                    dst = pair(item)
                                    order, keys = key_pair(par)
                                    for bank in range(2):
                                        nc.tensor.matmul(dst[:, bank, :], ident16[:, :],
                                                         mask_q[:, order, :, :].rearrange("p s k -> p (s k)").unsqueeze(1)
                                                         .broadcast_to([P, 2, 2 * P]),
                                                         start=True, stop=False)
                                        for h in range(2):
                                            m = nc.tensor.matmul(dst[:, bank, h * 2 * P:(h + 1) * 2 * P],
                                                                 q_bd[:, 0, par % 2, g, 2 * bank + h, :],
                                                                 k_mix[:, g, keys, :], start=False, stop=(h == 1))
                                    m.then_inc(qs_product, 1)

                                def maxima_state(n, par):
                                    pe.wait_ge(f_ready, 2 * GROUPS * n + 4)
                                    pe.wait_ge(penal_ready, n + 1)
                                    dst = pair(10)
                                    nc.tensor.transpose(dst[:, 1, :].bitcast(BF16)[0:2 * HEADS, 0:P],
                                                        neg_max[:, :, :].rearrange("p a h -> p (a h)"), ident16[:, :])\
                                        .then_inc(max_turned, 1)
                                    if isinstance(n, int) and n == 0:
                                        pe.wait_ge(cleared, 3)
                                    before = (par - 1) % RING
                                    for g in range(GROUPS):
                                        m = nc.tensor.matmul(dst[:, 0, g * P:(g + 1) * P],
                                                             kf_tok[:, before % 2, g * P:(g + 1) * P],
                                                             flat(v_ext[:, before, g * PER_G:(g + 1) * PER_G, :]),
                                                             start=True, stop=True)
                                    m.then_inc(inc_product, 1)

                                def feature_scores(n, par, g):
                                    item = FEATURE_ITEMS[g]
                                    if g == 0:
                                        pe.wait_ge(qf_bd_ready, 2 * n + 2)
                                        pe.wait_ge(kf_low_ready, n + 1)
                                        pe.wait_ge(qs_max, GROUPS * n + 3)
                                    if g == 1:
                                        pe.wait_ge(qs_max, GROUPS * (n + 1))
                                    if g == 2:
                                        wait(pe, ctx_ready, n)
                                        if isinstance(n, int) and n == 0:
                                            pe.wait_ge(k32_ready, 2)
                                    if g == 3:
                                        pe.wait_ge(f_ready, 2 * GROUPS * n + 6)
                                    dst = pair(item)
                                    for side in range(2):
                                        at = (par - side) % RING
                                        parts = ((kf_high, 0), (kf_high, 1), (kf_low, 0))
                                        for i, (kf, part) in enumerate(parts):
                                            m = nc.tensor.matmul(dst[:, side, :], kf[:, at, g, :],
                                                                 flat(qf_bd[:, part, 0, g, :, :]),
                                                                 start=(i == 0), stop=(i == 2))
                                        m.then_inc(f_product, 1)

                                def state_part(n, par):
                                    wait(pe, sums_ready, 2 * n)
                                    wait(pe, state_ready, n)
                                    if isinstance(n, int) and n == 0:
                                        pe.wait_ge(cleared, 3)
                                    for g in range(GROUPS):
                                        m = nc.tensor.matmul(ps_global[:, g * P:(g + 1) * P], state[:, g, :],
                                                             qf32[:, par % 2, g, :], start=(g == 0), stop=False,
                                                             skip_group_check=True)
                                    m.then_inc(state_read, 1)

                                def weighted(n, par, g, bank, weights, ready, done, unit, first):
                                    pe.wait_ge(ready, unit * (GROUPS * n + g + 1))
                                    if g == 0:
                                        pe.wait_ge(v_ready, n + 1)
                                    for side in range(2):
                                        at = (par - side) % RING
                                        for h in range(PER_G):
                                            m = nc.tensor.matmul(bank[h * STRIP:(h + 1) * STRIP, g * P:(g + 1) * P],
                                                                 v_ext[:, at, g * PER_G + h, :], weights[:, g % 2, side, h, :],
                                                                 start=(first and side == 0), stop=(side == 1),
                                                                 skip_group_check=True)
                                    m.then_inc(done, 1)

                                def weighted_features(n, par, g):
                                    weighted(n, par, g, ps_global, feats, f_ready, global_done, 2, False)

                                def weighted_probs(n, par, g):
                                    weighted(n, par, g, ps_local, probs, p_ready, local_done, 1, True)

                                def key_scores(n, par, g):
                                    item = 14 + g
                                    if g == 0:
                                        pe.wait_ge(max_placed, 32 * (n + 1))
                                        wait(pe, y_ready, n)
                                        if isinstance(n, int) and n == 0:
                                            pe.wait_ge(qf_ready, 2)
                                    if g == 1:
                                        pe.wait_ge(f_ready, 2 * GROUPS * (n + 1))
                                    if g == 2:
                                        pe.wait_ge(kf_tok_ready, n + 2)
                                    if g == 3:
                                        pe.wait_ge(p_ready, GROUPS * n + 1)
                                    dst = pair(item)
                                    for side, (left, right) in enumerate(((stair_own_l, stair_own_r),
                                                                          (stair_prev_l, stair_prev_r))):
                                        at = (par - side) % RING
                                        nc.tensor.matmul(dst[:, side, :], left[:, :], flat(right[:, g * PER_G:(g + 1) * PER_G, :]),
                                                         start=True, stop=False)
                                        for part in range(2):
                                            m = nc.tensor.matmul(dst[:, side, :], k_mix[:, g, at, :],
                                                                 flat(q_bd[:, part, par % 2, g, :, :]), start=False,
                                                                 stop=(part == 1))
                                    m.then_inc(ks_product, 1)

                                def turn_sums(n):
                                    pe.wait_ge(sums_ready, 2 * n + 2)
                                    pe.wait_ge(k32_ready, n + 3)
                                    dst = pair(6)
                                    for which in range(2):
                                        for g in range(GROUPS):
                                            m = nc.tensor.transpose(dst[:, which, g * P:(g + 1) * P],
                                                                    sums[:, which, g * P:(g + 1) * P], ident[:, :])
                                    m.then_inc(sums_turned, 1)

                                def turn_context(n, last=False):
                                    pe.wait_ge(ctx_ready, n + 1)
                                    if not last:
                                        pe.wait_ge(qf_ready, n + 3)
                                    dst = pair(11)
                                    for k in range(HALVES):
                                        m = nc.tensor.transpose(dst[:, 0, k * P:(k + 1) * P], ctx[:, k * P:(k + 1) * P],
                                                                ident[:, :])
                                    m.then_inc(ctx_turned, 1)

                                def output_product(n):
                                    pe.wait_ge(ctx_ch_ready, n + 1)
                                    dst = pair(11)
                                    for k in range(HALVES):
                                        m = nc.tensor.matmul(dst[:, 1, 0:DM], ctx_ch[:, k, :], w_o[:, k, :],
                                                             start=(k == 0), stop=(k == HALVES - 1))
                                    m.then_inc(y_product, 1)

                                queries_keys(0, 0)
                                values(0, 0)
                                turn_features(0)

                                def one_block(n, par):
                                    tail = not (isinstance(n, int) and n == 0)
                                    nxt = (par + 1) % RING
                                    query_scores(n, par, 0)
                                    query_scores(n, par, 1)
                                    query_scores(n, par, 2)
                                    queries_keys(n + 1, nxt)
                                    state_part(n, par)
                                    query_scores(n, par, 3)
                                    feature_scores(n, par, 0)
                                    if tail:
                                        turn_sums(n - 1)
                                    feature_scores(n, par, 1)
                                    values(n + 1, nxt)
                                    weighted_features(n, par, 0)
                                    feature_scores(n, par, 2)
                                    maxima_state(n, par)
                                    weighted_features(n, par, 1)
                                    if tail:
                                        turn_context(n - 1)
                                    feature_scores(n, par, 3)
                                    if tail:
                                        output_product(n - 1)
                                    weighted_features(n, par, 2)
                                    turn_features(n + 1)
                                    key_scores(n, par, 0)
                                    key_scores(n, par, 1)
                                    weighted_probs(n, par, 0)
                                    key_scores(n, par, 2)
                                    weighted_probs(n, par, 1)
                                    key_scores(n, par, 3)
                                    weighted_features(n, par, 3)
                                    weighted_probs(n, par, 2)
                                    weighted_probs(n, par, 3)

                                scheduled(pe, one_block)
                                pe.wait_ge(p_ready, GROUPS * NBLK)
                                pe.wait_ge(sums_ready, 2 * NBLK)
                                dst = pair(6)
                                for which in range(2):
                                    for g in range(GROUPS):
                                        m = nc.tensor.transpose(dst[:, which, g * P:(g + 1) * P],
                                                                sums[:, which, g * P:(g + 1) * P], ident[:, :])
                                m.then_inc(sums_turned, 1)
                                turn_context(NBLK - 1, last=True)
                                output_product(NBLK - 1)

                            @block.scalar
                            def _(act):
                                def high_x(f, par):
                                    wait(act, vq_product, f - 1)
                                    nc.scalar.activation(x_high[:, par % 2, :, :], xn_ch[:, :, ds(f * P, P)], ACT.Copy)\
                                        .then_inc(x_high_ready, 1)

                                def load_logs(f):
                                    wait(act, kf32_ready, f)
                                    act.dma_start(log_blk[:, :, :],
                                                  log_k[ds(f, 1), :, :, :].rearrange("a p g q -> (a p) g q"))\
                                        .then_inc(log_loaded, 16)

                                def key_exponentials(f):
                                    act.wait_ge(log_loaded, 16 * (f + 1))
                                    for g in range(GROUPS):
                                        a = nc.scalar.activation(log_blk[:, g, :], log_blk[:, g, :], ACT.Exp,
                                                                 bias=neg_kmax[:, ds(f, 1), g:g + 1].rearrange("p a b -> p (a b)"))
                                    a.then_inc(kf_exp_ready, 1)
                                    act.wait_ge(kf_exp_ready, f + 1)
                                    if isinstance(f, int) and f == 0:
                                        act.wait_ge(cleared, 1)
                                    wait(act, kf_low_ready, f)
                                    wait(act, turned, f)
                                    nc.scalar.activation(kf32[:, :, :], log_blk[:, :, :], ACT.Identity,
                                                         bias=scaled_eps[:, 0:1], scale=FSCALE).then_inc(kf32_ready, 1)

                                def splits(f, par):
                                    act.wait_ge(q32_ready, f + 1)
                                    wait(act, q_bd_ready, 2 * f)
                                    wait(act, q_low_ready, f)
                                    nc.scalar.activation(q_high[:, :, :], q32[:, :, :], ACT.Copy).then_inc(q_high_ready, 1)
                                    act.wait_ge(k32_ready, f + 1)
                                    wait(act, k_mix_ready, f)
                                    nc.scalar.activation(k_lowhigh[:, :, :], k32[:, :, :], ACT.Copy, scale=low_rows[:, 0:1])\
                                        .then_inc(k_lowhigh_ready, 1)
                                    act.wait_ge(kf32_ready, f + 1)
                                    wait(act, f_product, 2 * GROUPS * (f - 2))
                                    nc.scalar.activation(kf_high[:, par, :, :], kf32[:, :, :], ACT.Copy)\
                                        .then_inc(kf_high_ready, 1)

                                def query_squares(f):
                                    act.wait_ge(q_tok_ready, f + 1)
                                    nc.scalar.activation(q_tok[:, :], q_tok[:, :], ACT.Square).then_inc(q_sq_ready, 1)

                                def feature_exponentials(f):
                                    act.wait_ge(qf_shifted, f + 1)
                                    nc.scalar.activation(qf_tok[:, :, :], qf_tok[:, :, :], ACT.Exp).then_inc(qf_exp_ready, 1)

                                def turned_features(f, par):
                                    act.wait_ge(turned, f + 1)
                                    wait(act, state_read, f - 1)
                                    dst = pair(13)
                                    nc.scalar.activation(flat(qf32[:, par % 2, :, :]), dst[:, 0, :], ACT.Copy)\
                                        .then_inc(qf32_ready, 1)
                                    nc.scalar.activation(kf_tok[:, par % 2, :], dst[:, 1, :], ACT.Copy).then_inc(kf_tok_ready, 1)
                                    act.wait_ge(qf32_ready, f + 1)
                                    wait(act, qf_bd_ready, 2 * f)
                                    wait(act, qf_low_ready, f)
                                    nc.scalar.activation(qf_high[:, :, :], qf32[:, par % 2, :, :], ACT.Copy)\
                                        .then_inc(qf_high_ready, 1)

                                def context_turned(n):
                                    act.wait_ge(ctx_turned, n + 1)
                                    wait(act, y_product, n)
                                    nc.scalar.activation(flat(ctx_ch[:, :, :]), pair(11)[:, 0, 0:DM], ACT.Copy)\
                                        .then_inc(ctx_ch_ready, 1)

                                high_x(0, 0)
                                load_logs(0)
                                key_exponentials(0)
                                act.wait_ge(cleared, 3)
                                act.wait_ge(cleared_dve, 1)
                                splits(0, 0)
                                query_squares(0)
                                feature_exponentials(0)
                                load_logs(1)
                                turned_features(0, 0)

                                def one_block(n, par):
                                    tail = not (isinstance(n, int) and n == 0)
                                    nxt = (par + 1) % RING
                                    high_x(n + 1, nxt)
                                    key_exponentials(n + 1)
                                    splits(n + 1, nxt)
                                    load_logs(n + 2)
                                    act.wait_ge(lift_arg_ready, n + 1)
                                    nc.scalar.activation(lift_exp[:, par % 2, :], lift_arg[:, :], ACT.Exp)\
                                        .then_inc(lift_exp_ready, 1)
                                    query_squares(n + 1)
                                    act.wait_ge(max_turned, n + 1)
                                    wait(act, max_placed, 32 * n)
                                    nc.scalar.activation(max_rows[:, :], pair(10)[:, 1, :].bitcast(BF16)[0:2 * HEADS, 0:P],
                                                         ACT.Copy).then_inc(max_rows_ready, 1)
                                    if tail:
                                        context_turned(n - 1)
                                    feature_exponentials(n + 1)
                                    turned_features(n + 1, nxt)
                                    for g in range(GROUPS):
                                        act.wait_ge(ks_product, GROUPS * n + g + 1)
                                        wait(act, local_done, GROUPS * n + g - 1)
                                        nc.scalar.activation(probs[:, g % 2, :, :, :].rearrange("p s h q -> p (s h q)"),
                                                             pair(14 + g)[:, :, :].rearrange("p s c -> p (s c)"), ACT.Exp)\
                                            .then_inc(p_ready, 1)
                                    wait(act, sums_turned, n)
                                    act.wait_ge(global_done, GROUPS * (n + 1))
                                    nc.scalar.activation(sums[:, 1, :], ps_global[:, :], ACT.Copy).then_inc(sums_ready, 1)
                                    act.wait_ge(local_done, GROUPS * (n + 1))
                                    nc.scalar.activation(sums[:, 0, :], ps_local[:, :], ACT.Copy).then_inc(sums_ready, 1)

                                scheduled(act, one_block)
                                context_turned(NBLK - 1)
                                act.wait_ge(log_loaded, 16 * (NBLK + 2))

                            @block.vector
                            def _(dve):
                                def queries_keys(f):
                                    src = pair(3)
                                    dve.wait_ge(qk_product, f + 1)
                                    wait(dve, q_low_ready, f)
                                    wait(dve, k_mix_ready, f)
                                    for which, bias, dst, ready in ((0, bq_s, q32, q32_ready), (1, bk_s, k32, k32_ready)):
                                        nc.vector.scalar_tensor_tensor(
                                            dst[:, :, :], src[:, which, :].rearrange("p (g q) -> p g q", q=P), 1.0 / WSCALE,
                                            bias[:, :].unsqueeze(2).broadcast_to([P, GROUPS, P]), ALU.mult, ALU.add)\
                                            .then_inc(ready, 1)

                                def values(f, par):
                                    src = pair(8)
                                    dve.wait_ge(vq_product, f + 1)
                                    wait(dve, local_done, GROUPS * (f - 2))
                                    nc.vector.scalar_tensor_tensor(v_ext[:, par, :, 0:DH],
                                                                   src[:, 0, 0:DM].rearrange("p (h d) -> p h d", d=DH), 1.0 / WSCALE,
                                                                   b_vq[:, 0:DM].rearrange("p (h d) -> p h d", d=DH),
                                                                   ALU.mult, ALU.add)\
                                        .then_inc(v_ready, 1)
                                    wait(dve, q_norm_ready, f)
                                    nc.vector.scalar_tensor_tensor(q_tok[:, :], src[:, 0, DM:], 1.0 / WSCALE, b_vq[:, DM:],
                                                                   ALU.mult, ALU.add)\
                                        .then_inc(q_tok_ready, 1)
                                    wait(dve, qf_pad_ready, f)
                                    nc.vector.scalar_tensor_tensor(
                                        qf_tok[:, :, :], src[:, 1, 0:HEADS * FEAT].rearrange("p (h m) -> p h m", m=FEAT),
                                        1.0 / WSCALE, b_qf[:, :].rearrange("p (h m) -> p h m", m=FEAT), ALU.mult, ALU.add)\
                                        .then_inc(qf_ready, 1)

                                def feature_maxima(f, par):
                                    dve.wait_ge(qf_ready, f + 1)
                                    nc.vector.tensor_reduce(qf_max[:, :], qf_tok[:, :, :], AX_X, ALU.max).then_inc(qf_max_ready, 1)
                                    dve.wait_ge(q_sq_ready, f + 1)
                                    nc.vector.tensor_reduce(q_norm[:, :], q_tok[:, :].rearrange("p (h d) -> p h d", d=DH), AX_X,
                                                            ALU.add).then_inc(q_norm_ready, 1)
                                    dve.wait_ge(q_norm_ready, f + 1)
                                    dve.wait_ge(qf_max_ready, f + 1)
                                    nc.vector.scalar_tensor_tensor(q_scale[:, :], q_norm[:, :], -SCALE / 2, qf_max[:, :],
                                                                   ALU.mult, ALU.add).then_inc(q_scale_ready, 1)
                                    dve.wait_ge(q_scale_ready, f + 1)
                                    nc.vector.tensor_tensor(g_scale[:, par % 2, :], q_scale[:, :],
                                                            kmax_tok[:, ds(f, 1), :].rearrange("p a h -> p (a h)"), ALU.add)\
                                        .then_inc(g_scale_ready, 1)

                                def place(f, slot, bd, high, low, high_ready, low_ready, placed):
                                    for part, src, ready in ((0, high, high_ready), (1, low, low_ready)):
                                        dve.wait_ge(ready, f + 1)
                                        for r in range(PER_G):
                                            rows = slice(r * STRIP, (r + 1) * STRIP)
                                            c = nc.vector.tensor_copy(bd[rows, part, slot, :, r, :], src[rows, :, :])
                                        c.then_inc(placed, 1)

                                def place_queries(f, par):
                                    wait(dve, ks_product, GROUPS * (f - 1))
                                    place(f, par % 2, q_bd, q_high, q_low, q_high_ready, q_low_ready, q_bd_ready)

                                def place_features(f, par):
                                    wait(dve, f_product, 2 * GROUPS * f)
                                    place(f, 0, qf_bd, qf_high, qf_low, qf_high_ready, qf_low_ready, qf_bd_ready)

                                def pad_features(f):
                                    dve.wait_ge(qf_exp_ready, f + 1)
                                    wait(dve, turned, f)
                                    nc.vector.tensor_scalar(qf_pad[:, :, 0:FEAT], qf_tok[:, :, :], FEATURE_EPS, FSCALE,
                                                            ALU.add, ALU.mult).then_inc(qf_pad_ready, 1)

                                def maximum(n, par, g):
                                    dve.wait_ge(qs_product, GROUPS * n + g + 1)
                                    if g == 0:
                                        wait(dve, row_top_ready, n)
                                    nc.vector.tensor_reduce(
                                        block_max[:, g, :, :],
                                        pair(g if g < 3 else 4)[:, :, :].rearrange("p b (h s k) -> p (b h s) k", h=2, s=2),
                                        AX_X, ALU.max).then_inc(qs_max, 1)

                                def maxima(n, par):
                                    order, _ = key_pair(par)
                                    own, prev = 1 - order, order
                                    bm = block_max[:, :, :, :].rearrange("p g h s -> p (g h) s")
                                    dve.wait_ge(qs_max, GROUPS * (n + 1))
                                    nc.vector.scalar_tensor_tensor(row_top[:, :], bm[:, :, prev], penalty[:, ds(n, 1)],
                                                                   bm[:, :, own], ALU.add, ALU.max).then_inc(row_top_ready, 1)
                                    dve.wait_ge(row_top_ready, n + 1)
                                    wait(dve, max_turned, n)
                                    wait(dve, lift_arg_ready, n)
                                    nc.vector.tensor_scalar(neg_max[:, 0, :], row_top[:, :], -1.0, None, ALU.mult)\
                                        .then_inc(neg_max_ready, 1)
                                    dve.wait_ge(neg_max_ready, n + 1)
                                    nc.vector.tensor_scalar(neg_max[:, 1, :], neg_max[:, 0, :], penalty[:, ds(n, 1)], None,
                                                            ALU.add).then_inc(penal_ready, 1)

                                def lift_argument(n, par):
                                    dve.wait_ge(neg_max_ready, n + 1)
                                    dve.wait_ge(g_scale_ready, n + 1)
                                    wait(dve, lift_exp_ready, n)
                                    nc.vector.scalar_tensor_tensor(lift_arg[:, :], neg_max[:, 0, :], -1.0,
                                                                   g_scale[:, par % 2, :], ALU.mult, ALU.subtract)\
                                        .then_inc(lift_arg_ready, 1)

                                def masked_features(n, par, g):
                                    src = pair(FEATURE_ITEMS[g])
                                    for side in range(2):
                                        dve.wait_ge(f_product, 2 * (GROUPS * n + g) + side + 1)
                                        wait(dve, global_done, GROUPS * n + g - 1)
                                        s = src[:, side, :].rearrange("p (h q) -> p h q", q=P)
                                        mask = gmask[:, side:side + 1, :].broadcast_to([P, PER_G, P])
                                        if side == 0:
                                            m = nc.vector.tensor_tensor(feats[:, g % 2, side, :, :], s, mask, ALU.mult)
                                        else:
                                            m = nc.vector.scalar_tensor_tensor(feats[:, g % 2, side, :, :], s,
                                                                               has_prev[:, ds(n, 1)], mask, ALU.mult, ALU.mult)
                                        m.then_inc(f_ready, 1)

                                def state_increment(n):
                                    src = pair(10)[:, 0, :]
                                    dve.wait_ge(inc_product, n + 1)
                                    nc.vector.scalar_tensor_tensor(
                                        state_inc[:, :, :], src.rearrange("p (g c) -> p g c", c=P), keep_state[:, ds(n, 1)],
                                        flat(diag_strips[:, :, :]).unsqueeze(1).broadcast_to([P, GROUPS, P]),
                                        ALU.mult, ALU.mult).then_inc(inc_ready, 1)

                                def add_state(n):
                                    dve.wait_ge(inc_ready, n + 1)
                                    dve.wait_ge(state_read, n + 1)
                                    nc.vector.scalar_tensor_tensor(state[:, :, :], state[:, :, :], keep_state[:, ds(n, 1)],
                                                                   state_inc[:, :, :], ALU.mult, ALU.add)\
                                        .then_inc(state_ready, 1)

                                def normalise(n, par):
                                    src = pair(6)
                                    local = src[:, 0, :].rearrange("p (h d) -> p h d", d=STRIP)
                                    whole = src[:, 1, :].rearrange("p (h d) -> p h d", d=STRIP)
                                    dve.wait_ge(sums_turned, n + 1)
                                    dve.wait_ge(lift_exp_ready, n + 1)
                                    nc.vector.tensor_tensor(norm_a[:, :], lift_exp[:, par % 2, :], local[:, :, DH], ALU.mult)\
                                        .then_inc(norm_parts, 1)
                                    nc.vector.tensor_scalar(norm_b[:, :], whole[:, :, DH], UNSCALE, 1e-24, ALU.mult, ALU.max)\
                                        .then_inc(norm_parts, 1)
                                    nc.vector.reciprocal(r_local[:, :], local[:, :, DH]).then_inc(r_ready, 1)
                                    dve.wait_ge(norm_parts, 2 * n + 2)
                                    nc.vector.tensor_tensor(norm_c[:, :], norm_a[:, :], norm_b[:, :], ALU.add).then_inc(norm_ready, 1)
                                    dve.wait_ge(r_ready, 2 * n + 1)
                                    nc.vector.tensor_tensor(ctx_a[:, :, :], local[:, :, 0:DH],
                                                            r_local[:, :].unsqueeze(2).broadcast_to([P, HEADS, DH]), ALU.mult)\
                                        .then_inc(ctx_parts, 1)
                                    dve.wait_ge(norm_ready, 2 * n + 1)
                                    nc.vector.reciprocal(norm_r[:, :], norm_c[:, :]).then_inc(norm_ready, 1)
                                    dve.wait_ge(norm_ready, 2 * n + 2)
                                    nc.vector.tensor_scalar(r_global[:, :], norm_r[:, :], UNSCALE, None, ALU.mult)\
                                        .then_inc(r_ready, 1)
                                    dve.wait_ge(r_ready, 2 * n + 2)
                                    wait(dve, ctx_turned, n)
                                    nc.vector.tensor_tensor(ctx[:, :].rearrange("p (h d) -> p h d", d=DH), whole[:, :, 0:DH],
                                                            r_global[:, :].unsqueeze(2).broadcast_to([P, HEADS, DH]), ALU.mult)\
                                        .then_inc(ctx_parts, 1)
                                    dve.wait_ge(ctx_parts, 2 * n + 2)
                                    wait(dve, ctx_turned, n)
                                    nc.vector.tensor_tensor(ctx[:, :], flat(ctx_a[:, :, :]), ctx[:, :], ALU.add)\
                                        .then_inc(ctx_ready, 1)

                                def add_output(n):
                                    dve.wait_ge(y_product, n + 1)
                                    dve.wait_ge(x_biased, n + 1)
                                    x_row = x_tok[:, ds(n, 1), :].rearrange("p a c -> p (a c)")
                                    nc.vector.tensor_tensor(x_row, pair(11)[:, 1, 0:DM], x_row, ALU.add)\
                                        .then_inc(y_ready, 1)

                                def statistics(n):
                                    dve.wait_ge(y_ready, n + 1)
                                    nc.vector.bn_stats(stats[:, ds(n, 1), :].rearrange("p a c -> p (a c)"),
                                                       x_tok[:, ds(n, 1), :].rearrange("p a c -> p (a c)"))

                                for view in (q_bd[:, :, :, :, :, :], k_mix[:, :, RING - 1, :], kf_high[:, RING - 1, :, :],
                                             kf_low[:, RING - 1, :, :]):
                                    last = nc.vector.memset(view, 0.0)
                                last.then_inc(cleared_dve, 1)
                                dve.wait_ge(cleared_dve, 1)
                                dve.wait_ge(cleared, 3)
                                queries_keys(0)
                                values(0, 0)
                                feature_maxima(0, 0)
                                place_queries(0, 0)
                                pad_features(0)
                                dve.wait_ge(cleared, 4)
                                place_features(0, 0)

                                def one_block(n, par):
                                    tail = not (isinstance(n, int) and n == 0)
                                    nxt = (par + 1) % RING
                                    for g in range(3):
                                        maximum(n, par, g)
                                    queries_keys(n + 1)
                                    maximum(n, par, 3)
                                    maxima(n, par)
                                    masked_features(n, par, 0)
                                    lift_argument(n, par)
                                    if tail:
                                        normalise(n - 1, (par - 1) % RING)
                                    masked_features(n, par, 1)
                                    values(n + 1, nxt)
                                    masked_features(n, par, 2)
                                    feature_maxima(n + 1, nxt)
                                    state_increment(n)
                                    pad_features(n + 1)
                                    add_state(n)
                                    if tail:
                                        add_output(n - 1)
                                    masked_features(n, par, 3)
                                    place_queries(n + 1, nxt)
                                    place_features(n + 1, nxt)
                                    if tail:
                                        statistics(n - 1)

                                scheduled(dve, one_block)
                                normalise(NBLK - 1, (NBLK - 1) % RING)
                                add_output(NBLK - 1)
                                statistics(NBLK - 1)

                def key_pair(par):
                    return (0, slice(par - 1, par + 1)) if par else (1, slice(0, 4, 3))

                with ExitStack() as prep:
                    proj_bd = sb("proj_bd", [P, HALF_HEADS, FEAT], F32, prep)
                    w_k = sb("w_k", [P, HALVES, DM], F32, prep)
                    bk_col = sb("bk_col", [P, HALVES], F32, prep)
                    with ExitStack() as early:
                        weights = attention_weights(early)
                        ffn("ffn1", True, False, weights)
                        layernorm("ln2", weights)
                    key_features(prep)
                attention_blocks(scope)

        first_ffn_and_attention()
        ffn("ffn2", False, True)


_INS = ["L0_attn_x", "L0_attn_Wqkv_w", "L0_attn_Wqkv_b", "L0_attn_proj", "L0_attn_out_w", "L0_attn_out_b",
        "L0_ffn_cn_w1", "L0_ffn_cn_b1", "L0_ffn_cn_w2", "L0_ffn_cn_b2", "L0_ffn_cn_w3", "L0_ffn_cn_b3",
        "L0_ffn_cn_w4", "L0_ffn_cn_b4", "L0_ffn_gc_w1", "L0_ffn_gc_b1", "L0_ffn_gc_w2", "L0_ffn_gc_b2",
        "L0_ffn_gc_w3", "L0_ffn_gc_b3", "L0_ffn_adaptive_range"]


def kernel(**inputs):
    import numpy as _np
    import concourse.bacc as _bacc
    from concourse.bass_utils import run_bass_kernel_spmd as _run

    nc = _bacc.Bacc("TRN2", target_bir_lowering=False, num_devices=1)
    arrays, args = {}, []
    for name in _INS:
        a = _np.ascontiguousarray(inputs[name])
        arrays[name + "_dram"] = a
        args.append(nc.dram_tensor(name + "_dram", a.shape, mybir.dt.from_np(a.dtype),
                                   kind="ExternalInput").ap())
    x = inputs["L0_attn_x"]
    out = nc.dram_tensor("out_dram", tuple(x.shape), F32, kind="ExternalOutput").ap()
    macaron_kernel(nc, *args, out)
    r = _run(nc, [arrays], core_ids=[0])
    return r.results[0]["out_dram"]
```
